# Optimizing a Trainium2 kernel written in Bass

```python
import numpy as np
import jax
import jax.numpy as jnp

def _softmax(x, axis=-1):
    return jax.nn.softmax(x, axis=axis)

def _gelu(x):
    return jax.nn.gelu(x, approximate=True)

def _silu(x):
    return jax.nn.silu(x)

def _sigmoid(x):
    return jax.nn.sigmoid(x)

def _layernorm(x, axis=-1, eps=1e-05):
    m = jnp.mean(x, axis=axis, keepdims=True)
    v = jnp.var(x, axis=axis, keepdims=True)
    return (x - m) / jnp.sqrt(v + eps)

def _scatter_add(tgt, idx, src, axis=0):
    return tgt.at[idx].add(src)

def _segment_sum(src, seg, n):
    return jax.ops.segment_sum(src, seg, n)
kernel_name = 'mk_gnn_resnorm_d2_gnn_r8_c2c75f'

def setup_inputs(seed: int=0):
    np.random.seed(seed)
    _w = jnp.asarray

    def _rec_inputs():
        import jax
        import jax.numpy as jnp
        _gk = jax.random.key(seed)
        x = -0.0005121 + 1.001 * jax.random.normal(jax.random.fold_in(_gk, 1), (12500, 32), jnp.float32)
        _s = jax.random.randint(jax.random.fold_in(_gk, 2), (100000,), 0, 12500, jnp.int32)
        _d = jax.random.randint(jax.random.fold_in(_gk, 3), (100000,), 0, 12500, jnp.int32)
        _loop = jnp.arange(12500, dtype=jnp.int32)
        src = jnp.concatenate([_s, _d, _loop])
        dst = jnp.concatenate([_d, _s, _loop])
        _o = jnp.argsort(dst, stable=True)
        src = src[_o]
        dst = dst[_o]
        edge_attr_10 = jax.random.uniform(jax.random.fold_in(_gk, 12), (212500, 10), jnp.float32, 0.0, 0.999998)
        edge_attr_3 = 0.00158508 + 0.999651 * jax.random.normal(jax.random.fold_in(_gk, 13), (212500, 3), jnp.float32)
        edge_weight = jax.random.uniform(jax.random.fold_in(_gk, 15), (212500,), jnp.float32, 0.0, 0.999997)
        return (x, src, dst, edge_attr_10, edge_attr_3, edge_weight)
    x, src, dst, edge_attr_10, edge_attr_3, edge_weight = _rec_inputs()

    def _L0_gnn_setup():
        import jax, jax.numpy as jnp
        import numpy as np
        N = 12500
        F = 32
        E = 200000
        NEG_SLOPE = 0.2
        key = jax.random.key(seed)
        ks = jax.random.split(key, 6)
        x = jax.random.normal(ks[0], (N, F), dtype=jnp.float32)
        edge_index = jax.random.randint(ks[1], (2, E), 0, N, dtype=jnp.int32)
        scale = 1.0 / np.sqrt(F)
        W = jax.random.normal(ks[2], (F, F), dtype=jnp.float32) * scale
        att_src = jax.random.normal(ks[3], (F,), dtype=jnp.float32) * scale
        att_dst = jax.random.normal(ks[4], (F,), dtype=jnp.float32) * scale
        bias = jax.random.normal(ks[5], (F,), dtype=jnp.float32) * 0.01
        return {'x': x, 'edge_index': edge_index, 'W': W, 'att_src': att_src, 'att_dst': att_dst, 'bias': bias}
    _L0_gnn_all = _L0_gnn_setup()
    _L0_gnn_in = {k: v for k, v in _L0_gnn_all.items() if k in ('W', 'att_src', 'att_dst', 'bias')}
    del _L0_gnn_all

    def _L1_gnn_setup():
        import jax, jax.numpy as jnp
        import numpy as np
        SQRT3 = 3.0 ** 0.5

        def _mlp(emb, w1, w2):
            h = jax.nn.relu(emb @ w1 / jnp.sqrt(jnp.float32(w1.shape[0])))
            return h @ w2 / jnp.sqrt(jnp.float32(w2.shape[0]))
        key = jax.random.key(seed)
        ks = jax.random.split(key, 10)
        N, E = (1250, 20000)
        x = jax.random.normal(ks[0], (N, 32), jnp.float32)
        edge_src = jax.random.randint(ks[1], (E,), 0, N)
        edge_dst = jax.random.randint(ks[2], (E,), 0, N)
        edge_vec = jax.random.normal(ks[3], (E, 3), jnp.float32)
        emb = jax.random.uniform(ks[4], (E, 10), jnp.float32)
        norm = jax.random.uniform(ks[5], (E,), jnp.float32)
        fc1_w1 = jax.random.normal(ks[6], (10, 16), jnp.float32)
        fc1_w2 = jax.random.normal(ks[7], (16, 512), jnp.float32)
        fc2_w1 = jax.random.normal(ks[8], (10, 16), jnp.float32)
        fc2_w2 = jax.random.normal(ks[9], (16, 384), jnp.float32)
        return dict(x=x, edge_src=edge_src, edge_dst=edge_dst, edge_vec=edge_vec, emb=emb, norm=norm, num_nodes=N, fc1_w1=fc1_w1, fc1_w2=fc1_w2, fc2_w1=fc2_w1, fc2_w2=fc2_w2)
    _L1_gnn_all = _L1_gnn_setup()
    _L1_gnn_in = {k: v for k, v in _L1_gnn_all.items() if k in ('fc1_w1', 'fc1_w2', 'fc2_w1', 'fc2_w2')}
    del _L1_gnn_all
    return {'x': x, 'src': src, 'dst': dst, 'edge_attr_10': edge_attr_10, 'edge_attr_3': edge_attr_3, 'edge_weight': edge_weight, 'L0_gnn_W': _L0_gnn_in['W'], 'L0_gnn_att_src': _L0_gnn_in['att_src'], 'L0_gnn_att_dst': _L0_gnn_in['att_dst'], 'L0_gnn_bias': _L0_gnn_in['bias'], 'L1_gnn_fc1_w1': _L1_gnn_in['fc1_w1'], 'L1_gnn_fc1_w2': _L1_gnn_in['fc1_w2'], 'L1_gnn_fc2_w1': _L1_gnn_in['fc2_w1'], 'L1_gnn_fc2_w2': _L1_gnn_in['fc2_w2']}

def reference(x, src, dst, edge_attr_10, edge_attr_3, edge_weight, L0_gnn_W, L0_gnn_att_src, L0_gnn_att_dst, L0_gnn_bias, L1_gnn_fc1_w1, L1_gnn_fc1_w2, L1_gnn_fc2_w1, L1_gnn_fc2_w2):
    import jax
    import jax.numpy as jnp

    def _L0_gnn_ref(x, edge_index, W, att_src, att_dst, bias):
        import jax, jax.numpy as jnp
        import numpy as np
        N = 12500
        F = 32
        E = 200000
        NEG_SLOPE = 0.2
        h = x @ W
        loops = jnp.arange(N, dtype=edge_index.dtype)
        src = jnp.concatenate([edge_index[0], loops])
        dst = jnp.concatenate([edge_index[1], loops])
        a_src = h @ att_src
        a_dst = h @ att_dst
        e = jax.nn.leaky_relu(a_src[src] + a_dst[dst], NEG_SLOPE)
        m = jax.ops.segment_max(e, dst, num_segments=N)
        ex = jnp.exp(e - m[dst])
        denom = jax.ops.segment_sum(ex, dst, num_segments=N)
        alpha = ex / denom[dst]
        out = jax.ops.segment_sum(alpha[:, None] * h[src], dst, num_segments=N)
        return out + bias

    def _L1_gnn_ref(x, edge_src, edge_dst, edge_vec, emb, norm, num_nodes, fc1_w1, fc1_w2, fc2_w1, fc2_w2):
        import jax, jax.numpy as jnp
        import numpy as np
        SQRT3 = 3.0 ** 0.5

        def _mlp(emb, w1, w2):
            h = jax.nn.relu(emb @ w1 / jnp.sqrt(jnp.float32(w1.shape[0])))
            return h @ w2 / jnp.sqrt(jnp.float32(w2.shape[0]))
        E = edge_vec.shape[0]
        r = edge_vec / jnp.linalg.norm(edge_vec, axis=1, keepdims=True)
        sh1 = SQRT3 * r
        xs, xd = (x[edge_src], x[edge_dst])
        s1 = jnp.concatenate([xs[:, :8], xd[:, :8]], axis=1)
        v1 = jnp.concatenate([xs[:, 8:].reshape(E, 8, 3), xd[:, 8:].reshape(E, 8, 3)], axis=1)
        w = _mlp(emb, fc1_w1, fc1_w2)
        Wss = w[:, 0:128].reshape(E, 16, 8)
        Wvv = w[:, 128:256].reshape(E, 16, 8)
        Wsv = w[:, 256:384].reshape(E, 16, 8)
        Wvs = w[:, 384:512].reshape(E, 16, 8)
        a1 = 1.0 / jnp.sqrt(32.0)
        vdot1 = jnp.einsum('euk,ek->eu', v1, sh1) / SQRT3
        s_t = a1 * (jnp.einsum('eu,euw->ew', s1, Wss) + jnp.einsum('eu,euw->ew', vdot1, Wvv))
        v_t = a1 * (jnp.einsum('eu,euw->ew', s1, Wsv)[:, :, None] * sh1[:, None, :] + jnp.einsum('euk,euw->ewk', v1, Wvs))
        w2 = _mlp(emb, fc2_w1, fc2_w2)
        Ass = w2[:, 0:64].reshape(E, 8, 8)
        Avv = w2[:, 64:128].reshape(E, 8, 8)
        Bss = w2[:, 128:192].reshape(E, 8, 8)
        Bvv = w2[:, 192:256].reshape(E, 8, 8)
        Csv = w2[:, 256:320].reshape(E, 8, 8)
        Cvs = w2[:, 320:384].reshape(E, 8, 8)
        a2 = 1.0 / jnp.sqrt(16.0)
        vdot2 = jnp.einsum('euk,ek->eu', v_t, sh1) / SQRT3
        scal = a2 * (jnp.einsum('eu,euw->ew', s_t, Ass) + jnp.einsum('eu,euw->ew', vdot2, Avv))
        gates = a2 * (jnp.einsum('eu,euw->ew', s_t, Bss) + jnp.einsum('eu,euw->ew', vdot2, Bvv))
        vecs = a2 * (jnp.einsum('eu,euw->ew', s_t, Csv)[:, :, None] * sh1[:, None, :] + jnp.einsum('euk,euw->ewk', v_t, Cvs))
        edge_out = jnp.concatenate([jnp.tanh(scal), (vecs * jnp.tanh(gates)[:, :, None]).reshape(E, 24)], axis=1)
        edge_out = edge_out * norm[:, None]
        return jax.ops.segment_sum(edge_out, edge_dst, num_segments=num_nodes)
    edge_index = jnp.stack([src, dst])
    x = _layernorm(x + _L0_gnn_ref(x, edge_index, L0_gnn_W, L0_gnn_att_src, L0_gnn_att_dst, L0_gnn_bias), axis=-1)
    x = _layernorm(x + _L1_gnn_ref(x, src, dst, edge_attr_3, edge_attr_10, edge_weight, 12500, L1_gnn_fc1_w1, L1_gnn_fc1_w2, L1_gnn_fc2_w1, L1_gnn_fc2_w2), axis=-1)
    return x

_drawn_inputs = setup_inputs


def setup_inputs(seed=0):
    import zlib

    import numpy as np

    out = dict(_drawn_inputs(seed))
    spreads = {}
    factors = {'L0_gnn_bias': 5.59}
    for name, (base, spread) in spreads.items():
        noise = np.random.default_rng([zlib.crc32(name.encode()), seed]).standard_normal(out[name].shape)
        drawn = base * np.exp(spread * noise) if base else spread * noise
        out[name] = jnp.asarray(drawn.astype(out[name].dtype))
    for name, factor in factors.items():
        out[name] = (out[name] * factor).astype(out[name].dtype)
    return out
```

```python
from contextlib import ExitStack

import numpy as np

import concourse.bass as bass
from concourse import mybir

F32 = mybir.dt.float32
BF16 = mybir.dt.bfloat16
I32 = mybir.dt.int32
ALU = mybir.AluOpType
ACT = mybir.ActivationFunctionType
AX_X = mybir.AxisListType.X

P = 128
T = 8
RING = 4
F = 32
H = 16
EMB = 10
R0 = F + 2
BIG = 1.0e30
EPS = 1.0e-5
SLOPE = 0.2
K6 = 6 * H
HID_PART = (0, 0, 1, 0, 1, 2)
W_PART = (0, 1, 0, 2, 1, 0)
NG = 14


def gnn_kernel(nc, xT, xN, w, wT, att, bias, idx, dst_ext, src_flat, emb, vec, weight,
               fc1, w2, parts, out, NN, NT):
    NB = NT // T
    NC = NT // P
    ACC = (NN + 1) * P
    assert NB % RING == 0 and NT % P == 0

    table = nc.dram_tensor("table0", (NN * P, R0), F32).ap()
    table1 = nc.dram_tensor("table1", (NN * P, F), F32).ap()
    spill = nc.dram_tensor("spill", (P, NT * R0), F32).ap()
    hid_d = nc.dram_tensor("hid_d", (K6, NT * P * 2), BF16).ap()
    ends_d = nc.dram_tensor("ends_d", (4, NT), F32).ap()
    carry_d = nc.dram_tensor("carry_d", (4, NT), F32).ap()

    outer = ExitStack()
    with outer:
        outer.enter_context(nc.allow_non_contiguous_dma(reason="one element of each edge tile, once"))

        def maker(stack):
            def sb(name, shape, dt=F32):
                return stack.enter_context(nc.sbuf_tensor(name, shape, dt))

            def ps(name, shape=(P, 512)):
                return stack.enter_context(nc.psum_tensor(name, list(shape), F32))

            def sem(name):
                return outer.enter_context(nc.semaphore(name))
            return sb, ps, sem

        sb, _, sem = maker(outer)

        iota_n = sb("iota_n", [P, P])
        ident = sb("ident", [P, P])
        first_i = sb("first_i", [1, NT], I32)
        local = sb("local", [P, NT])
        parts_s = sb("parts_s", [K6, 4])
        bias_b = sb("bias_b", [P, F])
        layer0 = ExitStack()
        idx_all = layer0.enter_context(nc.sbuf_tensor("idx_all", [P, NT, 2], I32))
        nodes0 = layer0.enter_context(nc.sbuf_tensor("nodes0", [P, NN, R0], F32))

        asd = layer0.enter_context(nc.sbuf_tensor("asd", [P, 2, NT], F32))
        with ExitStack() as st:
            sb, ps, sem = maker(st)
            xT_s = sb("xT_s", [F, NN * P])
            w_s = sb("w_s", [F, R0])
            wT_s = sb("wT_s", [F, F])
            att_s = sb("att_s", [F, 2])
            iota_i = sb("iota_i", [P, P], I32)
            part_i = sb("part_i", [P, 1], I32)
            part_f = sb("part_f", [P, 1])
            idx_b = sb("idx_b", [P, RING, T], I32)
            rows = sb("rows", [P, RING, T, R0])
            fc1_s = sb("fc1_s", [EMB, 2, K6])
            emb_s = sb("emb_s", [EMB, RING, T * P])
            hid = sb("hid", [K6, 2, 2, T * P])
            top = sb("top", [K6, 2, 2, T * P], BF16)
            part = sb("part", [K6, 2, 2, T * P], BF16)
            p_hid = [[ps(f"p_hid{n}{h}") for h in range(2)] for n in range(2)]
            p_att = ps("p_att")
            p_tab = [ps("p_tab0"), ps("p_tab1")]

            w_landed, xT_landed, idx_landed, first_landed = sem("w_landed"), sem("xT_landed"), sem("idx_landed"), sem("first_landed")
            iota_made, part_cast, consts_made = sem("iota_made"), sem("part_cast"), sem("consts_made")
            att_mm, att_copied, tab_mm, tab_copied, tab_stored = sem("att_mm"), sem("att_copied"), sem("tab_mm"), sem("tab_copied"), sem("tab_stored")
            idx_copied, rows_split = sem("idx_copied"), sem("rows_split")
            rows_landed = [sem(f"rows_landed{b}") for b in range(RING)]
            rows_spilled = [sem(f"rows_spilled{b}") for b in range(RING)]
            emb_landed = [sem(f"emb_landed{b}") for b in range(RING)]
            part_stored = [sem(f"part_stored{b}") for b in range(2)]
            hid_mm, hid_done, top_done, less_done, mid_done, part_done = (
                sem("hid_mm"), sem("hid_done"), sem("top_done"), sem("less_done"), sem("middle_done"), sem("part_done"))
            groups = NN // NG

            block = st.enter_context(nc.Block())

            @block.sync
            def _(sp):
                sp.dma_start(w_s[:, 0:F], w).then_inc(w_landed, 16)
                sp.dma_start(wT_s[:], wT).then_inc(w_landed, 16)
                sp.dma_start(att_s[:], att).then_inc(w_landed, 16)
                sp.dma_start(xT_s[:], xT).then_inc(xT_landed, 16)
                sp.dma_start(fc1_s[:].rearrange("p n h -> p (n h)"), fc1).then_inc(w_landed, 16)
                sp.dma_start(parts_s[:], parts).then_inc(w_landed, 16)
                sp.dma_start(idx_all[:].rearrange("p t two -> p (t two)"), idx).then_inc(idx_landed, 16)
                sp.dma_start(bias_b[:], bias.partition_broadcast(P)).then_inc(first_landed, 16)
                sp.dma_start(first_i[:], dst_ext[1:1 + NT * P].rearrange("(o t e) -> o t e", o=1, e=P)[:, :, 0]).then_inc(first_landed, 16)
                sp.wait_ge(tab_copied, groups)
                sp.dma_start(table.rearrange("(n p) f -> p n f", p=P), nodes0[:]).then_inc(tab_stored, 16)

                def load_emb(k, b, later):
                    i = k * RING + b
                    if later:
                        sp.wait_ge(hid_mm, 4 * (i - RING + 1))
                    sp.dma_start(emb_s[:, b], emb[:, bass.ds(i * (T * P), T * P)]).then_inc(emb_landed[b], 16)

                def spill_block(k, b):
                    i = k * RING + b
                    sp.wait_ge(part_done, i + 1)
                    sp.dma_start(hid_d[:, bass.ds(i * (2 * T * P), 2 * T * P)],
                                 part[:, b % 2].rearrange("p n e -> p (n e)")).then_inc(part_stored[b % 2], 16)
                    sp.wait_ge(rows_landed[b], (k + 1) * 16 * T)
                    sp.dma_start(spill[:, bass.ds(i * (T * R0), T * R0)],
                                 rows[:, b].rearrange("p t f -> p (t f)")).then_inc(rows_spilled[b], 16)
                for b in range(RING):
                    load_emb(0, b, False)
                for b in range(RING - 1):
                    spill_block(0, b)
                with sp.Fori(1, NB // RING) as k:
                    for b in range(RING):
                        load_emb(k, b, True)
                        if b:
                            spill_block(k, b - 1)
                        else:
                            spill_block(k - 1, RING - 1)
                spill_block(NB // RING - 1, RING - 1)
                sp.wait_ge(first_landed, 32)
                for b in range(2):
                    sp.wait_ge(part_stored[b], 16 * (NB // 2))
                for b in range(RING):
                    sp.wait_ge(rows_spilled[b], 16 * (NB // RING))

            @block.gpsimd
            def _(pool):
                pool.iota(iota_i[:], pattern=[[1, P]], base=0, channel_multiplier=0).then_inc(iota_made, 1)
                pool.iota(part_i[:], pattern=[[0, 1]], base=0, channel_multiplier=1).then_inc(iota_made, 1)
                pool.wait_ge(idx_landed, 16)
                pool.wait_ge(tab_stored, 16)

                def gather_block(k, b, later):
                    i = k * RING + b
                    if later:
                        pool.wait_ge(rows_spilled[b], k * 16)
                        pool.wait_ge(rows_split, i - RING + 1)
                    pool.tensor_copy(idx_b[:, b], idx_all[:, bass.ds(i * T, T), 0]).then_inc(idx_copied, 1)
                    pool.wait_ge(idx_copied, i + 1)
                    pool.nop(nofuse=True)
                    for t in range(T):
                        pool.indirect_dma_start(rows[:, b, t], None, table,
                                                bass.IndirectOffsetOnAxis(ap=idx_b[:, b, t:t + 1], axis=0)
                                                ).then_inc(rows_landed[b], 16)
                for b in range(RING):
                    gather_block(0, b, False)
                with pool.Fori(1, NB // RING) as k:
                    for b in range(RING):
                        gather_block(k, b, True)

            @block.tensor
            def _(pe):
                pe.wait_ge(w_landed, 80)
                pe.matmul(p_att[0:F, 0:2], wT_s[:], att_s[:], start=True, stop=True).then_inc(att_mm, 1)
                pe.wait_ge(att_copied, 1)
                pe.wait_ge(xT_landed, 16)
                for g in range(groups):
                    if g >= 2:
                        pe.wait_ge(tab_copied, g - 1)
                    for j in range(NG):
                        n = g * NG + j
                        mm = pe.matmul(p_tab[g % 2][:, j * R0:(j + 1) * R0], xT_s[:, n * P:(n + 1) * P], w_s[:],
                                       start=True, stop=True)
                    mm.then_inc(tab_mm, 1)

                def hidden(k, b, later):
                    i = k * RING + b
                    pe.wait_ge(emb_landed[b], (k + 1) * 16)
                    for n in range(2):
                        for h in range(2):
                            if later or b:
                                pe.wait_ge(hid_done, 4 * (i - 1) + 2 * n + h + 1)
                            pe.matmul(p_hid[n][h][0:K6, :], fc1_s[:, n], emb_s[:, b, h * 512:(h + 1) * 512],
                                      start=True, stop=True).then_inc(hid_mm, 1)
                for b in range(RING):
                    hidden(0, b, False)
                with pe.Fori(1, NB // RING) as k:
                    for b in range(RING):
                        hidden(k, b, True)

            @block.scalar
            def _(act):
                def hidden(k, b, later):
                    i = k * RING + b
                    r = b % 2
                    if later or b >= 2:
                        act.wait_ge(part_done, i - 1)
                    for n in range(2):
                        for h in range(2):
                            act.wait_ge(hid_mm, 4 * i + 2 * n + h + 1)
                            act.activation(hid[:, r, n, h * 512:(h + 1) * 512], p_hid[n][h][0:K6, :], ACT.Relu,
                                           scale=float(1.0 / np.sqrt(EMB))).then_inc(hid_done, 1)
                    act.wait_ge(hid_done, 4 * (i + 1))
                    act.activation(top[:, r], hid[:, r], ACT.Copy).then_inc(top_done, 1)

                def middle(k, b, i):
                    act.wait_ge(less_done, i + 1)
                    act.activation(top[:, b % 2], hid[:, b % 2], ACT.Copy).then_inc(mid_done, 1)
                hidden(0, 0, False)
                for b in range(1, RING):
                    hidden(0, b, False)
                    middle(0, b - 1, b - 1)
                with act.Fori(1, NB // RING) as k:
                    for b in range(RING):
                        hidden(k, b, True)
                        middle(k, b - 1, k * RING + b - 1)
                middle(0, RING - 1, NB - 1)

            @block.vector
            def _(dve):
                dve.wait_ge(iota_made, 2)
                dve.tensor_copy(part_f[:], part_i[:]).then_inc(part_cast, 1)
                dve.tensor_copy(iota_n[:], iota_i[:]).then_inc(part_cast, 1)
                dve.wait_ge(part_cast, 2)
                dve.tensor_scalar(ident[:], iota_n[:], part_f[:, 0:1], None, ALU.is_equal).then_inc(consts_made, 1)
                dve.wait_ge(att_mm, 1)
                dve.tensor_copy(w_s[:, F:R0], p_att[0:F, 0:2]).then_inc(att_copied, 1)
                for g in range(groups):
                    dve.wait_ge(tab_mm, g + 1)
                    dve.tensor_copy(nodes0[:, g * NG:(g + 1) * NG, :].rearrange("p n f -> p (n f)"),
                                    p_tab[g % 2][:, 0:NG * R0]).then_inc(tab_copied, 1)

                def split_block(k, b):
                    i = k * RING + b
                    dve.wait_ge(rows_landed[b], (k + 1) * 16 * T)
                    dve.tensor_copy(asd[:, :, bass.ds(i * T, T)],
                                    rows[:, b, :, F:R0].rearrange("p t two -> p two t")).then_inc(rows_split, 1)

                def less(k, b, i):
                    r = b % 2
                    dve.wait_ge(top_done, i + 1)
                    dve.scalar_tensor_tensor(out=hid[:, r], in0=top[:, r], scalar=parts_s[:, 0:1], in1=hid[:, r],
                                             op0=ALU.mult, op1=ALU.add).then_inc(less_done, 1)

                def lowest(k, b, i, first):
                    r = b % 2
                    dve.wait_ge(mid_done, i + 1)
                    if not first:
                        dve.wait_ge(part_stored[r], stored(k, b))
                    dve.scalar_tensor_tensor(out=part[:, r], in0=top[:, r], scalar=parts_s[:, 1:2], in1=hid[:, r],
                                             op0=ALU.mult, op1=ALU.add).then_inc(part_done, 1)

                def stored(k, b):
                    return 32 * k + 16 * (b // 2)

                for b in range(RING):
                    less(0, b, b)
                    if b:
                        lowest(0, b - 1, b - 1, b - 1 < 2)
                    split_block(0, b)
                with dve.Fori(1, NB // RING) as k:
                    for b in range(RING):
                        less(k, b, k * RING + b)
                        if b:
                            lowest(k, b - 1, k * RING + b - 1, False)
                        else:
                            lowest(k - 1, RING - 1, k * RING - 1, False)
                        split_block(k, b)
                lowest(NB // RING - 1, RING - 1, NB - 1, False)
                dve.wait_ge(rows_split, NB)

        ex_e = asd
        with ExitStack() as st:
            sb, ps, sem = maker(st)
            BEFORE, AFTER, SRC, SELF, LAST, CUR = range(6)
            big = sb("big", [P, 6, NC * P])
            big_i = big[:].bitcast(I32)
            aT = sb("aT", [P, 2, NC * P])
            pen = sb("pen", [P, 2, NC * P])
            scan = sb("scan", [P, 4, NC * P])
            ends = sb("ends", [P, 4, NC])
            carry = sb("carry", [P, 4, NC])
            row_i = sb("row_i", [1, 4, NT], I32)
            row_pen = sb("row_pen", [1, 4, NT])
            row_in = big[0:1, 0:4, :]
            row_out = row_i[:].bitcast(F32)
            ones = sb("ones", [1, P])
            p_t = [ps(f"p_t{j}") for j in range(4)]

            dst_loaded, row_loaded, a_mm, a_copied, d = (
                sem("dst_loaded"), sem("row_loaded"), sem("a_mm"), sem("a_copied"), sem("d"))
            base_row, base_mm, ends_made, ends_out, rows_in, carry_made, carry_out, carry_in = (
                sem("base_row"), sem("base_mm"), sem("ends_made"), sem("ends_out"), sem("rows_in"),
                sem("carry_made"), sem("carry_out"), sem("carry_in"))
            exponent_made, exp_done, max_made, ex_mm, ex_copied = (
                sem("exponent_made"), sem("exp_done"), sem("max_made"), sem("ex_mm"), sem("ex_copied"))
            quarters = -(-NT // 512)

            block = st.enter_context(nc.Block())

            @block.sync
            def _(sp):
                for j, at in ((BEFORE, 0), (CUR, 1), (AFTER, 2)):
                    sp.dma_start(big_i[:, j].rearrange("p (c e) -> p c e", e=P),
                                 dst_ext[at:at + NT * P].rearrange("(c p e) -> p c e", p=P, e=P)).then_inc(dst_loaded, 16)
                sp.dma_start(big_i[:, SRC].rearrange("p (c e) -> p c e", e=P),
                             src_flat.rearrange("(c p e) -> p c e", p=P, e=P)).then_inc(dst_loaded, 16)
                for j, at in enumerate((0, 1, P, P + 1)):
                    sp.dma_start(row_i[:, j], dst_ext[at:at + NT * P].rearrange("(o t e) -> o t e", o=1, e=P)[:, :, 0]
                                 ).then_inc(row_loaded, 16)
                sp.wait_ge(ends_made, 1)
                for j in range(4):
                    sp.dma_start(ends_d[j].rearrange("(c p) -> p c", p=P), ends[:, j]).then_inc(ends_out, 16)
                sp.wait_ge(ends_out, 64)
                sp.dma_start(row_in, ends_d.rearrange("(o j) t -> o j t", o=1)).then_inc(rows_in, 16)
                sp.wait_ge(carry_made, 1)
                sp.dma_start(carry_d.rearrange("(o j) t -> o j t", o=1), row_out).then_inc(carry_out, 16)
                sp.wait_ge(carry_out, 16)
                for j in range(4):
                    sp.dma_start(carry[:, j], carry_d[j].rearrange("(c p) -> p c", p=P)).then_inc(carry_in, 16)
                sp.wait_ge(carry_in, 64)

            @block.tensor
            def _(pe):
                for m in range(2 * NC):
                    if m >= 4:
                        pe.wait_ge(a_copied, m - 3)
                    pe.transpose(p_t[m % 4][:, 0:P], asd[:, m // NC, m % NC * P:(m % NC + 1) * P], ident[:]).then_inc(a_mm, 1)
                pe.wait_ge(base_row, 1)
                for q in range(quarters):
                    wq = min(512, NT - q * 512)
                    pe.wait_ge(a_copied, 2 * NC + q)
                    pe.matmul(p_t[0][:, 0:wq], ones[:], row_pen[:, 0, q * 512:q * 512 + wq], start=True, stop=True
                              ).then_inc(base_mm, 1)
                pe.wait_ge(a_copied, 2 * NC + quarters)
                pe.wait_ge(exp_done, 1)
                pe.wait_ge(max_made, 1)
                for m in range(2 * NC):
                    if m >= 4:
                        pe.wait_ge(ex_copied, m - 3)
                    pe.transpose(p_t[m % 4][:, 0:P], aT[:, m // NC, m % NC * P:(m % NC + 1) * P], ident[:]).then_inc(ex_mm, 1)

            @block.scalar
            def _(act):
                act.wait_ge(exponent_made, 1)
                act.activation(aT[:, 0], big[:, AFTER], ACT.Exp).then_inc(exp_done, 1)

            @block.vector
            def _(dve):
                done = [0]

                def then(ins):
                    done[0] += 1
                    ins.then_inc(d, 1)
                    dve.wait_ge(d, done[0])

                def chunks(ap):
                    return ap.rearrange("p (c e) -> p c e", e=P)

                for m in range(2 * NC):
                    dve.wait_ge(a_mm, m + 1)
                    dve.tensor_copy(aT[:, m // NC, m % NC * P:(m % NC + 1) * P], p_t[m % 4][:, 0:P]).then_inc(a_copied, 1)
                then(dve.memset(ones[:], 1.0))
                dve.wait_ge(row_loaded, 64)
                then(dve.tensor_copy(row_pen[:, 0], row_i[:, 1]))
                dve.sem_inc(base_row, 1)
                then(dve.tensor_copy(local[:], idx_all[:, :, 1]))
                for q in range(quarters):
                    wq = min(512, NT - q * 512)
                    dve.wait_ge(base_mm, q + 1)
                    dve.tensor_tensor(local[:, q * 512:q * 512 + wq], local[:, q * 512:q * 512 + wq],
                                      p_t[0][:, 0:wq], ALU.subtract).then_inc(a_copied, 1)
                dve.wait_ge(a_copied, 2 * NC + quarters)
                dve.wait_ge(dst_loaded, 64)
                then(dve.tensor_tensor(big[:, LAST], big_i[:, CUR], big_i[:, AFTER], ALU.not_equal))
                then(dve.tensor_tensor(pen[:, 0], big_i[:, CUR], big_i[:, BEFORE], ALU.not_equal))
                then(dve.tensor_scalar(pen[:, 0], pen[:, 0], -BIG, None, ALU.mult))
                then(dve.tensor_scalar(pen[:, 1], big[:, LAST], -BIG, None, ALU.mult))
                then(dve.memset(chunks(pen[:, 0])[:, :, 0], -BIG))
                then(dve.memset(chunks(pen[:, 1])[:, :, P - 1], -BIG))
                then(dve.tensor_tensor(big[:, SELF], big_i[:, SRC], big_i[:, CUR], ALU.is_equal))
                then(dve.tensor_scalar(big[:, AFTER], big[:, SELF], BIG, -BIG, ALU.mult, ALU.add))
                then(dve.tensor_tensor(big[:, SELF], big[:, SELF], aT[:, 1], ALU.mult))
                then(dve.tensor_tensor(big[:, SELF], big[:, SELF], big[:, AFTER], ALU.add))
                for j, a in ((0, aT[:, 0]), (1, big[:, SELF])):
                    then(dve.tensor_tensor_scan(scan[:, j], pen[:, 0], a, -BIG, ALU.add, ALU.max))
                    then(dve.tensor_tensor_scan(scan[:, 2 + j, ::-1], pen[:, 1, ::-1], a[:, ::-1], -BIG, ALU.add, ALU.max))
                then(dve.tensor_copy(ends[:, 0:2], scan[:, 0:2].rearrange("p j (c e) -> p j c e", e=P)[:, :, :, P - 1]))
                then(dve.tensor_copy(ends[:, 2:4], scan[:, 2:4].rearrange("p j (c e) -> p j c e", e=P)[:, :, :, 0]))
                dve.sem_inc(ends_made, 1)
                last_before, first, last, first_after = (row_i[:, j] for j in range(4))
                for j, (one, other) in enumerate(((last, last_before), (first, first_after),
                                                  (first, last_before), (last, first_after))):
                    then(dve.tensor_tensor(row_pen[:, j], one, other, ALU.not_equal))
                then(dve.tensor_scalar(row_pen[:], row_pen[:], -BIG, None, ALU.mult))
                then(dve.memset(row_out, -BIG))
                dve.wait_ge(rows_in, 16)
                for j in range(2):
                    then(dve.tensor_tensor_scan(row_in[:, j], row_pen[:, 0], row_in[:, j], -BIG, ALU.add, ALU.max))
                    then(dve.tensor_tensor_scan(row_in[:, 2 + j, ::-1], row_pen[:, 1, ::-1],
                                                row_in[:, 2 + j, ::-1], -BIG, ALU.add, ALU.max))
                    then(dve.tensor_tensor(row_out[:, j, 1:NT], row_in[:, j, 0:NT - 1], row_pen[:, 2, 1:NT], ALU.add))
                    then(dve.tensor_tensor(row_out[:, 2 + j, 0:NT - 1], row_in[:, 2 + j, 1:NT], row_pen[:, 3, 0:NT - 1],
                                           ALU.add))
                dve.sem_inc(carry_made, 1)
                cur3 = chunks(big_i[:, CUR])
                for j, at in ((0, 0), (1, P - 1)):
                    then(dve.tensor_tensor(chunks(pen[:, j]), cur3, cur3[:, :, at:at + 1].to_broadcast([P, NC, P]),
                                           ALU.not_equal))
                then(dve.tensor_scalar(pen[:], pen[:], -BIG, None, ALU.mult))
                dve.wait_ge(carry_in, 64)
                for j in range(4):
                    then(dve.tensor_tensor(chunks(big[:, BEFORE]), chunks(pen[:, j // 2]),
                                           carry[:, j].unsqueeze(2).to_broadcast([P, NC, P]), ALU.add))
                    then(dve.tensor_tensor(scan[:, j], scan[:, j], big[:, BEFORE], ALU.max))
                then(dve.tensor_tensor(scan[:, 0:2], scan[:, 0:2], scan[:, 2:4], ALU.max))
                then(dve.tensor_tensor(pen[:, 0], scan[:, 0], scan[:, 1], ALU.add))
                then(dve.tensor_tensor(pen[:, 1], aT[:, 0], scan[:, 1], ALU.add))
                then(dve.scalar_tensor_tensor(out=pen[:], in0=pen[:], scalar=SLOPE, in1=pen[:], op0=ALU.mult, op1=ALU.max))
                then(dve.tensor_tensor(big[:, AFTER], pen[:, 1], pen[:, 0], ALU.subtract))
                dve.sem_inc(exponent_made, 1)
                then(dve.tensor_tensor(aT[:, 1], big[:, LAST], pen[:, 0], ALU.mult))
                dve.sem_inc(max_made, 1)
                for m in range(2 * NC):
                    dve.wait_ge(ex_mm, m + 1)
                    dve.tensor_copy(ex_e[:, m // NC, m % NC * P:(m % NC + 1) * P], p_t[m % 4][:, 0:P]).then_inc(ex_copied, 1)
                dve.wait_ge(ex_copied, 2 * NC)

        acc = layer0.enter_context(nc.sbuf_tensor("acc", [R0, ACC], F32))
        with ExitStack() as st:
            sb, ps, sem = maker(st)
            rows = sb("rows3", [P, RING, T, R0])
            z = sb("z3", [P, RING, T, R0])
            hot = sb("hot3", [P, RING, T, P])
            diff = sb("diff3", [P, RING, T, P])
            win = [[ps(f"win3_{a}{h}") for h in range(2)] for a in range(2)]
            acc_zeroed, z_made, hot_made, win_mm, win_added = (
                sem("acc_zeroed"), sem("z_made"), sem("hot_made"), sem("win_mm"), sem("win_added"))
            diff_made, abs_made = sem("diff_made"), sem("abs_made")
            back = [sem(f"back{b}") for b in range(RING)]

            block = st.enter_context(nc.Block())

            @block.sync
            def _(sp):
                def load_block(k, b, later):
                    i = k * RING + b
                    if later:
                        sp.wait_ge(z_made, 2 * (i - RING + 1))
                    sp.dma_start(rows[:, b].rearrange("p t f -> p (t f)"),
                                 spill[:, bass.ds(i * (T * R0), T * R0)]).then_inc(back[b], 16)
                for b in range(RING):
                    load_block(0, b, False)
                with sp.Fori(1, NB // RING) as k:
                    for b in range(RING):
                        load_block(k, b, True)

            @block.gpsimd
            def _(pool):
                def offsets(k, b, later):
                    i = k * RING + b
                    if later:
                        pool.wait_ge(hot_made, i - RING + 1)
                    pool.tensor_tensor(diff[:, b], iota_n[:].unsqueeze(1).to_broadcast([P, T, P]),
                                       local[:, bass.ds(i * T, T)].unsqueeze(2).to_broadcast([P, T, P]),
                                       ALU.subtract).then_inc(diff_made, 1)
                for b in range(RING):
                    offsets(0, b, False)
                with pool.Fori(1, NB // RING) as k:
                    for b in range(RING):
                        offsets(k, b, True)

            @block.scalar
            def _(act):
                def one_hot(k, b, later):
                    i = k * RING + b
                    act.wait_ge(diff_made, i + 1)
                    act.activation(diff[:, b], diff[:, b], ACT.Abs).then_inc(abs_made, 1)
                    if later:
                        act.wait_ge(win_mm, i - RING + 1)
                    act.wait_ge(abs_made, i + 1)
                    act.activation(hot[:, b], diff[:, b], ACT.Relu, scale=-1.0, bias=1.0).then_inc(hot_made, 1)
                for b in range(RING):
                    one_hot(0, b, False)
                with act.Fori(1, NB // RING) as k:
                    for b in range(RING):
                        one_hot(k, b, True)

            @block.tensor
            def _(pe):
                def windows(k, b, later):
                    i = k * RING + b
                    pe.wait_ge(z_made, 2 * (i + 1))
                    pe.wait_ge(hot_made, i + 1)
                    if later or b >= 2:
                        pe.wait_ge(win_added, T * (i - 1))
                    for t in range(T):
                        mm = pe.matmul(win[b % 2][t // 4][0:R0, (t % 4) * P:(t % 4 + 1) * P], z[:, b, t], hot[:, b, t],
                                       start=True, stop=True)
                    mm.then_inc(win_mm, 1)
                for b in range(RING):
                    windows(0, b, False)
                with pe.Fori(1, NB // RING) as k:
                    for b in range(RING):
                        windows(k, b, True)

            @block.vector
            def _(dve):
                dve.memset(acc[:], 0.0).then_inc(acc_zeroed, 1)
                dve.wait_ge(acc_zeroed, 1)

                def weigh(k, b, later):
                    i = k * RING + b
                    if later:
                        dve.wait_ge(win_mm, i - RING + 1)
                    dve.wait_ge(back[b], (k + 1) * 16)
                    dve.tensor_tensor(z[:, b, :, 0:F], rows[:, b, :, 0:F],
                                      ex_e[:, 0, bass.ds(i * T, T)].unsqueeze(2).to_broadcast([P, T, F]),
                                      ALU.mult).then_inc(z_made, 1)
                    dve.tensor_copy(z[:, b, :, F:R0].rearrange("p t two -> p two t"),
                                    ex_e[:, :, bass.ds(i * T, T)]).then_inc(z_made, 1)

                def add(k, b, first):
                    i = k * RING + b
                    dve.wait_ge(win_mm, i + 1)
                    for t in range(T):
                        base = dve.value_load(first_i[0:1, bass.ds(i * T + t, 1)], min_val=0, max_val=ACC - P)
                        if not first or t:
                            dve.wait_ge(win_added, T * i + t)
                        dve.tensor_tensor(acc[:, bass.ds(base, P)], acc[:, bass.ds(base, P)],
                                          win[b % 2][t // 4][0:R0, (t % 4) * P:(t % 4 + 1) * P], ALU.add
                                          ).then_inc(win_added, 1)
                weigh(0, 0, False)
                for b in range(RING - 1):
                    weigh(0, b + 1, False)
                    add(0, b, b == 0)
                with dve.Fori(1, NB // RING) as k:
                    weigh(k, 0, True)
                    add(k - 1, RING - 1, False)
                    for b in range(RING - 1):
                        weigh(k, b + 1, True)
                        add(k, b, False)
                add(NB // RING - 1, RING - 1, False)
                dve.wait_ge(win_added, T * NB)

        def layernorm(then, dve, act_done, want_sqrt, y, stat, sq):
            mean, var = stat[:, 0], stat[:, 1]
            then(dve.tensor_reduce(mean, y, AX_X, ALU.add))
            then(dve.tensor_scalar(mean, mean, 1.0 / F, None, ALU.mult))
            then(dve.tensor_tensor(y, y, mean.unsqueeze(2).to_broadcast([P, NN, F]), ALU.subtract))
            then(dve.tensor_tensor(sq, y, y, ALU.mult))
            then(dve.tensor_reduce(var, sq, AX_X, ALU.add))
            then(dve.tensor_scalar(var, var, 1.0 / F, EPS, ALU.mult, ALU.add))
            dve.sem_inc(want_sqrt, 1)
            dve.wait_ge(act_done, 1)
            then(dve.reciprocal(var, mean))
            then(dve.tensor_tensor(y, y, var.unsqueeze(2).to_broadcast([P, NN, F]), ALU.mult))

        with ExitStack() as st:
            sb, ps, sem = maker(st)
            xn = sb("xn", [P, NN, F])
            sums = sb("sums", [P, NN, R0])
            sq = sb("sq", [P, NN, F])
            x1 = sb("x1", [P, NN, F])
            stat = sb("stat", [P, 4, NN])
            p_n = [ps("p_n0"), ps("p_n1")]
            x_landed, sums_mm, sums_copied, d4, self_ready, self_exp, want_sqrt, got_sqrt, x1_made, x1_stored = (
                sem("x_landed"), sem("sums_mm"), sem("sums_copied"), sem("d4"), sem("self_ready"), sem("self_exp"),
                sem("want_sqrt"), sem("got_sqrt"), sem("x1_made"), sem("x1_stored"))

            block = st.enter_context(nc.Block())

            @block.sync
            def _(sp):
                sp.dma_start(xn[:], xN.rearrange("(n p) f -> p n f", p=P)).then_inc(x_landed, 16)
                sp.wait_ge(x1_made, 1)
                sp.dma_start(table1.rearrange("(n p) f -> p n f", p=P), x1[:]).then_inc(x1_stored, 16)
                sp.wait_ge(x1_stored, 16)

            @block.tensor
            def _(pe):
                for g in range(NN // NG):
                    if g >= 2:
                        pe.wait_ge(sums_copied, g - 1)
                    for j in range(NG):
                        n = g * NG + j
                        mm = pe.transpose(p_n[g % 2][:, j * R0:(j + 1) * R0], acc[:, n * P:(n + 1) * P],
                                          ident[0:R0, 0:R0])
                    mm.then_inc(sums_mm, 1)

            @block.scalar
            def _(act):
                act.wait_ge(self_ready, 1)
                act.activation(stat[:, 1], stat[:, 0], ACT.Exp).then_inc(self_exp, 1)
                act.wait_ge(want_sqrt, 1)
                act.activation(stat[:, 0], stat[:, 1], ACT.Sqrt).then_inc(got_sqrt, 1)

            @block.vector
            def _(dve):
                done = [0]

                def then(ins):
                    done[0] += 1
                    ins.then_inc(d4, 1)
                    dve.wait_ge(d4, done[0])

                for g in range(NN // NG):
                    dve.wait_ge(sums_mm, g + 1)
                    dve.tensor_copy(sums[:, g * NG:(g + 1) * NG].rearrange("p n f -> p (n f)"),
                                    p_n[g % 2][:, 0:NG * R0]).then_inc(sums_copied, 1)
                dve.wait_ge(sums_copied, NN // NG)
                s0 = stat[:, 0]
                then(dve.tensor_tensor(s0, nodes0[:, :, F], nodes0[:, :, F + 1], ALU.add))
                then(dve.scalar_tensor_tensor(out=s0, in0=s0, scalar=SLOPE, in1=s0, op0=ALU.mult, op1=ALU.max))
                then(dve.tensor_tensor(s0, s0, sums[:, :, F + 1], ALU.subtract))
                dve.sem_inc(self_ready, 1)
                dve.wait_ge(self_exp, 1)
                s1 = stat[:, 1]
                then(dve.tensor_tensor(x1[:], nodes0[:, :, 0:F], s1.unsqueeze(2).to_broadcast([P, NN, F]), ALU.mult))
                then(dve.tensor_tensor(x1[:], x1[:], sums[:, :, 0:F], ALU.add))
                then(dve.tensor_tensor(stat[:, 2], sums[:, :, F], s1, ALU.add))
                then(dve.reciprocal(stat[:, 3], stat[:, 2]))
                then(dve.tensor_tensor(x1[:], x1[:], stat[:, 3].unsqueeze(2).to_broadcast([P, NN, F]), ALU.mult))
                then(dve.tensor_tensor(x1[:], x1[:], bias_b[:].unsqueeze(1).to_broadcast([P, NN, F]), ALU.add))
                dve.wait_ge(x_landed, 16)
                then(dve.tensor_tensor(x1[:], x1[:], xn[:], ALU.add))
                layernorm(then, dve, got_sqrt, want_sqrt, x1[:], stat, sq[:])
                dve.sem_inc(x1_made, 1)

        layer0.close()

        acc = outer.enter_context(nc.sbuf_tensor("acc1", [F, ACC], F32))
        edge_layer(nc, maker, NB, NT, ACC, local, first_i, iota_n, ident, acc, table1,
                   idx, hid_d, vec, weight, w2, parts_s)

        with ExitStack() as st:
            sb, ps, sem = maker(st)
            y = sb("y6", [P, NN, F])
            x1 = sb("x1_again", [P, NN, F])
            sq = sb("sq6", [P, NN, F])
            stat = sb("stat6", [P, 2, NN])
            p_n = [ps("p_m0"), ps("p_m1")]
            sums6_mm, sums6_copied, d6, want6, got6, y_made, y_stored, x1_back = (
                sem("sums6_mm"), sem("sums6_copied"), sem("d6"), sem("want6"), sem("got6"), sem("y_made"), sem("y_stored"),
                sem("x1_back"))

            block = st.enter_context(nc.Block())

            @block.sync
            def _(sp):
                sp.dma_start(x1[:], table1.rearrange("(n p) f -> p n f", p=P)).then_inc(x1_back, 16)
                sp.wait_ge(y_made, 1)
                sp.dma_start(out.rearrange("(n p) f -> p n f", p=P), y[:]).then_inc(y_stored, 16)
                sp.wait_ge(y_stored, 16)

            @block.tensor
            def _(pe):
                for g in range(NN // NG):
                    if g >= 2:
                        pe.wait_ge(sums6_copied, g - 1)
                    for j in range(NG):
                        n = g * NG + j
                        mm = pe.transpose(p_n[g % 2][:, j * F:(j + 1) * F], acc[0:F, n * P:(n + 1) * P],
                                          ident[0:F, 0:F])
                    mm.then_inc(sums6_mm, 1)

            @block.scalar
            def _(act):
                act.wait_ge(want6, 1)
                act.activation(stat[:, 0], stat[:, 1], ACT.Sqrt).then_inc(got6, 1)

            @block.vector
            def _(dve):
                done = [0]

                def then(ins):
                    done[0] += 1
                    ins.then_inc(d6, 1)
                    dve.wait_ge(d6, done[0])

                dve.wait_ge(x1_back, 16)
                for g in range(NN // NG):
                    dve.wait_ge(sums6_mm, g + 1)
                    dve.tensor_tensor(y[:, g * NG:(g + 1) * NG].rearrange("p n f -> p (n f)"),
                                      p_n[g % 2][:, 0:NG * F],
                                      x1[:, g * NG:(g + 1) * NG].rearrange("p n f -> p (n f)"), ALU.add
                                      ).then_inc(sums6_copied, 1)
                dve.wait_ge(sums6_copied, NN // NG)
                layernorm(then, dve, got6, want6, y[:], stat, sq[:])
                dve.sem_inc(y_made, 1)


def edge_layer(nc, maker, NB, NT, ACC, local, first_i, iota_n, ident, acc, table1,
               idx, hid_d, vec, weight, w2, parts_s):
    U = 2 * T
    OA = 48
    G = 8
    with ExitStack() as st:
        sb, ps, sem = maker(st)
        vec_s = sb("vec_s", [P, NT, 3])
        weight_s = sb("weight_s", [P, NT])
        w_f = sb("w_f", [K6, 896])
        w_top = sb("w_top", [K6, 896], BF16)
        w_part = sb("w_part", [K6, 896], BF16)
        hid = sb("hid5", [K6, RING, 2, T * P], BF16)
        idx_b = sb("idx_b5", [P, RING, T, 2], I32)
        ends = sb("ends5", [P, RING, T, 2, F])
        s1 = sb("s1", [P, 2, T, 16])
        v1 = sb("v1", [P, 2, T, 3, 16])
        vr = sb("vr", [P, T, 3, 16])
        vdot = sb("vdot", [P, 2, T, 16])
        prod = sb("prod", [P, 2, T, 16, OA])
        suma = sb("suma", [P, 2, T, OA])
        in_b = sb("in_b", [P, T, 16])
        vt = sb("vt", [P, T, 3, 8])
        vt_r = sb("vt_r", [P, T, 3, 8])
        prodb = sb("prodb", [P, 4, 512])
        gs = sb("gs", [P, 2, T, 16])
        cv = sb("cv", [P, 2, T, 32])
        th = sb("th", [P, 2, T, 16])
        msg = sb("msg", [P, T, 3, 8])
        z = sb("z5", [P, 2, T, F])
        hot = sb("hot5", [P, 2, T, P])
        absd = sb("absd", [P, T, P])
        flat = prod[:].rearrange("p a t u o -> p (a t u o)")
        sq = flat[:, 0:NT * 3].rearrange("p (t k) -> p t k", k=3)
        length, root = flat[:, NT * 3:NT * 4], flat[:, NT * 4:NT * 5]
        p_wa = [ps("p_wa0"), ps("p_wa1")]
        p_wb = [ps("p_wb0"), ps("p_wb1")]
        p_sum = ps("p_sum")
        p_win = [ps("p_win0"), ps("p_win1")]

        const_landed, vec_landed, weight_landed = sem("const_landed"), sem("vec_landed"), sem("weight_landed")
        hid_landed = [sem(f"hid_landed{b}") for b in range(RING)]
        idx_landed5 = [sem(f"idx_landed5_{b}") for b in range(RING)]
        ends_landed = [sem(f"ends_landed{b}") for b in range(RING)]
        ends_read = sem("ends_read")
        wa_mm, wa_used, wb_mm, wb_used = (
            sem("wa_mm"), sem("wa_used"), sem("wb_mm"), sem("wb_used"))
        suma_mm, suma_copied, split_done, dir_step, dir_want, dir_root = (
            sem("suma_mm"), sem("suma_copied"), sem("split_done"), sem("dir_step"), sem("dir_want"), sem("dir_root"))
        vr_done, vdot_done, mid_done, prodb_done, sumb_done, th_done, z_done, msg_done = (
            sem("vr_done"), sem("vdot_done"), sem("mid_done"), sem("prodb_done"), sem("sumb_done"), sem("th_done"),
            sem("z_done"), sem("msg_done"))
        abs_done, hot_done, win_mm5, win_added5 = sem("abs_done"), sem("hot_done"), sem("win_mm5"), sem("win_added5")
        acc_zeroed5, weights_split = sem("acc_zeroed5"), sem("weights_split")

        block = st.enter_context(nc.Block())

        def run(eng, body):
            for b in range(RING):
                body(0, b, b)
            with eng.Fori(1, NB // RING - 1) as k:
                for b in range(RING):
                    body(k, b, None)
            for b in range(RING):
                body(NB // RING - 1, b, NB - RING + b)
            for b in range(2):
                body(NB // RING, b, NB + b)

        def has(lo, lag):
            return lo is None or 0 <= lo - lag < NB

        @block.sync
        def _(sp):
            sp.dma_start(w_f[:], w2).then_inc(const_landed, 16)
            sp.dma_start(vec_s[:].rearrange("p t k -> p (t k)"), vec).then_inc(vec_landed, 16)
            sp.dma_start(weight_s[:], weight).then_inc(weight_landed, 16)

            def body(k, b, lo):
                i = k * RING + b
                if not has(lo, 0):
                    return
                if lo is None or lo >= RING:
                    sp.wait_ge(wb_mm, (i - RING + 1) * T)
                    sp.wait_ge(ends_read, i - RING + 1)
                sp.dma_start(idx_b[:, b].rearrange("p t two -> p (t two)"), idx[:, bass.ds(i * (2 * T), 2 * T)]
                             ).then_inc(idx_landed5[b], 16)
                sp.dma_start(hid[:, b].rearrange("p n e -> p (n e)"), hid_d[:, bass.ds(i * (2 * T * P), 2 * T * P)]
                             ).then_inc(hid_landed[b], 16)
            run(sp, body)

        @block.gpsimd
        def _(pool):
            def body(k, b, lo):
                i = k * RING + b
                if not has(lo, 0):
                    return
                if lo is None or lo >= RING:
                    pool.wait_ge(ends_read, i - RING + 1)
                pool.wait_ge(idx_landed5[b], 16 * (k + 1))
                pool.nop(nofuse=True)
                for t in range(T):
                    for j in range(2):
                        pool.indirect_dma_start(ends[:, b, t, j], None, table1,
                                                bass.IndirectOffsetOnAxis(ap=idx_b[:, b, t, j:j + 1], axis=0)
                                                ).then_inc(ends_landed[b], 16)
            run(pool, body)

        @block.tensor
        def _(pe):
            def body(k, b, lo):
                i = k * RING + b
                for t in range(T):
                    if has(lo, 0):
                        if t == 0:
                            pe.wait_ge(hid_landed[b], 16 * (k + 1))
                        if lo is None or lo or t >= 2:
                            pe.wait_ge(wa_used, i * T + t - 1)
                        pe.matmul(p_wa[t % 2][:], hid[:, b, 0, t * P:(t + 1) * P], w_part[:, 0:512], start=True, stop=True
                                  ).then_inc(wa_mm, 1)
                    if has(lo, 1):
                        if t == 0:
                            pe.wait_ge(wa_used, i * T)
                            if lo is None or lo >= 2:
                                pe.wait_ge(suma_copied, i - 1)
                        for u in (2 * t, 2 * t + 1):
                            mm = pe.matmul(p_sum[:, 0:T * OA], ident[:], prod[:, (b - 1) % 2, :, u, :],
                                           start=(u == 0), stop=(u == 15))
                        if t == T - 1:
                            mm.then_inc(suma_mm, 1)
                for t in range(T):
                    if has(lo, 1):
                        if lo is None or lo > 1 or t >= 2:
                            pe.wait_ge(wb_used, (i - 1) * T + t - 1)
                        pe.matmul(p_wb[t % 2][:, 0:384], hid[:, (b - 1) % RING, 1, t * P:(t + 1) * P], w_part[:, 512:896],
                                  start=True, stop=True).then_inc(wb_mm, 1)
                    if has(lo, 2):
                        if t == 0:
                            pe.wait_ge(z_done, i - 1)
                            pe.wait_ge(hot_done, i - 1)
                            if lo is None or lo > 2:
                                pe.wait_ge(win_added5, (i - 2) * T)
                        mm = pe.matmul(p_win[t // 4][0:F, (t % 4) * P:(t % 4 + 1) * P], z[:, b % 2, t], hot[:, b % 2, t],
                                       start=True, stop=True)
                        if t == T - 1:
                            mm.then_inc(win_mm5, 1)
            pe.wait_ge(weights_split, 1)
            run(pe, body)

        @block.scalar
        def _(act):
            act.wait_ge(dir_want, 1)
            act.activation(root, length, ACT.Sqrt).then_inc(dir_root, 1)

            def body(k, b, lo):
                i = k * RING + b
                if has(lo, 0):
                    act.wait_ge(ends_landed[b], (k + 1) * 16 * 2 * T)
                    if lo is None or lo >= 2:
                        act.wait_ge(wa_used, (i - 1) * T)
                    act.activation(s1[:, b % 2].rearrange("p t (j u) -> p t j u", j=2), ends[:, b, :, :, 0:8], ACT.Copy
                                   ).then_inc(split_done, 1)
                    for j in range(2):
                        ins = act.activation(v1[:, b % 2, :, :, 8 * j:8 * j + 8],
                                             ends[:, b, :, j, 8:F].rearrange("p t (u k) -> p t k u", k=3), ACT.Copy)
                        ins.then_inc(split_done, 1)
                    act.wait_ge(split_done, 3 * (i + 1))
                    act.sem_inc(ends_read, 1)
                if has(lo, 1):
                    act.wait_ge(suma_mm, i)
                    if lo is None or lo > 2:
                        act.wait_ge(mid_done, 5 * (i - 2))
                    act.activation(suma[:, (b - 1) % 2].rearrange("p t o -> p (t o)"), p_sum[:, 0:T * OA], ACT.Copy
                                   ).then_inc(suma_copied, 1)
                    if lo is None or lo >= 2:
                        act.wait_ge(hot_done, i - 1)
                    for t in range(T):
                        act.activation(absd[:, t], iota_n[:], ACT.Abs, bias=local[:, bass.ds((i - 1) * T + t, 1)]
                                       ).then_inc(abs_done, 1)
                    act.wait_ge(abs_done, i * T)
                    if lo is None or lo >= 3:
                        act.wait_ge(win_mm5, i - 2)
                    act.activation(hot[:, (b - 1) % 2], absd[:], ACT.Relu, scale=-1.0, bias=1.0).then_inc(hot_done, 1)
                    act.wait_ge(sumb_done, i * 2 * T)
                    if lo is None or lo >= 3:
                        act.wait_ge(z_done, i - 2)
                    act.activation(th[:, (b - 1) % 2], gs[:, (b - 1) % 2], ACT.Tanh).then_inc(th_done, 1)
            run(act, body)

        @block.vector
        def _(dve):
            done = [0]

            def then(ins):
                done[0] += 1
                ins.then_inc(dir_step, 1)
                dve.wait_ge(dir_step, done[0])

            dve.memset(acc[:], 0.0).then_inc(acc_zeroed5, 1)
            dve.wait_ge(const_landed, 16)
            sa, sb_ = 1.0 / np.sqrt(H) / np.sqrt(32.0), 1.0 / np.sqrt(H) / np.sqrt(16.0)
            for a, b, scale in ((0, 128, sa), (128, 256, sa * np.sqrt(3.0)), (256, 512, sa), (512, 768, sb_),
                                (768, 832, sb_ * np.sqrt(3.0)), (832, 896, sb_)):
                then(dve.tensor_scalar(w_f[:, a:b], w_f[:, a:b], float(scale), None, ALU.mult))
            then(dve.tensor_copy(w_top[:], w_f[:]))
            then(dve.scalar_tensor_tensor(out=w_f[:], in0=w_top[:], scalar=parts_s[:, 2:3], in1=w_f[:],
                                          op0=ALU.mult, op1=ALU.add))
            then(dve.tensor_copy(w_top[:], w_f[:]))
            then(dve.scalar_tensor_tensor(out=w_part[:], in0=w_top[:], scalar=parts_s[:, 3:4], in1=w_f[:],
                                          op0=ALU.mult, op1=ALU.add))
            dve.sem_inc(weights_split, 1)
            dve.wait_ge(vec_landed, 16)
            then(dve.tensor_tensor(sq, vec_s[:], vec_s[:], ALU.mult))
            then(dve.tensor_reduce(length, sq, AX_X, ALU.add))
            dve.sem_inc(dir_want, 1)
            dve.wait_ge(dir_root, 1)
            then(dve.reciprocal(length, root))
            then(dve.tensor_tensor(vec_s[:], vec_s[:], length.unsqueeze(2).to_broadcast([P, NT, 3]), ALU.mult))
            then(dve.tensor_scalar(local[:], local[:], -1.0, None, ALU.mult))
            dve.wait_ge(acc_zeroed5, 1)
            dve.wait_ge(weight_landed, 16)

            def direction(i):
                return vec_s[:, bass.ds(i * T, T)]

            def add(k, b, i, first):
                dve.wait_ge(win_mm5, i + 1)
                for t in range(T):
                    base = dve.value_load(first_i[0:1, bass.ds(i * T + t, 1)], min_val=0, max_val=ACC - P)
                    if not first or t:
                        dve.wait_ge(win_added5, T * i + t)
                    dve.tensor_tensor(acc[:, bass.ds(base, P)], acc[:, bass.ds(base, P)],
                                      p_win[t // 4][0:F, (t % 4) * P:(t % 4 + 1) * P], ALU.add).then_inc(win_added5, 1)

            def layer_a(k, b, i, lo):
                r = b % 2
                dve.wait_ge(split_done, 3 * (i + 1))
                dve.tensor_tensor(vr[:], v1[:, r], direction(i).unsqueeze(3).to_broadcast([P, T, 3, 16]), ALU.mult
                                  ).then_inc(vr_done, 1)
                dve.wait_ge(vr_done, i + 1)
                dve.tensor_reduce(vdot[:, r], vr[:].rearrange("p t k u -> p t u k"), AX_X, ALU.add).then_inc(vdot_done, 1)
                dve.wait_ge(vdot_done, i + 1)
                if lo is None or lo >= 2:
                    dve.wait_ge(suma_mm, i - 1)
                for t in range(T):
                    pw = p_wa[t % 2]
                    o = prod[:, r, t].rearrange("p u o -> p o u")
                    dve.wait_ge(wa_mm, i * T + t + 1)
                    dve.tensor_tensor(o[:, 0:16], pw[:, 0:256].rearrange("p (o u) -> p o u", u=16),
                                      s1[:, r, t].unsqueeze(1).to_broadcast([P, 16, 16]), ALU.mult)
                    dve.tensor_tensor(o[:, 16:24], pw[:, 256:384].rearrange("p (o u) -> p o u", u=16),
                                      vdot[:, r, t].unsqueeze(1).to_broadcast([P, 8, 16]), ALU.mult)
                    dve.tensor_tensor(o[:, 24:48].rearrange("p (k o) u -> p k o u", k=3),
                                      pw[:, 384:512].rearrange("p (o u) -> p o u", u=16).unsqueeze(1).to_broadcast([P, 3, 8, 16]),
                                      v1[:, r, t].unsqueeze(2).to_broadcast([P, 3, 8, 16]), ALU.mult).then_inc(wa_used, 1)

            def layer_b(k, b, i, lo):
                r = b % 2
                dve.wait_ge(suma_copied, i + 1)
                sa = suma[:, r]
                dve.tensor_tensor(in_b[:, :, 0:8], sa[:, :, 0:8], sa[:, :, 16:24], ALU.add).then_inc(mid_done, 1)
                dve.tensor_tensor(vt_r[:], sa[:, :, 8:16].unsqueeze(2).to_broadcast([P, T, 3, 8]),
                                  direction(i).unsqueeze(3).to_broadcast([P, T, 3, 8]), ALU.mult).then_inc(mid_done, 1)
                dve.wait_ge(mid_done, 5 * i + 2)
                dve.tensor_tensor(vt[:].rearrange("p t k o -> p t (k o)"), vt_r[:].rearrange("p t k o -> p t (k o)"),
                                  sa[:, :, 24:48], ALU.add).then_inc(mid_done, 1)
                dve.wait_ge(mid_done, 5 * i + 3)
                dve.tensor_tensor(vt_r[:], vt[:], direction(i).unsqueeze(3).to_broadcast([P, T, 3, 8]), ALU.mult
                                  ).then_inc(mid_done, 1)
                dve.wait_ge(mid_done, 5 * i + 4)
                dve.tensor_reduce(in_b[:, :, 8:16], vt_r[:].rearrange("p t k o -> p t o k"), AX_X, ALU.add
                                  ).then_inc(mid_done, 1)
                dve.wait_ge(mid_done, 5 * i + 5)

                def multiply(t):
                    pw, q = p_wb[t % 2], prodb[:, t % 4]
                    if lo is None or lo > 1 or t >= 4:
                        dve.wait_ge(sumb_done, 2 * (i * T + t - 3))
                    dve.wait_ge(wb_mm, i * T + t + 1)
                    dve.tensor_tensor(q[:, 0:256].rearrange("p (o u) -> p o u", u=16),
                                      pw[:, 0:256].rearrange("p (o u) -> p o u", u=16),
                                      in_b[:, t].unsqueeze(1).to_broadcast([P, 16, 16]), ALU.mult).then_inc(prodb_done, 1)
                    dve.tensor_tensor(q[:, 256:320].rearrange("p (o u) -> p o u", u=8),
                                      pw[:, 256:320].rearrange("p (o u) -> p o u", u=8),
                                      in_b[:, t, 0:8].unsqueeze(1).to_broadcast([P, 8, 8]), ALU.mult).then_inc(prodb_done, 1)
                    dve.tensor_tensor(q[:, 320:512].rearrange("p (k o u) -> p k o u", k=3, u=8),
                                      pw[:, 320:384].rearrange("p (o u) -> p o u", u=8).unsqueeze(1).to_broadcast([P, 3, 8, 8]),
                                      vt[:, t].unsqueeze(2).to_broadcast([P, 3, 8, 8]), ALU.mult).then_inc(wb_used, 1)

                def reduce(t):
                    dve.wait_ge(prodb_done, i * 2 * T + 2 * t + 2)
                    dve.wait_ge(wb_used, i * T + t + 1)
                    dve.tensor_reduce(gs[:, r, t], prodb[:, t % 4, 0:256].rearrange("p (o u) -> p o u", u=16), AX_X,
                                      ALU.add).then_inc(sumb_done, 1)
                    dve.tensor_reduce(cv[:, r, t], prodb[:, t % 4, 256:512].rearrange("p (o u) -> p o u", u=8), AX_X,
                                      ALU.add).then_inc(sumb_done, 1)

                multiply(0)
                for t in range(1, T):
                    multiply(t)
                    reduce(t - 1)
                reduce(T - 1)

            def message(k, b, i, lo):
                r = b % 2
                dve.wait_ge(sumb_done, (i + 1) * 2 * T)
                dve.tensor_tensor(msg[:], cv[:, r, :, 0:8].unsqueeze(2).to_broadcast([P, T, 3, 8]),
                                  direction(i).unsqueeze(3).to_broadcast([P, T, 3, 8]), ALU.mult).then_inc(msg_done, 1)
                dve.wait_ge(msg_done, 4 * i + 1)
                dve.tensor_tensor(msg[:].rearrange("p t k o -> p t (k o)"), msg[:].rearrange("p t k o -> p t (k o)"),
                                  cv[:, r, :, 8:32], ALU.add).then_inc(msg_done, 1)
                dve.wait_ge(th_done, i + 1)
                dve.tensor_tensor(gs[:, r], th[:, r],
                                  weight_s[:, bass.ds(i * T, T)].unsqueeze(2).to_broadcast([P, T, 16]), ALU.mult
                                  ).then_inc(msg_done, 1)
                dve.wait_ge(msg_done, 4 * i + 3)
                if lo is None or lo >= 3:
                    dve.wait_ge(win_mm5, i - 1)
                dve.tensor_copy(z[:, r, :, 0:8], gs[:, r, :, 0:8]).then_inc(msg_done, 1)
                dve.wait_ge(msg_done, 4 * i + 4)
                dve.tensor_tensor(z[:, r, :, 8:F].rearrange("p t (o k) -> p t k o", k=3), msg[:],
                                  gs[:, r, :, 8:16].unsqueeze(2).to_broadcast([P, T, 3, 8]), ALU.mult).then_inc(z_done, 1)

            def body(k, b, lo):
                i = k * RING + b
                if has(lo, 0):
                    layer_a(k, b, i, lo)
                if has(lo, 1):
                    layer_b(k, b - 1, i - 1, lo)
                    message(k, b - 1, i - 1, lo)
                if has(lo, 2):
                    add(k, b - 2, i - 2, lo == 2)
            run(dve, body)
            dve.wait_ge(win_added5, T * NB)


def kernel(x, src, dst, edge_attr_10, edge_attr_3, edge_weight, L0_gnn_W, L0_gnn_att_src, L0_gnn_att_dst, L0_gnn_bias,
           L1_gnn_fc1_w1, L1_gnn_fc1_w2, L1_gnn_fc2_w1, L1_gnn_fc2_w2):
    import concourse.bacc as bacc
    from concourse.bass_utils import run_bass_kernel_spmd

    n, e = x.shape[0], src.shape[0]
    NN = -(-(n + 1) // (P * NG)) * NG
    NT = -(-e // (P * P)) * P
    x, src, dst = np.asarray(x), np.asarray(src), np.asarray(dst)
    e10, e3, ew = np.asarray(edge_attr_10), np.asarray(edge_attr_3), np.asarray(edge_weight)
    E = NT * P

    x_pad = np.zeros((NN * P, F), x.dtype)
    x_pad[:n] = x
    src_pad = np.full(E, n, src.dtype)
    src_pad[:e] = src
    dst_ext = np.full(E + P + 1, n + 1, dst.dtype)
    dst_ext[0] = -1
    dst_ext[1:e + 1] = dst
    dst_ext[e + 1:E + 1] = n
    emb = np.zeros((EMB, E), e10.dtype)
    emb[:, :e] = e10.T
    vec = np.ones((E, 3), e3.dtype)
    vec[:e] = e3
    wgt = np.zeros(E, ew.dtype)
    wgt[:e] = ew

    def by_tile(a):
        return np.ascontiguousarray(np.moveaxis(a.reshape((NT, P) + a.shape[1:]), 0, 1))

    def columns(w, first, u):
        return np.asarray(w)[:, first:first + u * 8].reshape(H, u, 8).transpose(0, 2, 1).reshape(H, u * 8)

    f1, f2 = L1_gnn_fc1_w2, L1_gnn_fc2_w2
    w2 = [columns(f1, first, 16) for first in (0, 256, 128, 384)]
    for ss, vv in ((0, 64), (128, 192)):
        both = np.concatenate([columns(f2, ss, 8).reshape(H, 8, 8), columns(f2, vv, 8).reshape(H, 8, 8)], axis=2)
        w2.append(both.reshape(H, 128))
    w2 += [columns(f2, 256, 8), columns(f2, 320, 8)]
    parts = np.repeat(np.array([[-float(a > 0), -float(a > 1), -float(b > 0), -float(b > 1)]
                                for a, b in zip(HID_PART, W_PART)], np.float32), H, axis=0)

    arrays = {
        "xT": np.ascontiguousarray(x_pad.T), "xN": x_pad,
        "w": np.asarray(L0_gnn_W), "wT": np.ascontiguousarray(np.asarray(L0_gnn_W).T),
        "att": np.stack([np.asarray(L0_gnn_att_src), np.asarray(L0_gnn_att_dst)], axis=1),
        "bias": np.asarray(L0_gnn_bias),
        "idx": by_tile(np.stack([src_pad, dst_ext[1:E + 1]], axis=1)).reshape(P, NT * 2),
        "dst_ext": dst_ext, "src_flat": src_pad,
        "emb": emb, "vec": by_tile(vec).reshape(P, NT * 3), "weight": by_tile(wgt),
        "fc1": np.concatenate([np.tile(np.asarray(L1_gnn_fc1_w1), (1, 6)), np.tile(np.asarray(L1_gnn_fc2_w1), (1, 6))],
                              axis=1),
        "w2": np.tile(np.concatenate(w2, axis=1), (6, 1)), "parts": parts,
    }
    nc = bacc.Bacc("TRN2", target_bir_lowering=False, num_devices=1)
    args = [nc.dram_tensor("in_" + name, a.shape, mybir.dt.from_np(a.dtype), kind="ExternalInput").ap()
            for name, a in arrays.items()]
    out = nc.dram_tensor("nodes_out", (NN * P, F), F32, kind="ExternalOutput").ap()
    gnn_kernel(nc, *args, out, NN, NT)
    r = run_bass_kernel_spmd(nc, [{"in_" + name: a for name, a in arrays.items()}], core_ids=[0])
    return r.results[0]["nodes_out"][:n]
```

```python
from contextlib import ExitStack

import numpy as np

import concourse.bass as bass
from concourse import mybir

F32 = mybir.dt.float32
BF16 = mybir.dt.bfloat16
I32 = mybir.dt.int32
ALU = mybir.AluOpType
ACT = mybir.ActivationFunctionType
AX_X = mybir.AxisListType.X

P = 128
T = 8
RING = 4
F = 32
H = 16
EMB = 10
R0 = F + 2
BIG = 1.0e30
EPS = 1.0e-5
SLOPE = 0.2
K6 = 6 * H
HID_PART = (0, 0, 1, 0, 1, 2)
W_PART = (0, 1, 0, 2, 1, 0)
NG = 14


def gnn_kernel(nc, xT, xN, w, wT, att, bias, idx, dst_ext, src_flat, emb, vec, weight,
               fc1, w2, parts, out, NN, NT):
    NB = NT // T
    NC = NT // P
    ACC = (NN + 1) * P
    assert NB % RING == 0 and NT % P == 0

    table = nc.dram_tensor("table0", (NN * P, R0), F32).ap()
    table1 = nc.dram_tensor("table1", (NN * P, F), F32).ap()
    spill = nc.dram_tensor("spill", (P, NT * R0), F32).ap()
    hid_d = nc.dram_tensor("hid_d", (K6, NT * P * 2), BF16).ap()
    parts_d = nc.dram_tensor("parts_d", ((NN + 1) * P, 3 * F), BF16).ap()
    local_d = nc.dram_tensor("local_d", (NT * P,), F32).ap()
    ends_d = nc.dram_tensor("ends_d", (4, NT), F32).ap()
    carry_d = nc.dram_tensor("carry_d", (4, NT), F32).ap()

    outer = ExitStack()
    with outer:
        outer.enter_context(nc.allow_non_contiguous_dma(reason="one element of each edge tile, once"))

        def maker(stack):
            def sb(name, shape, dt=F32):
                return stack.enter_context(nc.sbuf_tensor(name, shape, dt))

            def ps(name, shape=(P, 512)):
                return stack.enter_context(nc.psum_tensor(name, list(shape), F32))

            def sem(name):
                return outer.enter_context(nc.semaphore(name))
            return sb, ps, sem

        sb, _, sem = maker(outer)

        iota_n = sb("iota_n", [P, P])
        ident = sb("ident", [P, P])
        first_i = sb("first_i", [1, NT], I32)
        local = sb("local", [P, NT])
        parts_s = sb("parts_s", [K6, 4])
        minus_p = sb("minus_p", [P, 1])
        bias_b = sb("bias_b", [P, F])
        layer0 = ExitStack()
        idx_all = layer0.enter_context(nc.sbuf_tensor("idx_all", [P, NT, 2], I32))
        nodes0 = layer0.enter_context(nc.sbuf_tensor("nodes0", [P, NN, R0], F32))

        asd = layer0.enter_context(nc.sbuf_tensor("asd", [P, 2, NT], F32))
        with ExitStack() as st:
            sb, ps, sem = maker(st)
            xT_s = sb("xT_s", [F, NN * P])
            w_s = sb("w_s", [F, R0])
            wT_s = sb("wT_s", [F, F])
            att_s = sb("att_s", [F, 2])
            iota_i = sb("iota_i", [P, P], I32)
            part_i = sb("part_i", [P, 1], I32)
            part_f = sb("part_f", [P, 1])
            idx_b = sb("idx_b", [P, RING, T], I32)
            rows = sb("rows", [P, RING, T, R0])
            fc1_s = sb("fc1_s", [EMB, 2, K6])
            emb_s = sb("emb_s", [EMB, RING, T * P])
            hid = sb("hid", [K6, 2, 2, T * P])
            top = sb("top", [K6, 2, 2, T * P], BF16)
            part = sb("part", [K6, 2, 2, T * P], BF16)
            p_hid = [[ps(f"p_hid{n}{h}") for h in range(2)] for n in range(2)]
            p_att = ps("p_att")
            p_tab = [ps("p_tab0"), ps("p_tab1")]

            w_landed, xT_landed, idx_landed, first_landed = sem("w_landed"), sem("xT_landed"), sem("idx_landed"), sem("first_landed")
            iota_made, part_cast, consts_made = sem("iota_made"), sem("part_cast"), sem("consts_made")
            att_mm, att_copied, tab_mm, tab_copied, tab_stored = sem("att_mm"), sem("att_copied"), sem("tab_mm"), sem("tab_copied"), sem("tab_stored")
            idx_copied, rows_split = sem("idx_copied"), sem("rows_split")
            rows_landed = [sem(f"rows_landed{b}") for b in range(RING)]
            rows_spilled = [sem(f"rows_spilled{b}") for b in range(RING)]
            emb_landed = [sem(f"emb_landed{b}") for b in range(RING)]
            part_stored = [sem(f"part_stored{b}") for b in range(2)]
            hid_mm, hid_done, top_done, less_done, mid_done, part_done = (
                sem("hid_mm"), sem("hid_done"), sem("top_done"), sem("less_done"), sem("middle_done"), sem("part_done"))
            groups = NN // NG

            block = st.enter_context(nc.Block())

            @block.sync
            def _(sp):
                sp.dma_start(w_s[:, 0:F], w).then_inc(w_landed, 16)
                sp.dma_start(wT_s[:], wT).then_inc(w_landed, 16)
                sp.dma_start(att_s[:], att).then_inc(w_landed, 16)
                sp.dma_start(xT_s[:], xT).then_inc(xT_landed, 16)
                sp.dma_start(fc1_s[:].rearrange("p n h -> p (n h)"), fc1).then_inc(w_landed, 16)
                sp.dma_start(parts_s[:], parts).then_inc(w_landed, 16)
                sp.dma_start(idx_all[:].rearrange("p t two -> p (t two)"), idx).then_inc(idx_landed, 16)
                sp.dma_start(bias_b[:], bias.partition_broadcast(P)).then_inc(first_landed, 16)
                sp.dma_start(first_i[:], dst_ext[1:1 + NT * P].rearrange("(o t e) -> o t e", o=1, e=P)[:, :, 0]).then_inc(first_landed, 16)
                sp.wait_ge(tab_copied, groups)
                sp.dma_start(table.rearrange("(n p) f -> p n f", p=P), nodes0[:]).then_inc(tab_stored, 16)

                def load_emb(k, b, later):
                    i = k * RING + b
                    if later:
                        sp.wait_ge(hid_mm, 4 * (i - RING + 1))
                    sp.dma_start(emb_s[:, b], emb[:, bass.ds(i * (T * P), T * P)]).then_inc(emb_landed[b], 16)

                def spill_block(k, b):
                    i = k * RING + b
                    sp.wait_ge(part_done, i + 1)
                    sp.dma_start(hid_d[:, bass.ds(i * (2 * T * P), 2 * T * P)],
                                 part[:, b % 2].rearrange("p n e -> p (n e)")).then_inc(part_stored[b % 2], 16)
                    sp.wait_ge(rows_landed[b], (k + 1) * 16 * T)
                    sp.dma_start(spill[:, bass.ds(i * (T * R0), T * R0)],
                                 rows[:, b].rearrange("p t f -> p (t f)")).then_inc(rows_spilled[b], 16)
                for b in range(RING):
                    load_emb(0, b, False)
                spill_block(0, 0)
                with sp.Fori(1, NB // RING) as k:
                    for b in range(RING):
                        load_emb(k, b, True)
                        if b < RING - 1:
                            spill_block(k - 1, b + 1)
                        else:
                            spill_block(k, 0)
                for b in range(1, RING):
                    spill_block(NB // RING - 1, b)
                sp.wait_ge(first_landed, 32)
                for b in range(2):
                    sp.wait_ge(part_stored[b], 16 * (NB // 2))
                for b in range(RING):
                    sp.wait_ge(rows_spilled[b], 16 * (NB // RING))

            @block.gpsimd
            def _(pool):
                pool.iota(iota_i[:], pattern=[[1, P]], base=0, channel_multiplier=0).then_inc(iota_made, 1)
                pool.iota(part_i[:], pattern=[[0, 1]], base=0, channel_multiplier=1).then_inc(iota_made, 1)
                pool.wait_ge(idx_landed, 16)
                pool.wait_ge(tab_stored, 16)

                def gather_block(k, b, later):
                    i = k * RING + b
                    if later:
                        pool.wait_ge(rows_spilled[b], k * 16)
                        pool.wait_ge(rows_split, i - RING + 1)
                    pool.tensor_copy(idx_b[:, b], idx_all[:, bass.ds(i * T, T), 0]).then_inc(idx_copied, 1)
                    pool.wait_ge(idx_copied, i + 1)
                    pool.nop(nofuse=True)
                    for t in range(T):
                        pool.indirect_dma_start(rows[:, b, t], None, table,
                                                bass.IndirectOffsetOnAxis(ap=idx_b[:, b, t:t + 1], axis=0)
                                                ).then_inc(rows_landed[b], 16)
                for b in range(RING):
                    gather_block(0, b, False)
                with pool.Fori(1, NB // RING) as k:
                    for b in range(RING):
                        gather_block(k, b, True)

            @block.tensor
            def _(pe):
                pe.wait_ge(w_landed, 80)
                pe.matmul(p_att[0:F, 0:2], wT_s[:], att_s[:], start=True, stop=True).then_inc(att_mm, 1)
                pe.wait_ge(att_copied, 1)
                pe.wait_ge(xT_landed, 16)
                for g in range(groups):
                    if g >= 2:
                        pe.wait_ge(tab_copied, g - 1)
                    for j in range(NG):
                        n = g * NG + j
                        mm = pe.matmul(p_tab[g % 2][:, j * R0:(j + 1) * R0], xT_s[:, n * P:(n + 1) * P], w_s[:],
                                       start=True, stop=True)
                    mm.then_inc(tab_mm, 1)

                def hidden(k, b, later):
                    i = k * RING + b
                    pe.wait_ge(emb_landed[b], (k + 1) * 16)
                    for n in range(2):
                        for h in range(2):
                            if later or b:
                                pe.wait_ge(hid_done, 4 * (i - 1) + 2 * n + h + 1)
                            pe.matmul(p_hid[n][h][0:K6, :], fc1_s[:, n], emb_s[:, b, h * 512:(h + 1) * 512],
                                      start=True, stop=True).then_inc(hid_mm, 1)
                for b in range(RING):
                    hidden(0, b, False)
                with pe.Fori(1, NB // RING) as k:
                    for b in range(RING):
                        hidden(k, b, True)

            @block.scalar
            def _(act):
                def hidden(k, b, later):
                    i = k * RING + b
                    r = b % 2
                    if later or b >= 2:
                        act.wait_ge(part_done, i - 1)
                    for n in range(2):
                        for h in range(2):
                            act.wait_ge(hid_mm, 4 * i + 2 * n + h + 1)
                            act.activation(hid[:, r, n, h * 512:(h + 1) * 512], p_hid[n][h][0:K6, :], ACT.Relu,
                                           scale=float(1.0 / np.sqrt(EMB))).then_inc(hid_done, 1)
                    act.wait_ge(hid_done, 4 * (i + 1))
                    act.activation(top[:, r], hid[:, r], ACT.Copy).then_inc(top_done, 1)

                def middle(k, b, i):
                    act.wait_ge(less_done, i + 1)
                    act.activation(top[:, b % 2], hid[:, b % 2], ACT.Copy).then_inc(mid_done, 1)
                hidden(0, 0, False)
                for b in range(1, RING):
                    hidden(0, b, False)
                    middle(0, b - 1, b - 1)
                with act.Fori(1, NB // RING) as k:
                    for b in range(RING):
                        hidden(k, b, True)
                        middle(k, b - 1, k * RING + b - 1)
                middle(0, RING - 1, NB - 1)

            @block.vector
            def _(dve):
                dve.wait_ge(iota_made, 2)
                dve.tensor_copy(part_f[:], part_i[:]).then_inc(part_cast, 1)
                dve.tensor_copy(iota_n[:], iota_i[:]).then_inc(part_cast, 1)
                dve.wait_ge(part_cast, 2)
                dve.tensor_scalar(minus_p[:], part_f[:], -1.0, None, ALU.mult).then_inc(consts_made, 1)
                dve.tensor_scalar(ident[:], iota_n[:], part_f[:, 0:1], None, ALU.is_equal).then_inc(consts_made, 1)
                dve.wait_ge(att_mm, 1)
                dve.tensor_copy(w_s[:, F:R0], p_att[0:F, 0:2]).then_inc(att_copied, 1)
                for g in range(groups):
                    dve.wait_ge(tab_mm, g + 1)
                    dve.tensor_copy(nodes0[:, g * NG:(g + 1) * NG, :].rearrange("p n f -> p (n f)"),
                                    p_tab[g % 2][:, 0:NG * R0]).then_inc(tab_copied, 1)

                def split_block(k, b):
                    i = k * RING + b
                    dve.wait_ge(rows_landed[b], (k + 1) * 16 * T)
                    dve.tensor_copy(asd[:, :, bass.ds(i * T, T)],
                                    rows[:, b, :, F:R0].rearrange("p t two -> p two t")).then_inc(rows_split, 1)

                def less(k, b, i):
                    r = b % 2
                    dve.wait_ge(top_done, i + 1)
                    dve.scalar_tensor_tensor(out=hid[:, r], in0=top[:, r], scalar=parts_s[:, 0:1], in1=hid[:, r],
                                             op0=ALU.mult, op1=ALU.add).then_inc(less_done, 1)

                def lowest(k, b, i, first):
                    r = b % 2
                    dve.wait_ge(mid_done, i + 1)
                    if not first:
                        dve.wait_ge(part_stored[r], stored(k, b))
                    dve.scalar_tensor_tensor(out=part[:, r], in0=top[:, r], scalar=parts_s[:, 1:2], in1=hid[:, r],
                                             op0=ALU.mult, op1=ALU.add).then_inc(part_done, 1)

                def stored(k, b):
                    return 32 * k + 16 * (b // 2)

                for b in range(RING):
                    less(0, b, b)
                    if b:
                        lowest(0, b - 1, b - 1, b - 1 < 2)
                    split_block(0, b)
                with dve.Fori(1, NB // RING) as k:
                    for b in range(RING):
                        less(k, b, k * RING + b)
                        if b:
                            lowest(k, b - 1, k * RING + b - 1, False)
                        else:
                            lowest(k - 1, RING - 1, k * RING - 1, False)
                        split_block(k, b)
                lowest(NB // RING - 1, RING - 1, NB - 1, False)
                dve.wait_ge(rows_split, NB)

        ex_e = asd
        with ExitStack() as st:
            sb, ps, sem = maker(st)
            BEFORE, AFTER, SRC, SELF, LAST, CUR = range(6)
            big = sb("big", [P, 6, NC * P])
            big_i = big[:].bitcast(I32)
            aT = sb("aT", [P, 2, NC * P])
            pen = sb("pen", [P, 2, NC * P])
            scan = sb("scan", [P, 4, NC * P])
            ends = sb("ends", [P, 4, NC])
            carry = sb("carry", [P, 4, NC])
            row_i = sb("row_i", [1, 4, NT], I32)
            row_pen = sb("row_pen", [1, 4, NT])
            row_in = big[0:1, 0:4, :]
            row_out = row_i[:].bitcast(F32)
            ones = sb("ones", [1, P])
            p_t = [ps(f"p_t{j}") for j in range(4)]

            dst_loaded, row_loaded, a_mm, a_copied, d = (
                sem("dst_loaded"), sem("row_loaded"), sem("a_mm"), sem("a_copied"), sem("d"))
            base_row, base_mm, ends_made, ends_out, rows_in, carry_made, carry_out, carry_in = (
                sem("base_row"), sem("base_mm"), sem("ends_made"), sem("ends_out"), sem("rows_in"),
                sem("carry_made"), sem("carry_out"), sem("carry_in"))
            exponent_made, exp_done, max_made, ex_mm, ex_copied = (
                sem("exponent_made"), sem("exp_done"), sem("max_made"), sem("ex_mm"), sem("ex_copied"))
            local_made, local_stored = sem("local_made"), sem("local_stored")
            quarters = -(-NT // 512)

            block = st.enter_context(nc.Block())

            @block.sync
            def _(sp):
                for j, at in ((BEFORE, 0), (CUR, 1), (AFTER, 2)):
                    sp.dma_start(big_i[:, j].rearrange("p (c e) -> p c e", e=P),
                                 dst_ext[at:at + NT * P].rearrange("(c p e) -> p c e", p=P, e=P)).then_inc(dst_loaded, 16)
                sp.dma_start(big_i[:, SRC].rearrange("p (c e) -> p c e", e=P),
                             src_flat.rearrange("(c p e) -> p c e", p=P, e=P)).then_inc(dst_loaded, 16)
                for j, at in enumerate((0, 1, P, P + 1)):
                    sp.dma_start(row_i[:, j], dst_ext[at:at + NT * P].rearrange("(o t e) -> o t e", o=1, e=P)[:, :, 0]
                                 ).then_inc(row_loaded, 16)
                sp.wait_ge(local_made, 1)
                sp.dma_start(local_d.rearrange("(c p e) -> p c e", p=P, e=P), big[:, BEFORE].rearrange("p (c e) -> p c e", e=P)
                             ).then_inc(local_stored, 16)
                sp.wait_ge(ends_made, 1)
                for j in range(4):
                    sp.dma_start(ends_d[j].rearrange("(c p) -> p c", p=P), ends[:, j]).then_inc(ends_out, 16)
                sp.wait_ge(ends_out, 64)
                sp.wait_ge(local_stored, 16)
                sp.dma_start(row_in, ends_d.rearrange("(o j) t -> o j t", o=1)).then_inc(rows_in, 16)
                sp.wait_ge(carry_made, 1)
                sp.dma_start(carry_d.rearrange("(o j) t -> o j t", o=1), row_out).then_inc(carry_out, 16)
                sp.wait_ge(carry_out, 16)
                for j in range(4):
                    sp.dma_start(carry[:, j], carry_d[j].rearrange("(c p) -> p c", p=P)).then_inc(carry_in, 16)
                sp.wait_ge(carry_in, 64)

            @block.tensor
            def _(pe):
                for m in range(2 * NC):
                    if m >= 4:
                        pe.wait_ge(a_copied, m - 3)
                    pe.transpose(p_t[m % 4][:, 0:P], asd[:, m // NC, m % NC * P:(m % NC + 1) * P], ident[:]).then_inc(a_mm, 1)
                pe.wait_ge(base_row, 1)
                for q in range(quarters):
                    wq = min(512, NT - q * 512)
                    pe.wait_ge(a_copied, 2 * NC + q)
                    pe.matmul(p_t[0][:, 0:wq], ones[:], row_pen[:, 0, q * 512:q * 512 + wq], start=True, stop=True
                              ).then_inc(base_mm, 1)
                pe.wait_ge(a_copied, 2 * NC + quarters)
                pe.wait_ge(exp_done, 1)
                pe.wait_ge(max_made, 1)
                for m in range(2 * NC):
                    if m >= 4:
                        pe.wait_ge(ex_copied, m - 3)
                    pe.transpose(p_t[m % 4][:, 0:P], aT[:, m // NC, m % NC * P:(m % NC + 1) * P], ident[:]).then_inc(ex_mm, 1)

            @block.scalar
            def _(act):
                act.wait_ge(exponent_made, 1)
                act.activation(aT[:, 0], big[:, AFTER], ACT.Exp).then_inc(exp_done, 1)

            @block.vector
            def _(dve):
                done = [0]

                def then(ins):
                    done[0] += 1
                    ins.then_inc(d, 1)
                    dve.wait_ge(d, done[0])

                def chunks(ap):
                    return ap.rearrange("p (c e) -> p c e", e=P)

                for m in range(2 * NC):
                    dve.wait_ge(a_mm, m + 1)
                    dve.tensor_copy(aT[:, m // NC, m % NC * P:(m % NC + 1) * P], p_t[m % 4][:, 0:P]).then_inc(a_copied, 1)
                then(dve.memset(ones[:], 1.0))
                dve.wait_ge(row_loaded, 64)
                then(dve.tensor_copy(row_pen[:, 0], row_i[:, 1]))
                dve.sem_inc(base_row, 1)
                then(dve.tensor_copy(local[:], idx_all[:, :, 1]))
                for q in range(quarters):
                    wq = min(512, NT - q * 512)
                    dve.wait_ge(base_mm, q + 1)
                    dve.tensor_tensor(local[:, q * 512:q * 512 + wq], local[:, q * 512:q * 512 + wq],
                                      p_t[0][:, 0:wq], ALU.subtract).then_inc(a_copied, 1)
                dve.wait_ge(a_copied, 2 * NC + quarters)
                dve.wait_ge(dst_loaded, 64)
                then(dve.tensor_tensor(big[:, LAST], big_i[:, CUR], big_i[:, AFTER], ALU.not_equal))
                then(dve.tensor_tensor(pen[:, 0], big_i[:, CUR], big_i[:, BEFORE], ALU.not_equal))
                then(dve.tensor_scalar(pen[:, 0], pen[:, 0], -BIG, None, ALU.mult))
                then(dve.tensor_scalar(pen[:, 1], big[:, LAST], -BIG, None, ALU.mult))
                cur3 = chunks(big_i[:, CUR])
                then(dve.tensor_tensor(chunks(big[:, BEFORE]), cur3, cur3[:, :, 0:1].to_broadcast([P, NC, P]),
                                       ALU.subtract))
                dve.sem_inc(local_made, 1)
                then(dve.memset(chunks(pen[:, 0])[:, :, 0], -BIG))
                then(dve.memset(chunks(pen[:, 1])[:, :, P - 1], -BIG))
                then(dve.tensor_tensor(big[:, SELF], big_i[:, SRC], big_i[:, CUR], ALU.is_equal))
                then(dve.tensor_scalar(big[:, AFTER], big[:, SELF], BIG, -BIG, ALU.mult, ALU.add))
                then(dve.tensor_tensor(big[:, SELF], big[:, SELF], aT[:, 1], ALU.mult))
                then(dve.tensor_tensor(big[:, SELF], big[:, SELF], big[:, AFTER], ALU.add))
                for j, a in ((0, aT[:, 0]), (1, big[:, SELF])):
                    then(dve.tensor_tensor_scan(scan[:, j], pen[:, 0], a, -BIG, ALU.add, ALU.max))
                    then(dve.tensor_tensor_scan(scan[:, 2 + j, ::-1], pen[:, 1, ::-1], a[:, ::-1], -BIG, ALU.add, ALU.max))
                then(dve.tensor_copy(ends[:, 0:2], scan[:, 0:2].rearrange("p j (c e) -> p j c e", e=P)[:, :, :, P - 1]))
                then(dve.tensor_copy(ends[:, 2:4], scan[:, 2:4].rearrange("p j (c e) -> p j c e", e=P)[:, :, :, 0]))
                dve.sem_inc(ends_made, 1)
                last_before, first, last, first_after = (row_i[:, j] for j in range(4))
                for j, (one, other) in enumerate(((last, last_before), (first, first_after),
                                                  (first, last_before), (last, first_after))):
                    then(dve.tensor_tensor(row_pen[:, j], one, other, ALU.not_equal))
                then(dve.tensor_scalar(row_pen[:], row_pen[:], -BIG, None, ALU.mult))
                then(dve.memset(row_out, -BIG))
                dve.wait_ge(rows_in, 16)
                for j in range(2):
                    then(dve.tensor_tensor_scan(row_in[:, j], row_pen[:, 0], row_in[:, j], -BIG, ALU.add, ALU.max))
                    then(dve.tensor_tensor_scan(row_in[:, 2 + j, ::-1], row_pen[:, 1, ::-1],
                                                row_in[:, 2 + j, ::-1], -BIG, ALU.add, ALU.max))
                    then(dve.tensor_tensor(row_out[:, j, 1:NT], row_in[:, j, 0:NT - 1], row_pen[:, 2, 1:NT], ALU.add))
                    then(dve.tensor_tensor(row_out[:, 2 + j, 0:NT - 1], row_in[:, 2 + j, 1:NT], row_pen[:, 3, 0:NT - 1],
                                           ALU.add))
                dve.sem_inc(carry_made, 1)
                for j, at in ((0, 0), (1, P - 1)):
                    then(dve.tensor_tensor(chunks(pen[:, j]), cur3, cur3[:, :, at:at + 1].to_broadcast([P, NC, P]),
                                           ALU.not_equal))
                then(dve.tensor_scalar(pen[:], pen[:], -BIG, None, ALU.mult))
                dve.wait_ge(carry_in, 64)
                for j in range(4):
                    then(dve.tensor_tensor(chunks(big[:, BEFORE]), chunks(pen[:, j // 2]),
                                           carry[:, j].unsqueeze(2).to_broadcast([P, NC, P]), ALU.add))
                    then(dve.tensor_tensor(scan[:, j], scan[:, j], big[:, BEFORE], ALU.max))
                then(dve.tensor_tensor(scan[:, 0:2], scan[:, 0:2], scan[:, 2:4], ALU.max))
                then(dve.tensor_tensor(pen[:, 0], scan[:, 0], scan[:, 1], ALU.add))
                then(dve.tensor_tensor(pen[:, 1], aT[:, 0], scan[:, 1], ALU.add))
                then(dve.scalar_tensor_tensor(out=pen[:], in0=pen[:], scalar=SLOPE, in1=pen[:], op0=ALU.mult, op1=ALU.max))
                then(dve.tensor_tensor(big[:, AFTER], pen[:, 1], pen[:, 0], ALU.subtract))
                dve.sem_inc(exponent_made, 1)
                then(dve.tensor_tensor(aT[:, 1], big[:, LAST], pen[:, 0], ALU.mult))
                dve.sem_inc(max_made, 1)
                for m in range(2 * NC):
                    dve.wait_ge(ex_mm, m + 1)
                    dve.tensor_copy(ex_e[:, m // NC, m % NC * P:(m % NC + 1) * P], p_t[m % 4][:, 0:P]).then_inc(ex_copied, 1)
                dve.wait_ge(ex_copied, 2 * NC)

        acc = layer0.enter_context(nc.sbuf_tensor("acc", [R0, ACC], F32))
        with ExitStack() as st:
            sb, ps, sem = maker(st)
            rows = sb("rows3", [P, RING, T, R0])
            z = sb("z3", [P, RING, T, R0])
            hot = sb("hot3", [P, RING, T, P])
            diff = sb("diff3", [P, RING, T, P])
            win = [[ps(f"win3_{a}{h}") for h in range(2)] for a in range(2)]
            acc_zeroed, z_made, hot_made, win_mm, win_added = (
                sem("acc_zeroed"), sem("z_made"), sem("hot_made"), sem("win_mm"), sem("win_added"))
            diff_made, abs_made = sem("diff_made"), sem("abs_made")
            back = [sem(f"back{b}") for b in range(RING)]

            block = st.enter_context(nc.Block())

            @block.sync
            def _(sp):
                def load_block(k, b, later):
                    i = k * RING + b
                    if later:
                        sp.wait_ge(z_made, 2 * (i - RING + 1))
                    sp.dma_start(rows[:, b].rearrange("p t f -> p (t f)"),
                                 spill[:, bass.ds(i * (T * R0), T * R0)]).then_inc(back[b], 16)
                for b in range(RING):
                    load_block(0, b, False)
                with sp.Fori(1, NB // RING) as k:
                    for b in range(RING):
                        load_block(k, b, True)

            @block.gpsimd
            def _(pool):
                def offsets(k, b, later):
                    i = k * RING + b
                    if later:
                        pool.wait_ge(hot_made, i - RING + 1)
                    pool.tensor_tensor(diff[:, b], iota_n[:].unsqueeze(1).to_broadcast([P, T, P]),
                                       local[:, bass.ds(i * T, T)].unsqueeze(2).to_broadcast([P, T, P]),
                                       ALU.subtract).then_inc(diff_made, 1)
                for b in range(RING):
                    offsets(0, b, False)
                with pool.Fori(1, NB // RING) as k:
                    for b in range(RING):
                        offsets(k, b, True)

            @block.scalar
            def _(act):
                def one_hot(k, b, later):
                    i = k * RING + b
                    act.wait_ge(diff_made, i + 1)
                    act.activation(diff[:, b], diff[:, b], ACT.Abs).then_inc(abs_made, 1)
                    if later:
                        act.wait_ge(win_mm, i - RING + 1)
                    act.wait_ge(abs_made, i + 1)
                    act.activation(hot[:, b], diff[:, b], ACT.Relu, scale=-1.0, bias=1.0).then_inc(hot_made, 1)
                for b in range(RING):
                    one_hot(0, b, False)
                with act.Fori(1, NB // RING) as k:
                    for b in range(RING):
                        one_hot(k, b, True)

            @block.tensor
            def _(pe):
                def windows(k, b, later):
                    i = k * RING + b
                    pe.wait_ge(z_made, 2 * (i + 1))
                    pe.wait_ge(hot_made, i + 1)
                    if later or b >= 2:
                        pe.wait_ge(win_added, T * (i - 1))
                    for t in range(T):
                        mm = pe.matmul(win[b % 2][t // 4][0:R0, (t % 4) * P:(t % 4 + 1) * P], z[:, b, t], hot[:, b, t],
                                       start=True, stop=True)
                    mm.then_inc(win_mm, 1)
                for b in range(RING):
                    windows(0, b, False)
                with pe.Fori(1, NB // RING) as k:
                    for b in range(RING):
                        windows(k, b, True)

            @block.vector
            def _(dve):
                dve.memset(acc[:], 0.0).then_inc(acc_zeroed, 1)
                dve.wait_ge(acc_zeroed, 1)

                def weigh(k, b, later):
                    i = k * RING + b
                    if later:
                        dve.wait_ge(win_mm, i - RING + 1)
                    dve.wait_ge(back[b], (k + 1) * 16)
                    dve.tensor_tensor(z[:, b, :, 0:F], rows[:, b, :, 0:F],
                                      ex_e[:, 0, bass.ds(i * T, T)].unsqueeze(2).to_broadcast([P, T, F]),
                                      ALU.mult).then_inc(z_made, 1)
                    dve.tensor_copy(z[:, b, :, F:R0].rearrange("p t two -> p two t"),
                                    ex_e[:, :, bass.ds(i * T, T)]).then_inc(z_made, 1)

                def add(k, b, first):
                    i = k * RING + b
                    dve.wait_ge(win_mm, i + 1)
                    for t in range(T):
                        base = dve.value_load(first_i[0:1, bass.ds(i * T + t, 1)], min_val=0, max_val=ACC - P)
                        if not first or t:
                            dve.wait_ge(win_added, T * i + t)
                        dve.tensor_tensor(acc[:, bass.ds(base, P)], acc[:, bass.ds(base, P)],
                                          win[b % 2][t // 4][0:R0, (t % 4) * P:(t % 4 + 1) * P], ALU.add
                                          ).then_inc(win_added, 1)
                weigh(0, 0, False)
                for b in range(RING - 1):
                    weigh(0, b + 1, False)
                    add(0, b, b == 0)
                with dve.Fori(1, NB // RING) as k:
                    weigh(k, 0, True)
                    add(k - 1, RING - 1, False)
                    for b in range(RING - 1):
                        weigh(k, b + 1, True)
                        add(k, b, False)
                add(NB // RING - 1, RING - 1, False)
                dve.wait_ge(win_added, T * NB)

        def layernorm(then, dve, act_done, want_sqrt, y, stat, sq):
            mean, var = stat[:, 0], stat[:, 1]
            then(dve.tensor_reduce(mean, y, AX_X, ALU.add))
            then(dve.tensor_scalar(mean, mean, 1.0 / F, None, ALU.mult))
            then(dve.tensor_tensor(y, y, mean.unsqueeze(2).to_broadcast([P, NN, F]), ALU.subtract))
            then(dve.tensor_tensor(sq, y, y, ALU.mult))
            then(dve.tensor_reduce(var, sq, AX_X, ALU.add))
            then(dve.tensor_scalar(var, var, 1.0 / F, EPS, ALU.mult, ALU.add))
            dve.sem_inc(want_sqrt, 1)
            dve.wait_ge(act_done, 1)
            then(dve.reciprocal(var, mean))
            then(dve.tensor_tensor(y, y, var.unsqueeze(2).to_broadcast([P, NN, F]), ALU.mult))

        with ExitStack() as st:
            sb, ps, sem = maker(st)
            xn = sb("xn", [P, NN, F])
            sums = sb("sums", [P, NN, R0])
            sq = sb("sq", [P, NN, F])
            x1 = sb("x1", [P, NN, F])
            stat = sb("stat", [P, 4, NN])
            parts3 = sb("parts3", [P, NN, 3 * F], BF16)
            no_part = sb("no_part", [P, 3 * F], BF16)
            p_n = [ps("p_n0"), ps("p_n1")]
            x_landed, sums_mm, sums_copied, d4, self_ready, self_exp, want_sqrt, got_sqrt, x1_made, x1_stored = (
                sem("x_landed"), sem("sums_mm"), sem("sums_copied"), sem("d4"), sem("self_ready"), sem("self_exp"),
                sem("want_sqrt"), sem("got_sqrt"), sem("x1_made"), sem("x1_stored"))

            block = st.enter_context(nc.Block())

            @block.sync
            def _(sp):
                sp.dma_start(xn[:], xN.rearrange("(n p) f -> p n f", p=P)).then_inc(x_landed, 16)
                sp.wait_ge(x1_made, 1)
                sp.dma_start(table1.rearrange("(n p) f -> p n f", p=P), x1[:]).then_inc(x1_stored, 16)
                sp.dma_start(parts_d[0:NN * P].rearrange("(n p) f -> p n f", p=P), parts3[:]).then_inc(x1_stored, 16)
                sp.dma_start(parts_d[NN * P:(NN + 1) * P], no_part[:]).then_inc(x1_stored, 16)
                sp.wait_ge(x1_stored, 48)

            @block.tensor
            def _(pe):
                for g in range(NN // NG):
                    if g >= 2:
                        pe.wait_ge(sums_copied, g - 1)
                    for j in range(NG):
                        n = g * NG + j
                        mm = pe.transpose(p_n[g % 2][:, j * R0:(j + 1) * R0], acc[:, n * P:(n + 1) * P],
                                          ident[0:R0, 0:R0])
                    mm.then_inc(sums_mm, 1)

            @block.scalar
            def _(act):
                act.wait_ge(self_ready, 1)
                act.activation(stat[:, 1], stat[:, 0], ACT.Exp).then_inc(self_exp, 1)
                act.wait_ge(want_sqrt, 1)
                act.activation(stat[:, 0], stat[:, 1], ACT.Sqrt).then_inc(got_sqrt, 1)

            @block.vector
            def _(dve):
                done = [0]

                def then(ins):
                    done[0] += 1
                    ins.then_inc(d4, 1)
                    dve.wait_ge(d4, done[0])

                for g in range(NN // NG):
                    dve.wait_ge(sums_mm, g + 1)
                    dve.tensor_copy(sums[:, g * NG:(g + 1) * NG].rearrange("p n f -> p (n f)"),
                                    p_n[g % 2][:, 0:NG * R0]).then_inc(sums_copied, 1)
                dve.wait_ge(sums_copied, NN // NG)
                s0 = stat[:, 0]
                then(dve.tensor_tensor(s0, nodes0[:, :, F], nodes0[:, :, F + 1], ALU.add))
                then(dve.scalar_tensor_tensor(out=s0, in0=s0, scalar=SLOPE, in1=s0, op0=ALU.mult, op1=ALU.max))
                then(dve.tensor_tensor(s0, s0, sums[:, :, F + 1], ALU.subtract))
                dve.sem_inc(self_ready, 1)
                dve.wait_ge(self_exp, 1)
                s1 = stat[:, 1]
                then(dve.tensor_tensor(x1[:], nodes0[:, :, 0:F], s1.unsqueeze(2).to_broadcast([P, NN, F]), ALU.mult))
                then(dve.tensor_tensor(x1[:], x1[:], sums[:, :, 0:F], ALU.add))
                then(dve.tensor_tensor(stat[:, 2], sums[:, :, F], s1, ALU.add))
                then(dve.reciprocal(stat[:, 3], stat[:, 2]))
                then(dve.tensor_tensor(x1[:], x1[:], stat[:, 3].unsqueeze(2).to_broadcast([P, NN, F]), ALU.mult))
                then(dve.tensor_tensor(x1[:], x1[:], bias_b[:].unsqueeze(1).to_broadcast([P, NN, F]), ALU.add))
                dve.wait_ge(x_landed, 16)
                then(dve.tensor_tensor(x1[:], x1[:], xn[:], ALU.add))
                layernorm(then, dve, got_sqrt, want_sqrt, x1[:], stat, sq[:])
                then(dve.memset(no_part[:], 0.0))
                then(dve.tensor_copy(parts3[:, :, 0:F], x1[:]))
                then(dve.tensor_tensor(sq[:], x1[:], parts3[:, :, 0:F], ALU.subtract))
                then(dve.tensor_copy(parts3[:, :, F:2 * F], sq[:]))
                then(dve.tensor_tensor(sq[:], sq[:], parts3[:, :, F:2 * F], ALU.subtract))
                then(dve.tensor_copy(parts3[:, :, 2 * F:3 * F], sq[:]))
                dve.sem_inc(x1_made, 1)

        layer0.close()

        acc = outer.enter_context(nc.sbuf_tensor("acc1", [F, ACC], F32))
        edge_layer(nc, maker, NB, NT, ACC, local, first_i, iota_n, ident, minus_p, acc, table1,
                   parts_d, local_d, idx, hid_d, vec, weight, w2, parts_s)

        with ExitStack() as st:
            sb, ps, sem = maker(st)
            y = sb("y6", [P, NN, F])
            x1 = sb("x1_again", [P, NN, F])
            sq = sb("sq6", [P, NN, F])
            stat = sb("stat6", [P, 2, NN])
            p_n = [ps("p_m0"), ps("p_m1")]
            sums6_mm, sums6_copied, d6, want6, got6, y_made, y_stored, x1_back = (
                sem("sums6_mm"), sem("sums6_copied"), sem("d6"), sem("want6"), sem("got6"), sem("y_made"), sem("y_stored"),
                sem("x1_back"))

            block = st.enter_context(nc.Block())

            @block.sync
            def _(sp):
                sp.dma_start(x1[:], table1.rearrange("(n p) f -> p n f", p=P)).then_inc(x1_back, 16)
                sp.wait_ge(y_made, 1)
                sp.dma_start(out.rearrange("(n p) f -> p n f", p=P), y[:]).then_inc(y_stored, 16)
                sp.wait_ge(y_stored, 16)

            @block.tensor
            def _(pe):
                for g in range(NN // NG):
                    if g >= 2:
                        pe.wait_ge(sums6_copied, g - 1)
                    for j in range(NG):
                        n = g * NG + j
                        mm = pe.transpose(p_n[g % 2][:, j * F:(j + 1) * F], acc[0:F, n * P:(n + 1) * P],
                                          ident[0:F, 0:F])
                    mm.then_inc(sums6_mm, 1)

            @block.scalar
            def _(act):
                act.wait_ge(want6, 1)
                act.activation(stat[:, 0], stat[:, 1], ACT.Sqrt).then_inc(got6, 1)

            @block.vector
            def _(dve):
                done = [0]

                def then(ins):
                    done[0] += 1
                    ins.then_inc(d6, 1)
                    dve.wait_ge(d6, done[0])

                dve.wait_ge(x1_back, 16)
                for g in range(NN // NG):
                    dve.wait_ge(sums6_mm, g + 1)
                    dve.tensor_tensor(y[:, g * NG:(g + 1) * NG].rearrange("p n f -> p (n f)"),
                                      p_n[g % 2][:, 0:NG * F],
                                      x1[:, g * NG:(g + 1) * NG].rearrange("p n f -> p (n f)"), ALU.add
                                      ).then_inc(sums6_copied, 1)
                dve.wait_ge(sums6_copied, NN // NG)
                layernorm(then, dve, got6, want6, y[:], stat, sq[:])
                dve.sem_inc(y_made, 1)


def edge_layer(nc, maker, NB, NT, ACC, local, first_i, iota_n, ident, minus_p, acc, table1,
               parts_d, local_d, idx, hid_d, vec, weight, w2, parts_s):
    HT = T // 2
    OA = 48
    OB = 48
    QB = OB + 16
    LAST = 3
    with ExitStack() as st:
        sb, ps, sem = maker(st)
        vec_s = sb("vec_s", [P, NT, 3])
        weight_s = sb("weight_s", [P, NT])
        w_f = sb("w_f", [K6, 896])
        w_top = sb("w_top", [K6, 896], BF16)
        w_part = sb("w_part", [K6, 896], BF16)
        hid = sb("hid5", [K6, RING, 2, T * P], BF16)
        idx_b = sb("idx_b5", [P, RING, T, 2], I32)
        source = sb("source", [P, RING, T, F])
        dst_row = sb("dst_row", [P, 2, T * P])
        hot_n = sb("hot_n", [P, 2, T * P], BF16)
        nodes = sb("nodes", [P, RING, T, 3 * F], BF16)
        s1 = sb("s1", [P, 2, T, 16])
        v1 = sb("v1", [P, 2, T, 3, 16])
        vr = sb("vr", [P, T, 3, 16])
        vdot = sb("vdot", [P, 2, T, 16])
        prod = sb("prod", [P, 2, HT, 16, OA])
        suma = sb("suma", [P, 2, T, OA])
        in_b = sb("in_b", [P, T, 16])
        vt = sb("vt", [P, T, 3, 8])
        vt_r = sb("vt_r", [P, T, 3, 8])
        prodb = sb("prodb", [P, 2, HT, 8, QB])
        th = sb("th", [P, 2, T, 16])
        cv = sb("cv", [P, 2, T, 32])
        wth = sb("wth", [P, T, 16])
        msg = sb("msg", [P, T, 3, 8])
        z = sb("z5", [P, 2, T, F])
        hot = sb("hot5", [P, 2, T, P])
        absd = sb("absd", [P, T, P])
        sq = prod[:].rearrange("p a t u o -> p (a t u o)")[:, 0:NT * 3].rearrange("p (t k) -> p t k", k=3)
        flat = prodb[:].rearrange("p a t u o -> p (a t u o)")
        length, root = flat[:, 0:NT], flat[:, NT:NT * 2]
        p_w = [ps(f"p_w{n}") for n in range(4)]
        p_suma, p_sumb = ps("p_suma"), ps("p_sumb")
        p_win, p_dst = ps("p_win"), ps("p_dst")
        dst_v = p_dst[:, 0:T * F].rearrange("p (t f) -> p t f", f=F)
        suma_v = p_suma[:, 0:T * OA].rearrange("p (t o) -> p t o", o=OA)
        sumb_v = p_sumb[:, 0:T * OB].rearrange("p (t o) -> p t o", o=OB)

        const_landed, vec_landed, weight_landed = sem("const_landed"), sem("vec_landed"), sem("weight_landed")
        dir_step, dir_want, dir_root = sem("dir_step"), sem("dir_want"), sem("dir_root")
        acc_zeroed5, weights_split = sem("acc_zeroed5"), sem("weights_split")
        hid_landed = [sem(f"hid_landed{b}") for b in range(RING)]
        idx_landed5 = [sem(f"idx_landed5_{b}") for b in range(RING)]
        source_landed = [sem(f"source_landed{b}") for b in range(RING)]
        row_landed = [sem(f"row_landed{b}") for b in range(2)]
        nodes_landed = [sem(f"nodes_landed{b}") for b in range(RING)]
        row_abs, hot_n_done, dst_mm = sem("row_abs"), sem("hot_n_done"), sem("dst_mm")
        halved_a, halved_b = sem("halved_a"), sem("halved_b")
        ends_split, ends_read = sem("ends_split"), sem("ends_read")
        w_mm, w_used = sem("w_mm"), sem("w_used")
        suma_mm, suma_copied, sumb_mm = sem("suma_mm"), sem("suma_copied"), sem("sumb_mm")
        vdot_step, mid_step, msg_step = sem("vdot_step"), sem("mid_step"), sem("msg_step")
        sumb_read, z_done, abs_done, hot_done = sem("sumb_read"), sem("z_done"), sem("abs_done"), sem("hot_done")
        win_mm5, win_added5 = sem("win_mm5"), sem("win_added5")

        def run(eng, body):
            for b in range(RING):
                body(0, b, b)
            with eng.Fori(1, NB // RING - 1) as k:
                for b in range(RING):
                    body(k, b, None)
            for b in range(RING):
                body(NB // RING - 1, b, NB - RING + b)
            for b in range(LAST):
                body(NB // RING, b, NB + b)

        def has(lo, lag):
            return lo is None or 0 <= lo - lag < NB

        def past(lo, n):
            return lo is None or lo >= n

        def a_tiles(i, lo):
            return 0 if lo == 0 else 2 * T * i - T

        def b_tiles(i, lo):
            return 2 * T * NB - T if lo == NB else 2 * T * i

        def a_end(i, lo):
            return a_tiles(i, lo) + T

        block = st.enter_context(nc.Block())

        @block.sync
        def _(sp):
            sp.dma_start(w_f[:], w2).then_inc(const_landed, 16)
            sp.dma_start(vec_s[:].rearrange("p t k -> p (t k)"), vec).then_inc(vec_landed, 16)
            sp.dma_start(weight_s[:], weight).then_inc(weight_landed, 16)

            def body(k, b, lo):
                i = k * RING + b
                if not has(lo, 0):
                    return
                if past(lo, RING):
                    sp.wait_ge(ends_read, i - RING + 1)
                    sp.nop(nofuse=True)
                sp.dma_start(idx_b[:, b].rearrange("p t two -> p (t two)"), idx[:, bass.ds(i * (2 * T), 2 * T)]
                             ).then_inc(idx_landed5[b], 16)
                if past(lo, RING):
                    sp.wait_ge(dst_mm, i - RING + 1)
                    sp.nop(nofuse=True)
                if past(lo, 2):
                    sp.wait_ge(hot_n_done, i - 1)
                    sp.nop(nofuse=True)
                sp.dma_start(dst_row[:, b % 2], local_d[bass.ds(i * (T * P), T * P)].partition_broadcast(P)
                             ).then_inc(row_landed[b % 2], 16)
                _, bases = nc.values_load_multi_w_load_instructions(
                    first_i[0:1, bass.ds(i * T, T)], engines=[mybir.EngineType.SP], min_val=0, max_val=ACC - P)
                for t in range(T):
                    sp.dma_start(nodes[:, b, t], parts_d[bass.ds(bases[t], P)]).then_inc(nodes_landed[b], 16)
                if past(lo, RING):
                    sp.wait_ge(w_mm, 2 * T * (i - 3) + T)
                    sp.nop(nofuse=True)
                sp.dma_start(hid[:, b].rearrange("p n e -> p (n e)"), hid_d[:, bass.ds(i * (2 * T * P), 2 * T * P)]
                             ).then_inc(hid_landed[b], 16)
            run(sp, body)

        @block.gpsimd
        def _(pool):
            def gather(k, b, i, lo, ts):
                if ts[0] == 0:
                    if past(lo, RING):
                        pool.wait_ge(ends_read, i - RING + 1)
                    pool.wait_ge(idx_landed5[b], 16 * (k + 1))
                    pool.nop(nofuse=True)
                for t in ts:
                    pool.indirect_dma_start(source[:, b, t], None, table1,
                                            bass.IndirectOffsetOnAxis(ap=idx_b[:, b, t, 0:1], axis=0)
                                            ).then_inc(source_landed[b], 16)

            def halve_a(i, lo, h):
                pool.wait_ge(w_used, a_tiles(i, lo) + (h + 1) * HT)
                pool.tensor_tensor(prod[:, h, :, 0:8, :], prod[:, h, :, 0:8, :], prod[:, h, :, 8:16, :], ALU.add
                                   ).then_inc(halved_a, 1)

            def body(k, b, lo):
                i = k * RING + b
                kn, bn = k + (b + 2) // RING, (b + 2) % RING
                ahead = None if lo is None else lo + 2
                if has(lo, -2):
                    gather(kn, bn, i + 2, ahead, range(0, 3))
                if has(lo, 0):
                    halve_a(i, lo, 0)
                if has(lo, -2):
                    gather(kn, bn, i + 2, ahead, range(3, 6))
                if has(lo, 0):
                    halve_a(i, lo, 1)
                if has(lo, -2):
                    gather(kn, bn, i + 2, ahead, range(6, T))
                if has(lo, 1):
                    pool.wait_ge(w_used, b_tiles(i, lo) + HT)
                    pool.tensor_tensor(prodb[:, 0, :, 0:4, :], prodb[:, 0, :, 0:4, :], prodb[:, 0, :, 4:8, :], ALU.add
                                       ).then_inc(halved_b, 1)
            gather(0, 0, 0, 0, range(T))
            gather(0, 1, 1, 1, range(T))
            run(pool, body)

        @block.tensor
        def _(pe):
            def body(k, b, lo):
                i = k * RING + b

                def weights(t, net):
                    if not has(lo, net):
                        return
                    n = (b_tiles if net else a_tiles)(i, lo) + t
                    if t == 0 and net == 0:
                        pe.wait_ge(hid_landed[b], 16 * (k + 1))
                    if past(lo, 1) or t >= 4:
                        pe.wait_ge(w_used, n - 3)
                    cols = slice(512, 896) if net else slice(0, 512)
                    pe.matmul(p_w[t % 4][:, 0:cols.stop - cols.start], hid[:, (b - net) % RING, net, t * P:(t + 1) * P],
                              w_part[:, cols], start=True, stop=True).then_inc(w_mm, 1)

                def sum_a(h, us):
                    if not has(lo, 0):
                        return
                    if us[0] == 0:
                        pe.wait_ge(halved_a, 2 * i + h + 1)
                        if past(lo, 1) and h == 0:
                            pe.wait_ge(suma_copied, i)
                    for u in us:
                        mm = pe.matmul(p_suma[:, h * HT * OA:(h + 1) * HT * OA], ident[:], prod[:, h, :, u, :],
                                       start=(u == 0), stop=(u == 7))
                    if us[-1] == 7:
                        mm.then_inc(suma_mm, 1)

                def sum_b(h, us):
                    if not has(lo, 2):
                        return
                    last = 7 if h else 3
                    if us[0] == 0:
                        if h == 0:
                            pe.wait_ge(halved_b, i - 1)
                            if past(lo, 3):
                                pe.wait_ge(sumb_read, 2 * (i - 2))
                        else:
                            pe.wait_ge(w_used, b_tiles(i - 1, None if lo is None else lo - 1) + T)
                    for u in us:
                        pe.matmul(sumb_v[:, h * HT:(h + 1) * HT], ident[:], prodb[:, h, :, u, 0:OB],
                                  start=(u == 0), stop=False, skip_group_check=True)
                        mm = pe.matmul(sumb_v[:, h * HT:(h + 1) * HT, 0:16], ident[:], prodb[:, h, :, u, OB:QB],
                                       start=False, stop=(u == last), skip_group_check=True)
                    if us[-1] == last:
                        mm.then_inc(sumb_mm, 1)

                def windows(h):
                    if not has(lo, 3):
                        return
                    if h == 0:
                        pe.wait_ge(z_done, i - 2)
                        pe.wait_ge(hot_done, i - 2)
                    if past(lo, 4) or h:
                        pe.wait_ge(win_added5, 2 * T * (i - 3) + h * T)
                    for t in range(h * HT, (h + 1) * HT):
                        mm = pe.matmul(p_win[0:F, (t % HT) * P:(t % HT + 1) * P], z[:, (b - 3) % 2, t], hot[:, (b - 3) % 2, t],
                                       start=True, stop=True)
                    mm.then_inc(win_mm5, 1)

                for t in range(4):
                    weights(t, 0)
                windows(0)
                sum_b(0, range(4))
                weights(4, 0)
                sum_b(1, range(0, 4))
                weights(5, 0)
                sum_b(1, range(4, 8))
                weights(6, 0)
                weights(7, 0)
                if has(lo, -1):
                    destinations(k + (b + 1) // RING, (b + 1) % RING, i + 1, None if lo is None else lo + 1)
                weights(0, 1)
                weights(1, 1)
                sum_a(0, range(0, 4))
                weights(2, 1)
                sum_a(0, range(4, 8))
                weights(3, 1)
                windows(1)
                weights(4, 1)
                weights(5, 1)
                sum_a(1, range(0, 4))
                weights(6, 1)
                sum_a(1, range(4, 8))
                weights(7, 1)

            def destinations(k, b, i, lo):
                pe.wait_ge(nodes_landed[b], 16 * T * (k + 1))
                pe.wait_ge(hot_n_done, i + 1)
                if past(lo, 1):
                    pe.wait_ge(ends_split, 4 * i)
                for t in range(T):
                    for part in range(3):
                        mm = pe.matmul(dst_v[:, t], hot_n[:, b % 2, t * P:(t + 1) * P], nodes[:, b, t, part * F:(part + 1) * F],
                                       start=(part == 0), stop=(part == 2))
                mm.then_inc(dst_mm, 1)
            destinations(0, 0, 0, 0)
            pe.wait_ge(weights_split, 1)
            run(pe, body)

        @block.scalar
        def _(act):
            def split(k, b, i, lo):
                act.wait_ge(source_landed[b], (k + 1) * 16 * T)
                act.wait_ge(dst_mm, i + 1)
                if past(lo, 2):
                    act.wait_ge(w_used, a_end(i - 2, None if lo is None else lo - 2))
                for j, end in enumerate((source[:, b], dst_v)):
                    act.activation(s1[:, b % 2, :, 8 * j:8 * j + 8], end[:, :, 0:8], ACT.Copy).then_inc(ends_split, 1)
                    act.activation(v1[:, b % 2, :, :, 8 * j:8 * j + 8],
                                   end[:, :, 8:F].rearrange("p t (u k) -> p t k u", k=3), ACT.Copy
                                   ).then_inc(ends_split, 1)

            def one_hot_nodes(k, b, i, lo):
                act.wait_ge(row_landed[b % 2], 32 * k + 16 * (b // 2) + 16)
                act.activation(dst_row[:, b % 2], dst_row[:, b % 2], ACT.Abs, bias=minus_p[:, 0:1]).then_inc(row_abs, 1)
                if past(lo, 2):
                    act.wait_ge(dst_mm, i - 1)
                act.wait_ge(row_abs, i + 1)
                act.activation(hot_n[:, b % 2], dst_row[:, b % 2], ACT.Relu, scale=-1.0, bias=1.0).then_inc(hot_n_done, 1)

            def body(k, b, lo):
                i = k * RING + b
                if has(lo, 1):
                    act.wait_ge(suma_mm, 2 * i)
                    if past(lo, 3):
                        act.wait_ge(mid_step, 5 * (i - 2))
                    act.activation(suma[:, (b - 1) % 2], suma_v, ACT.Copy).then_inc(suma_copied, 1)
                if has(lo, 2):
                    if past(lo, 3):
                        act.wait_ge(hot_done, i - 2)
                    for t in range(T):
                        act.activation(absd[:, t], iota_n[:], ACT.Abs, bias=local[:, bass.ds((i - 2) * T + t, 1)]
                                       ).then_inc(abs_done, 1)
                    act.wait_ge(abs_done, (i - 1) * T)
                    if past(lo, 4):
                        act.wait_ge(win_mm5, 2 * (i - 3))
                    act.activation(hot[:, b % 2], absd[:], ACT.Relu, scale=-1.0, bias=1.0).then_inc(hot_done, 1)
                    act.wait_ge(sumb_mm, 2 * (i - 1))
                    if past(lo, 4):
                        act.wait_ge(z_done, i - 3)
                    act.activation(th[:, b % 2], sumb_v[:, :, 0:16], ACT.Tanh).then_inc(sumb_read, 1)
                    act.activation(cv[:, b % 2], sumb_v[:, :, 16:48], ACT.Copy).then_inc(sumb_read, 1)
                if has(lo, -1):
                    split(k + (b + 1) // RING, (b + 1) % RING, i + 1, None if lo is None else lo + 1)
                if has(lo, -1):
                    act.wait_ge(ends_split, 4 * (i + 2))
                    act.sem_inc(ends_read, 1)
                if has(lo, 3):
                    _, bases = nc.values_load_multi_w_load_instructions(
                        first_i[0:1, bass.ds((i - 3) * T, T)], engines=[mybir.EngineType.Activation],
                        min_val=0, max_val=ACC - P)
                    add_windows(lo, i, 0, bases)
                if has(lo, -2):
                    one_hot_nodes(k + (b + 2) // RING, (b + 2) % RING, i + 2, None if lo is None else lo + 2)
                if has(lo, 3):
                    add_windows(lo, i, 1, bases)

            def add_windows(lo, i, h, bases):
                act.wait_ge(win_mm5, 2 * (i - 3) + h + 1)
                for t in range(h * HT, (h + 1) * HT):
                    pw = p_win[0:F, (t % HT) * P:(t % HT + 1) * P]
                    if past(lo, 4) or t:
                        act.wait_ge(win_added5, 2 * (T * (i - 3) + t))
                    act.activation(acc[:, bass.ds(bases[t], 1)], pw[:, 0:1], ACT.Identity,
                                   bias=acc[:, bass.ds(bases[t], 1)]).then_inc(win_added5, 1)
                    act.activation(acc[:, bass.ds(bases[t] + 1, P - 1)], pw[:, 1:P], ACT.Copy).then_inc(win_added5, 1)
            act.wait_ge(dir_want, 1)
            act.activation(root, length, ACT.Sqrt).then_inc(dir_root, 1)
            act.wait_ge(acc_zeroed5, 2)
            one_hot_nodes(0, 0, 0, 0)
            one_hot_nodes(0, 1, 1, 1)
            split(0, 0, 0, 0)
            act.wait_ge(ends_split, 4)
            act.sem_inc(ends_read, 1)
            run(act, body)
            act.wait_ge(win_added5, 2 * T * NB)

        @block.vector
        def _(dve):
            done = [0]

            def then(ins):
                done[0] += 1
                ins.then_inc(dir_step, 1)
                dve.wait_ge(dir_step, done[0])

            dve.memset(acc[:], 0.0).then_inc(acc_zeroed5, 1)
            dve.wait_ge(const_landed, 16)
            sa, sb_ = 1.0 / np.sqrt(H) / np.sqrt(32.0), 1.0 / np.sqrt(H) / np.sqrt(16.0)
            for a, b, scale in ((0, 128, sa), (128, 256, sa * np.sqrt(3.0)), (256, 512, sa), (512, 768, sb_),
                                (768, 832, sb_ * np.sqrt(3.0)), (832, 896, sb_)):
                then(dve.tensor_scalar(w_f[:, a:b], w_f[:, a:b], float(scale), None, ALU.mult))
            then(dve.tensor_copy(w_top[:], w_f[:]))
            then(dve.scalar_tensor_tensor(out=w_f[:], in0=w_top[:], scalar=parts_s[:, 2:3], in1=w_f[:],
                                          op0=ALU.mult, op1=ALU.add))
            then(dve.tensor_copy(w_top[:], w_f[:]))
            then(dve.scalar_tensor_tensor(out=w_part[:], in0=w_top[:], scalar=parts_s[:, 3:4], in1=w_f[:],
                                          op0=ALU.mult, op1=ALU.add))
            dve.sem_inc(weights_split, 1)
            dve.wait_ge(vec_landed, 16)
            then(dve.tensor_tensor(sq, vec_s[:], vec_s[:], ALU.mult))
            then(dve.tensor_reduce(length, sq, AX_X, ALU.add))
            dve.sem_inc(dir_want, 1)
            dve.wait_ge(dir_root, 1)
            then(dve.reciprocal(length, root))
            then(dve.tensor_tensor(vec_s[:], vec_s[:], length.unsqueeze(2).to_broadcast([P, NT, 3]), ALU.mult))
            then(dve.tensor_scalar(local[:], local[:], -1.0, None, ALU.mult))
            dve.sem_inc(acc_zeroed5, 1)
            dve.wait_ge(weight_landed, 16)

            def direction(i):
                return vec_s[:, bass.ds(i * T, T)]

            def vdot_steps(b, i, lo):
                r = b % 2

                def one():
                    dve.wait_ge(ends_split, 4 * (i + 1))
                    dve.tensor_tensor(vr[:], v1[:, r], direction(i).unsqueeze(3).to_broadcast([P, T, 3, 16]), ALU.mult
                                      ).then_inc(vdot_step, 1)

                def two():
                    dve.wait_ge(vdot_step, 2 * i + 1)
                    if past(lo, 2):
                        dve.wait_ge(w_used, a_end(i - 2, None if lo is None else lo - 2))
                    dve.tensor_reduce(vdot[:, r], vr[:].rearrange("p t k u -> p t u k"), AX_X, ALU.add
                                      ).then_inc(vdot_step, 1)
                return [one, two]

            def multiply_a(b, i, lo, t):
                r, h = b % 2, t // HT
                pw = p_w[t % 4]
                o = prod[:, h, t % HT].rearrange("p u o -> p o u")
                if t == 0:
                    dve.wait_ge(vdot_step, 2 * i + 2)
                if t % HT == 0 and past(lo, 1):
                    dve.wait_ge(suma_mm, 2 * i - 1 + h)
                dve.wait_ge(w_mm, a_tiles(i, lo) + t + 1)
                dve.tensor_tensor(o[:, 0:16], pw[:, 0:256].rearrange("p (o u) -> p o u", u=16),
                                  s1[:, r, t].unsqueeze(1).to_broadcast([P, 16, 16]), ALU.mult)
                dve.tensor_tensor(o[:, 16:24], pw[:, 256:384].rearrange("p (o u) -> p o u", u=16),
                                  vdot[:, r, t].unsqueeze(1).to_broadcast([P, 8, 16]), ALU.mult)
                dve.tensor_tensor(o[:, 24:48].rearrange("p (k o) u -> p k o u", k=3),
                                  pw[:, 384:512].rearrange("p (o u) -> p o u", u=16).unsqueeze(1).to_broadcast([P, 3, 8, 16]),
                                  v1[:, r, t].unsqueeze(2).to_broadcast([P, 3, 8, 16]), ALU.mult).then_inc(w_used, 1)

            def mid_steps(b, i, lo):
                sa = suma[:, b % 2]

                def one():
                    dve.wait_ge(suma_copied, i + 1)
                    if past(lo, 2):
                        dve.wait_ge(w_used, 2 * T * i + T)
                    dve.tensor_tensor(in_b[:, :, 0:8], sa[:, :, 0:8], sa[:, :, 16:24], ALU.add).then_inc(mid_step, 1)

                def two():
                    dve.tensor_tensor(vt_r[:], sa[:, :, 8:16].unsqueeze(2).to_broadcast([P, T, 3, 8]),
                                      direction(i).unsqueeze(3).to_broadcast([P, T, 3, 8]), ALU.mult).then_inc(mid_step, 1)

                def three():
                    dve.wait_ge(mid_step, 5 * i + 2)
                    dve.tensor_tensor(vt[:].rearrange("p t k o -> p t (k o)"), vt_r[:].rearrange("p t k o -> p t (k o)"),
                                      sa[:, :, 24:48], ALU.add).then_inc(mid_step, 1)

                def four():
                    dve.wait_ge(mid_step, 5 * i + 3)
                    dve.tensor_tensor(vt_r[:], vt[:], direction(i).unsqueeze(3).to_broadcast([P, T, 3, 8]), ALU.mult
                                      ).then_inc(mid_step, 1)

                def five():
                    dve.wait_ge(mid_step, 5 * i + 4)
                    dve.tensor_reduce(in_b[:, :, 8:16], vt_r[:].rearrange("p t k o -> p t o k"), AX_X, ALU.add
                                      ).then_inc(mid_step, 1)
                return [one, two, three, four, five]

            def multiply_b(b, i, it, lo, t):
                h = t // HT
                pw, q = p_w[t % 4], prodb[:, h, t % HT]
                if t == 0:
                    dve.wait_ge(mid_step, 5 * i + 5)
                if t % HT == 0 and past(lo, 2):
                    dve.wait_ge(sumb_mm, 2 * i - 1 + h)
                dve.wait_ge(w_mm, b_tiles(it, lo) + t + 1)
                for half, at in ((0, 0), (1, OB)):
                    dve.tensor_tensor(q[:, :, at:at + 16].rearrange("p u o -> p o u"),
                                      pw[:, 0:256].rearrange("p (o j u) -> p j o u", j=2, u=8)[:, half],
                                      in_b[:, t, 8 * half:8 * half + 8].unsqueeze(1).to_broadcast([P, 16, 8]), ALU.mult)
                dve.tensor_tensor(q[:, :, 16:24].rearrange("p u o -> p o u"),
                                  pw[:, 256:320].rearrange("p (o u) -> p o u", u=8),
                                  in_b[:, t, 0:8].unsqueeze(1).to_broadcast([P, 8, 8]), ALU.mult)
                dve.tensor_tensor(q[:, :, 24:48].rearrange("p u (k o) -> p k o u", k=3),
                                  pw[:, 320:384].rearrange("p (o u) -> p o u", u=8).unsqueeze(1).to_broadcast([P, 3, 8, 8]),
                                  vt[:, t].unsqueeze(2).to_broadcast([P, 3, 8, 8]), ALU.mult).then_inc(w_used, 1)

            def message_steps(b, i, lo):
                r = b % 2

                def one():
                    dve.wait_ge(sumb_read, 2 * (i + 1))
                    dve.tensor_tensor(msg[:], cv[:, r, :, 0:8].unsqueeze(2).to_broadcast([P, T, 3, 8]),
                                      direction(i).unsqueeze(3).to_broadcast([P, T, 3, 8]), ALU.mult).then_inc(msg_step, 1)

                def two():
                    dve.wait_ge(msg_step, 4 * i + 1)
                    dve.tensor_tensor(msg[:].rearrange("p t k o -> p t (k o)"), msg[:].rearrange("p t k o -> p t (k o)"),
                                      cv[:, r, :, 8:32], ALU.add).then_inc(msg_step, 1)

                def three():
                    dve.tensor_tensor(wth[:], th[:, r],
                                      weight_s[:, bass.ds(i * T, T)].unsqueeze(2).to_broadcast([P, T, 16]), ALU.mult
                                      ).then_inc(msg_step, 1)

                def four():
                    dve.wait_ge(msg_step, 4 * i + 3)
                    if past(lo, 4):
                        dve.wait_ge(win_mm5, 2 * (i - 1))
                    dve.tensor_copy(z[:, r, :, 0:8], wth[:, :, 0:8]).then_inc(msg_step, 1)

                def five():
                    dve.wait_ge(msg_step, 4 * i + 4)
                    dve.tensor_tensor(z[:, r, :, 8:F].rearrange("p t (o k) -> p t k o", k=3), msg[:],
                                      wth[:, :, 8:16].unsqueeze(2).to_broadcast([P, T, 3, 8]), ALU.mult).then_inc(z_done, 1)
                return [one, two, three, four, five]

            def body(k, b, lo):
                i = k * RING + b
                mid = mid_steps(b - 1, i - 1, lo) if has(lo, 1) else []
                message = message_steps(b - 2, i - 2, lo) if has(lo, 2) else []
                vdot_next = vdot_steps(b + 1, i + 1, None if lo is None else lo + 1) if has(lo, -1) else []
                for t in range(T):
                    if has(lo, 0):
                        multiply_a(b, i, lo, t)
                    if mid:
                        mid.pop(0)()
                    elif message and t >= 6:
                        message.pop(0)()
                for step in mid:
                    step()
                for t in range(T):
                    if has(lo, 1):
                        multiply_b(b - 1, i - 1, i, lo, t)
                    if message:
                        message.pop(0)()
                    elif vdot_next:
                        vdot_next.pop(0)()
                for step in message + vdot_next:
                    step()
            for step in vdot_steps(0, 0, 0):
                step()
            run(dve, body)


def kernel(x, src, dst, edge_attr_10, edge_attr_3, edge_weight, L0_gnn_W, L0_gnn_att_src, L0_gnn_att_dst, L0_gnn_bias,
           L1_gnn_fc1_w1, L1_gnn_fc1_w2, L1_gnn_fc2_w1, L1_gnn_fc2_w2):
    import concourse.bacc as bacc
    from concourse.bass_utils import run_bass_kernel_spmd

    n, e = x.shape[0], src.shape[0]
    NN = -(-(n + 1) // (P * NG)) * NG
    NT = -(-e // (P * P)) * P
    x, src, dst = np.asarray(x), np.asarray(src), np.asarray(dst)
    e10, e3, ew = np.asarray(edge_attr_10), np.asarray(edge_attr_3), np.asarray(edge_weight)
    E = NT * P

    x_pad = np.zeros((NN * P, F), x.dtype)
    x_pad[:n] = x
    src_pad = np.full(E, n, src.dtype)
    src_pad[:e] = src
    dst_ext = np.full(E + P + 1, n + 1, dst.dtype)
    dst_ext[0] = -1
    dst_ext[1:e + 1] = dst
    dst_ext[e + 1:E + 1] = n
    emb = np.zeros((EMB, E), e10.dtype)
    emb[:, :e] = e10.T
    vec = np.ones((E, 3), e3.dtype)
    vec[:e] = e3
    wgt = np.zeros(E, ew.dtype)
    wgt[:e] = ew

    def by_tile(a):
        return np.ascontiguousarray(np.moveaxis(a.reshape((NT, P) + a.shape[1:]), 0, 1))

    def columns(w, first, u):
        return np.asarray(w)[:, first:first + u * 8].reshape(H, u, 8).transpose(0, 2, 1).reshape(H, u * 8)

    f1, f2 = L1_gnn_fc1_w2, L1_gnn_fc2_w2
    w2 = [columns(f1, first, 16) for first in (0, 256, 128, 384)]
    for ss, vv in ((0, 64), (128, 192)):
        both = np.concatenate([columns(f2, ss, 8).reshape(H, 8, 8), columns(f2, vv, 8).reshape(H, 8, 8)], axis=2)
        w2.append(both.reshape(H, 128))
    w2 += [columns(f2, 256, 8), columns(f2, 320, 8)]
    parts = np.repeat(np.array([[-float(a > 0), -float(a > 1), -float(b > 0), -float(b > 1)]
                                for a, b in zip(HID_PART, W_PART)], np.float32), H, axis=0)

    arrays = {
        "xT": np.ascontiguousarray(x_pad.T), "xN": x_pad,
        "w": np.asarray(L0_gnn_W), "wT": np.ascontiguousarray(np.asarray(L0_gnn_W).T),
        "att": np.stack([np.asarray(L0_gnn_att_src), np.asarray(L0_gnn_att_dst)], axis=1),
        "bias": np.asarray(L0_gnn_bias),
        "idx": by_tile(np.stack([src_pad, dst_ext[1:E + 1]], axis=1)).reshape(P, NT * 2),
        "dst_ext": dst_ext, "src_flat": src_pad,
        "emb": emb, "vec": by_tile(vec).reshape(P, NT * 3), "weight": by_tile(wgt),
        "fc1": np.concatenate([np.tile(np.asarray(L1_gnn_fc1_w1), (1, 6)), np.tile(np.asarray(L1_gnn_fc2_w1), (1, 6))],
                              axis=1),
        "w2": np.tile(np.concatenate(w2, axis=1), (6, 1)), "parts": parts,
    }
    nc = bacc.Bacc("TRN2", target_bir_lowering=False, num_devices=1)
    args = [nc.dram_tensor("in_" + name, a.shape, mybir.dt.from_np(a.dtype), kind="ExternalInput").ap()
            for name, a in arrays.items()]
    out = nc.dram_tensor("nodes_out", (NN * P, F), F32, kind="ExternalOutput").ap()
    gnn_kernel(nc, *args, out, NN, NT)
    r = run_bass_kernel_spmd(nc, [{"in_" + name: a for name, a in arrays.items()}], core_ids=[0])
    return r.results[0]["nodes_out"][:n]
```

```python
from contextlib import ExitStack

import numpy as np

import concourse.bass as bass
from concourse import mybir

F32 = mybir.dt.float32
BF16 = mybir.dt.bfloat16
I32 = mybir.dt.int32
ALU = mybir.AluOpType
ACT = mybir.ActivationFunctionType
AX_X = mybir.AxisListType.X

P = 128
T = 8
RING = 4
F = 32
H = 16
EMB = 10
R0 = F + 2
BIG = 1.0e30
EPS = 1.0e-5
SLOPE = 0.2
K6 = 6 * H
HID_PART = (0, 0, 1, 0, 1, 2)
W_PART = (0, 1, 0, 2, 1, 0)
NG = 14


def gnn_kernel(nc, xT, xN, w, wT, att, bias, idx, dst_ext, src_flat, emb, vec, weight,
               fc1, w2, parts, out, NN, NT):
    NB = NT // T
    NC = NT // P
    ACC = (NN + 1) * P
    assert NB % RING == 0 and NT % P == 0

    table = nc.dram_tensor("table0", (NN * P, R0), F32).ap()
    table1 = nc.dram_tensor("table1", (NN * P, F), F32).ap()
    spill = nc.dram_tensor("spill", (P, NT * R0), F32).ap()
    hid_d = nc.dram_tensor("hid_d", (K6, NT * P * 2), BF16).ap()
    parts_d = nc.dram_tensor("parts_d", ((NN + 1) * P, 3 * F), BF16).ap()
    direction_d = nc.dram_tensor("direction_d", (P, NT * 3), F32).ap()
    rows_d = nc.dram_tensor("rows_d", (P, NN * F), F32).ap()
    local_d = nc.dram_tensor("local_d", (NT * P,), F32).ap()
    ends_d = nc.dram_tensor("ends_d", (4, NT), F32).ap()
    carry_d = nc.dram_tensor("carry_d", (4, NT), F32).ap()

    outer = ExitStack()
    with outer:
        outer.enter_context(nc.allow_non_contiguous_dma(reason="one element of each edge tile, once"))

        def maker(stack):
            def sb(name, shape, dt=F32):
                return stack.enter_context(nc.sbuf_tensor(name, shape, dt))

            def ps(name, shape=(P, 512)):
                return stack.enter_context(nc.psum_tensor(name, list(shape), F32))

            def sem(name):
                return outer.enter_context(nc.semaphore(name))
            return sb, ps, sem

        sb, _, sem = maker(outer)

        iota_n = sb("iota_n", [P, P])
        ident = sb("ident", [P, P])
        first_i = sb("first_i", [1, NT], I32)
        local = sb("local", [P, NT])
        parts_s = sb("parts_s", [K6, 4])
        minus_p = sb("minus_p", [P, 1])
        bias_b = sb("bias_b", [P, F])
        layer0 = ExitStack()
        idx_all = layer0.enter_context(nc.sbuf_tensor("idx_all", [P, NT, 2], I32))
        nodes0 = layer0.enter_context(nc.sbuf_tensor("nodes0", [P, NN, R0], F32))

        asd = layer0.enter_context(nc.sbuf_tensor("asd", [P, 2, NT], F32))
        with ExitStack() as st:
            sb, ps, sem = maker(st)
            xT_s = sb("xT_s", [F, NN * P])
            w_s = sb("w_s", [F, R0])
            wT_s = sb("wT_s", [F, F])
            att_s = sb("att_s", [F, 2])
            iota_i = sb("iota_i", [P, P], I32)
            part_i = sb("part_i", [P, 1], I32)
            part_f = sb("part_f", [P, 1])
            idx_b = sb("idx_b", [P, RING, T, 2], I32)
            vec_s = sb("vec_1", [P, NT, 3])
            rows = sb("rows", [P, RING, T, R0])
            fc1_s = sb("fc1_s", [EMB, 2, K6])
            emb_s = sb("emb_s", [EMB, RING, T * P])
            hid = sb("hid", [K6, RING, 2, T * P])
            top = sb("top", [K6, 2, 2, T * P], BF16)
            part = sb("part", [K6, 2, 2, T * P], BF16)
            p_hid = [[ps(f"p_hid{n}{h}") for h in range(2)] for n in range(2)]
            p_att = ps("p_att")
            p_tab = [ps("p_tab0"), ps("p_tab1")]

            w_landed, xT_landed, idx_landed, first_landed = sem("w_landed"), sem("xT_landed"), sem("idx_landed"), sem("first_landed")
            iota_made, part_cast, consts_made = sem("iota_made"), sem("part_cast"), sem("consts_made")
            att_mm, att_copied, tab_mm, tab_copied, tab_stored = sem("att_mm"), sem("att_copied"), sem("tab_mm"), sem("tab_copied"), sem("tab_stored")
            rows_split = sem("rows_split")
            idx_fetched = [sem(f"idx_fetched{b}") for b in range(RING)]
            vec_landed, vec_root, vec_rooted, vec_step, vec_done, vec_stored = (
                sem("vec_landed1"), sem("vec_root"), sem("vec_rooted"), sem("vec_step"), sem("vec_done"), sem("vec_stored"))
            rows_landed = [sem(f"rows_landed{b}") for b in range(RING)]
            rows_spilled = [sem(f"rows_spilled{b}") for b in range(RING)]
            emb_landed = [sem(f"emb_landed{b}") for b in range(RING)]
            part_stored = [sem(f"part_stored{b}") for b in range(2)]
            hid_mm, hid_done, top_done, less_done, mid_done, part_done = (
                sem("hid_mm"), sem("hid_done"), sem("top_done"), sem("less_done"), sem("middle_done"), sem("part_done"))
            groups = NN // NG

            block = st.enter_context(nc.Block())

            @block.sync
            def _(sp):
                sp.dma_start(w_s[:, 0:F], w).then_inc(w_landed, 16)
                sp.dma_start(wT_s[:], wT).then_inc(w_landed, 16)
                sp.dma_start(att_s[:], att).then_inc(w_landed, 16)
                sp.dma_start(xT_s[:], xT).then_inc(xT_landed, 16)
                sp.dma_start(fc1_s[:].rearrange("p n h -> p (n h)"), fc1).then_inc(w_landed, 16)
                sp.dma_start(parts_s[:], parts).then_inc(w_landed, 16)
                sp.dma_start(idx_all[:].rearrange("p t two -> p (t two)"), idx).then_inc(idx_landed, 16)
                sp.dma_start(bias_b[:], bias.partition_broadcast(P)).then_inc(first_landed, 16)
                sp.dma_start(first_i[:], dst_ext[1:1 + NT * P].rearrange("(o t e) -> o t e", o=1, e=P)[:, :, 0]).then_inc(first_landed, 16)
                sp.dma_start(vec_s[:].rearrange("p t k -> p (t k)"), vec).then_inc(vec_landed, 16)

                def fetch_idx(k, b, later):
                    i = k * RING + b
                    if later:
                        sp.wait_ge(rows_landed[b], k * 16 * T)
                        sp.nop(nofuse=True)
                    sp.dma_start(idx_b[:, b].rearrange("p t two -> p (t two)"), idx[:, bass.ds(i * (2 * T), 2 * T)]
                                 ).then_inc(idx_fetched[b], 16)

                def load_emb(k, b, later):
                    i = k * RING + b
                    if later:
                        sp.wait_ge(hid_mm, 4 * (i - RING + 1))
                    sp.dma_start(emb_s[:, b], emb[:, bass.ds(i * (T * P), T * P)]).then_inc(emb_landed[b], 16)

                def spill_block(k, b):
                    i = k * RING + b
                    sp.wait_ge(part_done, i + 1)
                    sp.dma_start(hid_d[:, bass.ds(i * (2 * T * P), 2 * T * P)],
                                 part[:, b % 2].rearrange("p n e -> p (n e)")).then_inc(part_stored[b % 2], 16)
                    sp.wait_ge(rows_landed[b], (k + 1) * 16 * T)
                    sp.dma_start(spill[:, bass.ds(i * (T * R0), T * R0)],
                                 rows[:, b].rearrange("p t f -> p (t f)")).then_inc(rows_spilled[b], 16)
                for b in range(RING):
                    load_emb(0, b, False)
                    fetch_idx(0, b, False)
                for g in range(groups):
                    sp.wait_ge(tab_copied, g + 1)
                    sp.dma_start(table[g * NG * P:(g + 1) * NG * P].rearrange("(n p) f -> p n f", p=P),
                                 nodes0[:, g * NG:(g + 1) * NG]).then_inc(tab_stored, 16)
                sp.wait_ge(vec_done, 1)
                sp.dma_start(direction_d, vec_s[:].rearrange("p t k -> p (t k)")).then_inc(vec_stored, 16)
                spill_block(0, 0)
                with sp.Fori(1, NB // RING) as k:
                    for b in range(RING):
                        load_emb(k, b, True)
                        fetch_idx(k, b, True)
                        if b < RING - 1:
                            spill_block(k - 1, b + 1)
                        else:
                            spill_block(k, 0)
                for b in range(1, RING):
                    spill_block(NB // RING - 1, b)
                sp.wait_ge(first_landed, 32)
                sp.wait_ge(idx_landed, 16)
                sp.wait_ge(vec_stored, 16)
                for b in range(2):
                    sp.wait_ge(part_stored[b], 16 * (NB // 2))
                for b in range(RING):
                    sp.wait_ge(rows_spilled[b], 16 * (NB // RING))

            @block.gpsimd
            def _(pool):
                pool.iota(iota_i[:], pattern=[[1, P]], base=0, channel_multiplier=0).then_inc(iota_made, 1)
                pool.iota(part_i[:], pattern=[[0, 1]], base=0, channel_multiplier=1).then_inc(iota_made, 1)
                pool.wait_ge(tab_stored, 16 * groups)

                def gather_block(k, b, later):
                    i = k * RING + b
                    if later:
                        pool.wait_ge(rows_spilled[b], k * 16)
                        pool.wait_ge(rows_split, i - RING + 1)
                    pool.wait_ge(idx_fetched[b], 16 * (k + 1))
                    pool.nop(nofuse=True)
                    for t in range(T):
                        pool.indirect_dma_start(rows[:, b, t], None, table,
                                                bass.IndirectOffsetOnAxis(ap=idx_b[:, b, t, 0:1], axis=0)
                                                ).then_inc(rows_landed[b], 16)
                for b in range(RING):
                    gather_block(0, b, False)
                with pool.Fori(1, NB // RING) as k:
                    for b in range(RING):
                        gather_block(k, b, True)

            @block.tensor
            def _(pe):
                pe.wait_ge(w_landed, 80)
                pe.matmul(p_att[0:F, 0:2], wT_s[:], att_s[:], start=True, stop=True).then_inc(att_mm, 1)
                pe.wait_ge(att_copied, 1)
                pe.wait_ge(xT_landed, 16)
                for g in range(groups):
                    if g >= 2:
                        pe.wait_ge(tab_copied, g - 1)
                    for j in range(NG):
                        n = g * NG + j
                        mm = pe.matmul(p_tab[g % 2][:, j * R0:(j + 1) * R0], xT_s[:, n * P:(n + 1) * P], w_s[:],
                                       start=True, stop=True)
                    mm.then_inc(tab_mm, 1)

                def hidden(k, b, later):
                    i = k * RING + b
                    pe.wait_ge(emb_landed[b], (k + 1) * 16)
                    for n in range(2):
                        for h in range(2):
                            if later or b:
                                pe.wait_ge(hid_done, 4 * (i - 1) + 2 * n + h + 1)
                            pe.matmul(p_hid[n][h][0:K6, :], fc1_s[:, n], emb_s[:, b, h * 512:(h + 1) * 512],
                                      start=True, stop=True).then_inc(hid_mm, 1)
                for b in range(RING):
                    hidden(0, b, False)
                with pe.Fori(1, NB // RING) as k:
                    for b in range(RING):
                        hidden(k, b, True)

            @block.scalar
            def _(act):
                def hidden(k, b, later):
                    i = k * RING + b
                    if later:
                        act.wait_ge(part_done, i - RING + 1)
                    for n in range(2):
                        for h in range(2):
                            act.wait_ge(hid_mm, 4 * i + 2 * n + h + 1)
                            act.activation(hid[:, b, n, h * 512:(h + 1) * 512], p_hid[n][h][0:K6, :], ACT.Relu,
                                           scale=float(1.0 / np.sqrt(EMB))).then_inc(hid_done, 1)

                def highest(b, i, first):
                    if not first:
                        act.wait_ge(part_done, i - 1)
                    act.wait_ge(hid_done, 4 * (i + 1))
                    act.activation(top[:, b % 2], hid[:, b], ACT.Copy).then_inc(top_done, 1)

                def middle(b, i):
                    act.wait_ge(less_done, i + 1)
                    act.activation(top[:, b % 2], hid[:, b], ACT.Copy).then_inc(mid_done, 1)
                hidden(0, 0, False)
                act.wait_ge(vec_root, 1)
                act.activation(asd[:, 1], asd[:, 0], ACT.Sqrt).then_inc(vec_rooted, 1)
                for b in range(RING - 1):
                    highest(b, b, b < 2)
                    if b:
                        middle(b - 1, b - 1)
                    hidden(0, b + 1, False)
                with act.Fori(1, NB // RING) as k:
                    for b in range(RING):
                        last = k * RING + b - 1
                        highest((b - 1) % RING, last, False)
                        middle((b - 2) % RING, last - 1)
                        hidden(k, b, True)
                highest(RING - 1, NB - 1, False)
                middle(RING - 2, NB - 2)
                middle(RING - 1, NB - 1)

            @block.vector
            def _(dve):
                dve.wait_ge(iota_made, 2)
                dve.tensor_copy(part_f[:], part_i[:]).then_inc(part_cast, 1)
                dve.tensor_copy(iota_n[:], iota_i[:]).then_inc(part_cast, 1)
                dve.wait_ge(part_cast, 2)
                dve.tensor_scalar(minus_p[:], part_f[:], -1.0, None, ALU.mult).then_inc(consts_made, 1)
                dve.tensor_scalar(ident[:], iota_n[:], part_f[:, 0:1], None, ALU.is_equal).then_inc(consts_made, 1)
                dve.wait_ge(att_mm, 1)
                dve.tensor_copy(w_s[:, F:R0], p_att[0:F, 0:2]).then_inc(att_copied, 1)
                for g in range(groups):
                    dve.wait_ge(tab_mm, g + 1)
                    dve.tensor_copy(nodes0[:, g * NG:(g + 1) * NG, :].rearrange("p n f -> p (n f)"),
                                    p_tab[g % 2][:, 0:NG * R0]).then_inc(tab_copied, 1)

                done = [0]

                def then(ins):
                    done[0] += 1
                    ins.then_inc(vec_step, 1)
                    dve.wait_ge(vec_step, done[0])
                dve.wait_ge(vec_landed, 16)
                then(dve.tensor_tensor(asd[:, 0], vec_s[:, :, 0], vec_s[:, :, 0], ALU.mult))
                for c in (1, 2):
                    then(dve.tensor_tensor(asd[:, 1], vec_s[:, :, c], vec_s[:, :, c], ALU.mult))
                    then(dve.tensor_tensor(asd[:, 0], asd[:, 0], asd[:, 1], ALU.add))
                dve.sem_inc(vec_root, 1)
                dve.wait_ge(vec_rooted, 1)
                then(dve.reciprocal(asd[:, 0], asd[:, 1]))
                then(dve.tensor_tensor(vec_s[:], vec_s[:], asd[:, 0].unsqueeze(2).to_broadcast([P, NT, 3]), ALU.mult))
                dve.sem_inc(vec_done, 1)

                def split_block(k, b):
                    i = k * RING + b
                    dve.wait_ge(rows_landed[b], (k + 1) * 16 * T)
                    dve.tensor_copy(asd[:, :, bass.ds(i * T, T)],
                                    rows[:, b, :, F:R0].rearrange("p t two -> p two t")).then_inc(rows_split, 1)

                def less(k, b, i):
                    r = b % 2
                    dve.wait_ge(top_done, i + 1)
                    dve.scalar_tensor_tensor(out=hid[:, b], in0=top[:, r], scalar=parts_s[:, 0:1], in1=hid[:, b],
                                             op0=ALU.mult, op1=ALU.add).then_inc(less_done, 1)

                def lowest(k, b, i, first):
                    r = b % 2
                    dve.wait_ge(mid_done, i + 1)
                    if not first:
                        dve.wait_ge(part_stored[r], stored(k, b))
                    dve.scalar_tensor_tensor(out=part[:, r], in0=top[:, r], scalar=parts_s[:, 1:2], in1=hid[:, b],
                                             op0=ALU.mult, op1=ALU.add).then_inc(part_done, 1)

                def stored(k, b):
                    return 32 * k + 16 * (b // 2)

                for b in range(RING):
                    less(0, b, b)
                    if b:
                        lowest(0, b - 1, b - 1, b - 1 < 2)
                    split_block(0, b)
                with dve.Fori(1, NB // RING) as k:
                    for b in range(RING):
                        less(k, b, k * RING + b)
                        if b:
                            lowest(k, b - 1, k * RING + b - 1, False)
                        else:
                            lowest(k - 1, RING - 1, k * RING - 1, False)
                        split_block(k, b)
                lowest(NB // RING - 1, RING - 1, NB - 1, False)
                dve.wait_ge(rows_split, NB)

        ex_e = asd
        with ExitStack() as st:
            sb, ps, sem = maker(st)
            BEFORE, AFTER, SRC, SELF, LAST, CUR = range(6)
            big = sb("big", [P, 6, NC * P])
            big_i = big[:].bitcast(I32)
            aT = sb("aT", [P, 2, NC * P])
            pen = sb("pen", [P, 2, NC * P])
            scan = sb("scan", [P, 4, NC * P])
            ends = sb("ends", [P, 4, NC])
            carry = sb("carry", [P, 4, NC])
            row_i = sb("row_i", [1, 4, NT], I32)
            row_pen = sb("row_pen", [1, 4, NT])
            row_in = big[0:1, 0:4, :]
            row_out = row_i[:].bitcast(F32)
            ones = sb("ones", [1, P])
            p_t = [ps(f"p_t{j}") for j in range(4)]

            dst_loaded, row_loaded, a_mm, a_copied, d = (
                sem("dst_loaded"), sem("row_loaded"), sem("a_mm"), sem("a_copied"), sem("d"))
            base_row, base_mm, ends_made, ends_out, rows_in, carry_made, carry_out, carry_in = (
                sem("base_row"), sem("base_mm"), sem("ends_made"), sem("ends_out"), sem("rows_in"),
                sem("carry_made"), sem("carry_out"), sem("carry_in"))
            exponent_made, exp_done, max_made, ex_mm, ex_copied = (
                sem("exponent_made"), sem("exp_done"), sem("max_made"), sem("ex_mm"), sem("ex_copied"))
            local_made, local_stored = sem("local_made"), sem("local_stored")
            quarters = -(-NT // 512)

            block = st.enter_context(nc.Block())

            @block.sync
            def _(sp):
                for j, at in ((BEFORE, 0), (CUR, 1), (AFTER, 2)):
                    sp.dma_start(big_i[:, j].rearrange("p (c e) -> p c e", e=P),
                                 dst_ext[at:at + NT * P].rearrange("(c p e) -> p c e", p=P, e=P)).then_inc(dst_loaded, 16)
                sp.dma_start(big_i[:, SRC].rearrange("p (c e) -> p c e", e=P),
                             src_flat.rearrange("(c p e) -> p c e", p=P, e=P)).then_inc(dst_loaded, 16)
                for j, at in enumerate((0, 1, P, P + 1)):
                    sp.dma_start(row_i[:, j], dst_ext[at:at + NT * P].rearrange("(o t e) -> o t e", o=1, e=P)[:, :, 0]
                                 ).then_inc(row_loaded, 16)
                sp.wait_ge(local_made, 1)
                sp.dma_start(local_d.rearrange("(c p e) -> p c e", p=P, e=P), big[:, BEFORE].rearrange("p (c e) -> p c e", e=P)
                             ).then_inc(local_stored, 16)
                sp.wait_ge(ends_made, 1)
                for j in range(4):
                    sp.dma_start(ends_d[j].rearrange("(c p) -> p c", p=P), ends[:, j]).then_inc(ends_out, 16)
                sp.wait_ge(ends_out, 64)
                sp.wait_ge(local_stored, 16)
                sp.dma_start(row_in, ends_d.rearrange("(o j) t -> o j t", o=1)).then_inc(rows_in, 16)
                sp.wait_ge(carry_made, 1)
                sp.dma_start(carry_d.rearrange("(o j) t -> o j t", o=1), row_out).then_inc(carry_out, 16)
                sp.wait_ge(carry_out, 16)
                for j in range(4):
                    sp.dma_start(carry[:, j], carry_d[j].rearrange("(c p) -> p c", p=P)).then_inc(carry_in, 16)
                sp.wait_ge(carry_in, 64)

            @block.tensor
            def _(pe):
                for m in range(2 * NC):
                    if m >= 4:
                        pe.wait_ge(a_copied, m - 3)
                    pe.transpose(p_t[m % 4][:, 0:P], asd[:, m // NC, m % NC * P:(m % NC + 1) * P], ident[:]).then_inc(a_mm, 1)
                pe.wait_ge(base_row, 1)
                for q in range(quarters):
                    wq = min(512, NT - q * 512)
                    pe.wait_ge(a_copied, 2 * NC + q)
                    pe.matmul(p_t[0][:, 0:wq], ones[:], row_pen[:, 0, q * 512:q * 512 + wq], start=True, stop=True
                              ).then_inc(base_mm, 1)
                pe.wait_ge(a_copied, 2 * NC + quarters)
                pe.wait_ge(exp_done, 1)
                pe.wait_ge(max_made, 1)
                for m in range(2 * NC):
                    if m >= 4:
                        pe.wait_ge(ex_copied, m - 3)
                    pe.transpose(p_t[m % 4][:, 0:P], aT[:, m // NC, m % NC * P:(m % NC + 1) * P], ident[:]).then_inc(ex_mm, 1)

            @block.scalar
            def _(act):
                act.wait_ge(exponent_made, 1)
                act.activation(aT[:, 0], big[:, AFTER], ACT.Exp).then_inc(exp_done, 1)

            @block.vector
            def _(dve):
                done = [0]

                def then(ins):
                    done[0] += 1
                    ins.then_inc(d, 1)
                    dve.wait_ge(d, done[0])

                def chunks(ap):
                    return ap.rearrange("p (c e) -> p c e", e=P)

                for m in range(2 * NC):
                    dve.wait_ge(a_mm, m + 1)
                    dve.tensor_copy(aT[:, m // NC, m % NC * P:(m % NC + 1) * P], p_t[m % 4][:, 0:P]).then_inc(a_copied, 1)
                then(dve.memset(ones[:], 1.0))
                dve.wait_ge(row_loaded, 64)
                then(dve.tensor_copy(row_pen[:, 0], row_i[:, 1]))
                dve.sem_inc(base_row, 1)
                then(dve.tensor_copy(local[:], idx_all[:, :, 1]))
                for q in range(quarters):
                    wq = min(512, NT - q * 512)
                    dve.wait_ge(base_mm, q + 1)
                    dve.tensor_tensor(local[:, q * 512:q * 512 + wq], local[:, q * 512:q * 512 + wq],
                                      p_t[0][:, 0:wq], ALU.subtract).then_inc(a_copied, 1)
                dve.wait_ge(a_copied, 2 * NC + quarters)
                dve.wait_ge(dst_loaded, 64)
                then(dve.tensor_tensor(big[:, LAST], big_i[:, CUR], big_i[:, AFTER], ALU.not_equal))
                then(dve.tensor_tensor(pen[:, 0], big_i[:, CUR], big_i[:, BEFORE], ALU.not_equal))
                then(dve.tensor_scalar(pen[:, 0], pen[:, 0], -BIG, None, ALU.mult))
                then(dve.tensor_scalar(pen[:, 1], big[:, LAST], -BIG, None, ALU.mult))
                cur3 = chunks(big_i[:, CUR])
                then(dve.tensor_tensor(chunks(big[:, BEFORE]), cur3, cur3[:, :, 0:1].to_broadcast([P, NC, P]),
                                       ALU.subtract))
                dve.sem_inc(local_made, 1)
                then(dve.memset(chunks(pen[:, 0])[:, :, 0], -BIG))
                then(dve.memset(chunks(pen[:, 1])[:, :, P - 1], -BIG))
                then(dve.tensor_tensor(big[:, SELF], big_i[:, SRC], big_i[:, CUR], ALU.is_equal))
                then(dve.tensor_scalar(big[:, AFTER], big[:, SELF], BIG, -BIG, ALU.mult, ALU.add))
                then(dve.tensor_tensor(big[:, SELF], big[:, SELF], aT[:, 1], ALU.mult))
                then(dve.tensor_tensor(big[:, SELF], big[:, SELF], big[:, AFTER], ALU.add))
                for j, a in ((0, aT[:, 0]), (1, big[:, SELF])):
                    then(dve.tensor_tensor_scan(scan[:, j], pen[:, 0], a, -BIG, ALU.add, ALU.max))
                    then(dve.tensor_tensor_scan(scan[:, 2 + j, ::-1], pen[:, 1, ::-1], a[:, ::-1], -BIG, ALU.add, ALU.max))
                then(dve.tensor_copy(ends[:, 0:2], scan[:, 0:2].rearrange("p j (c e) -> p j c e", e=P)[:, :, :, P - 1]))
                then(dve.tensor_copy(ends[:, 2:4], scan[:, 2:4].rearrange("p j (c e) -> p j c e", e=P)[:, :, :, 0]))
                dve.sem_inc(ends_made, 1)
                last_before, first, last, first_after = (row_i[:, j] for j in range(4))
                for j, (one, other) in enumerate(((last, last_before), (first, first_after),
                                                  (first, last_before), (last, first_after))):
                    then(dve.tensor_tensor(row_pen[:, j], one, other, ALU.not_equal))
                then(dve.tensor_scalar(row_pen[:], row_pen[:], -BIG, None, ALU.mult))
                then(dve.memset(row_out, -BIG))
                dve.wait_ge(rows_in, 16)
                for j in range(2):
                    then(dve.tensor_tensor_scan(row_in[:, j], row_pen[:, 0], row_in[:, j], -BIG, ALU.add, ALU.max))
                    then(dve.tensor_tensor_scan(row_in[:, 2 + j, ::-1], row_pen[:, 1, ::-1],
                                                row_in[:, 2 + j, ::-1], -BIG, ALU.add, ALU.max))
                    then(dve.tensor_tensor(row_out[:, j, 1:NT], row_in[:, j, 0:NT - 1], row_pen[:, 2, 1:NT], ALU.add))
                    then(dve.tensor_tensor(row_out[:, 2 + j, 0:NT - 1], row_in[:, 2 + j, 1:NT], row_pen[:, 3, 0:NT - 1],
                                           ALU.add))
                dve.sem_inc(carry_made, 1)
                for j, at in ((0, 0), (1, P - 1)):
                    then(dve.tensor_tensor(chunks(pen[:, j]), cur3, cur3[:, :, at:at + 1].to_broadcast([P, NC, P]),
                                           ALU.not_equal))
                then(dve.tensor_scalar(pen[:], pen[:], -BIG, None, ALU.mult))
                dve.wait_ge(carry_in, 64)
                for j in range(4):
                    then(dve.tensor_tensor(chunks(big[:, BEFORE]), chunks(pen[:, j // 2]),
                                           carry[:, j].unsqueeze(2).to_broadcast([P, NC, P]), ALU.add))
                    then(dve.tensor_tensor(scan[:, j], scan[:, j], big[:, BEFORE], ALU.max))
                then(dve.tensor_tensor(scan[:, 0:2], scan[:, 0:2], scan[:, 2:4], ALU.max))
                then(dve.tensor_tensor(pen[:, 0], scan[:, 0], scan[:, 1], ALU.add))
                then(dve.tensor_tensor(pen[:, 1], aT[:, 0], scan[:, 1], ALU.add))
                then(dve.scalar_tensor_tensor(out=pen[:], in0=pen[:], scalar=SLOPE, in1=pen[:], op0=ALU.mult, op1=ALU.max))
                then(dve.tensor_tensor(big[:, AFTER], pen[:, 1], pen[:, 0], ALU.subtract))
                dve.sem_inc(exponent_made, 1)
                then(dve.tensor_tensor(aT[:, 1], big[:, LAST], pen[:, 0], ALU.mult))
                dve.sem_inc(max_made, 1)
                for m in range(2 * NC):
                    dve.wait_ge(ex_mm, m + 1)
                    dve.tensor_copy(ex_e[:, m // NC, m % NC * P:(m % NC + 1) * P], p_t[m % 4][:, 0:P]).then_inc(ex_copied, 1)
                dve.wait_ge(ex_copied, 2 * NC)

        acc = layer0.enter_context(nc.sbuf_tensor("acc", [64 + R0, ACC], F32))
        acc_a, acc_b = acc[0:R0], acc[64:64 + R0]
        with ExitStack() as st:
            sb, ps, sem = maker(st)
            HALF = T // 2
            rows = sb("rows3", [P, RING, T, R0])
            z = sb("z3", [P, RING, T, R0])
            hot = sb("hot3", [P, RING, T, P])
            win = [[ps(f"win3_{a}{h}") for h in range(2)] for a in range(2)]
            acc_zeroed, z_made, hot_made = sem("acc_zeroed"), sem("z_made"), sem("hot_made")
            win_mm = [sem("win_mm_a"), sem("win_mm_b")]
            added_a, added_b = sem("added_a"), sem("added_b")
            back = [sem(f"back{b}") for b in range(RING)]

            def run3(eng, body, last):
                for b in range(RING):
                    body(0, b, b)
                with eng.Fori(1, NB // RING - last) as k:
                    for b in range(RING):
                        body(k, b, None)
                if last:
                    for b in range(RING):
                        body(NB // RING - 1, b, NB - RING + b)

            block = st.enter_context(nc.Block())

            @block.sync
            def _(sp):
                def load_block(k, b, lo):
                    i = k * RING + b
                    if lo is None:
                        sp.wait_ge(z_made, 2 * (i - RING + 1))
                    sp.dma_start(rows[:, b].rearrange("p t f -> p (t f)"),
                                 spill[:, bass.ds(i * (T * R0), T * R0)]).then_inc(back[b], 16)
                run3(sp, load_block, 0)

            @block.gpsimd
            def _(pool):
                pool.memset(acc[:, ACC // 2:], 0.0).then_inc(acc_zeroed, 1)

                def weigh(k, b, lo):
                    i = k * RING + b
                    if lo is None:
                        pool.wait_ge(win_mm[1], i - RING + 1)
                    pool.wait_ge(back[b], (k + 1) * 16)
                    pool.tensor_tensor(z[:, b, :, 0:F], rows[:, b, :, 0:F],
                                       ex_e[:, 0, bass.ds(i * T, T)].unsqueeze(2).to_broadcast([P, T, F]),
                                       ALU.mult).then_inc(z_made, 1)
                    pool.tensor_copy(z[:, b, :, F:R0].rearrange("p t two -> p two t"),
                                     ex_e[:, :, bass.ds(i * T, T)]).then_inc(z_made, 1)
                run3(pool, weigh, 0)

            @block.tensor
            def _(pe):
                def windows(k, b, lo):
                    i = k * RING + b
                    pe.wait_ge(z_made, 2 * (i + 1))
                    pe.wait_ge(hot_made, HALF * (i + 1))
                    for h in range(2):
                        if lo is None or lo >= 2:
                            pe.wait_ge((added_a, added_b)[h], (h + 1) * HALF * (i - 1))
                        for t in range(h * HALF, (h + 1) * HALF):
                            mm = pe.matmul(win[b % 2][h][0:R0, (t % HALF) * P:(t % HALF + 1) * P], z[:, b, t], hot[:, b, t],
                                           start=True, stop=True)
                        mm.then_inc(win_mm[h], 1)
                run3(pe, windows, 0)

            @block.scalar
            def _(act):
                def add(k, b, lo):
                    i = k * RING + b
                    _, bases = nc.values_load_multi_w_load_instructions(
                        first_i[0:1, bass.ds(i * T + HALF, HALF)], engines=[mybir.EngineType.Activation],
                        min_val=0, max_val=ACC - P)
                    act.wait_ge(win_mm[1], i + 1)
                    for j in range(HALF):
                        pw = win[b % 2][1][0:R0, j * P:(j + 1) * P]
                        if lo != 0 or j:
                            act.wait_ge(added_b, 2 * (HALF * i + j))
                        act.activation(acc_b[:, bass.ds(bases[j], 1)], pw[:, 0:1], ACT.Identity,
                                       bias=acc_b[:, bass.ds(bases[j], 1)]).then_inc(added_b, 1)
                        act.activation(acc_b[:, bass.ds(bases[j] + 1, P - 1)], pw[:, 1:P], ACT.Copy).then_inc(added_b, 1)
                act.wait_ge(acc_zeroed, 2)
                run3(act, add, 0)
                act.wait_ge(added_b, 2 * HALF * NB)

            @block.vector
            def _(dve):
                def one_hot(b, i, lo, j):
                    if j == 0 and (lo is None or lo >= RING):
                        dve.wait_ge(win_mm[1], i - RING + 1)
                    dve.tensor_tensor(hot[:, b, 2 * j:2 * j + 2], iota_n[:].unsqueeze(1).to_broadcast([P, 2, P]),
                                      local[:, bass.ds(i * T + 2 * j, 2)].unsqueeze(2).to_broadcast([P, 2, P]),
                                      ALU.is_equal).then_inc(hot_made, 1)

                def add(k, b, lo):
                    i = k * RING + b
                    _, bases = nc.values_load_multi_w_load_instructions(
                        first_i[0:1, bass.ds(i * T, HALF)], engines=[mybir.EngineType.DVE], min_val=0, max_val=ACC - P)
                    dve.wait_ge(win_mm[0], i + 1)
                    for j in range(HALF):
                        if lo != 0 or j:
                            dve.wait_ge(added_a, HALF * i + j)
                        dve.tensor_tensor(acc_a[:, bass.ds(bases[j], P)], acc_a[:, bass.ds(bases[j], P)],
                                          win[b % 2][0][0:R0, j * P:(j + 1) * P], ALU.add).then_inc(added_a, 1)
                        if lo is None or lo + 2 < NB:
                            one_hot((b + 2) % RING, i + 2, None if lo is None else lo + 2, j)
                for i in range(2):
                    for j in range(T // 2):
                        one_hot(i, i, i, j)
                dve.memset(acc[:, 0:ACC // 2], 0.0).then_inc(acc_zeroed, 1)
                dve.wait_ge(acc_zeroed, 2)
                run3(dve, add, 1)
                dve.wait_ge(added_a, HALF * NB)

        def layernorm(then, dve, act_done, want_sqrt, y, stat, sq):
            mean, var = stat[:, 0], stat[:, 1]
            then(dve.tensor_reduce(mean, y, AX_X, ALU.add))
            then(dve.tensor_scalar(mean, mean, 1.0 / F, None, ALU.mult))
            then(dve.tensor_tensor(y, y, mean.unsqueeze(2).to_broadcast([P, NN, F]), ALU.subtract))
            then(dve.tensor_tensor(sq, y, y, ALU.mult))
            then(dve.tensor_reduce(var, sq, AX_X, ALU.add))
            then(dve.tensor_scalar(var, var, 1.0 / F, EPS, ALU.mult, ALU.add))
            dve.sem_inc(want_sqrt, 1)
            dve.wait_ge(act_done, 1)
            then(dve.reciprocal(var, mean))
            then(dve.tensor_tensor(y, y, var.unsqueeze(2).to_broadcast([P, NN, F]), ALU.mult))

        with ExitStack() as st:
            sb, ps, sem = maker(st)
            xn = sb("xn", [P, NN, F])
            sums = sb("sums", [P, NN, R0])
            sq = sb("sq", [P, NN, F])
            x1 = sb("x1", [P, NN, F])
            stat = sb("stat", [P, 4, NN])
            parts3 = sb("parts3", [P, NN, 3 * F], BF16)
            no_part = sb("no_part", [P, 3 * F], BF16)
            half_copied = sem("half_copied")
            p_n = [[ps(f"p_n{n}{half}") for half in range(2)] for n in range(2)]
            x_landed, sums_mm, sums_copied, d4, self_ready, self_exp, want_sqrt, got_sqrt, x1_made, x1_stored = (
                sem("x_landed"), sem("sums_mm"), sem("sums_copied"), sem("d4"), sem("self_ready"), sem("self_exp"),
                sem("want_sqrt"), sem("got_sqrt"), sem("x1_made"), sem("x1_stored"))

            block = st.enter_context(nc.Block())

            @block.sync
            def _(sp):
                sp.dma_start(xn[:].rearrange("p n f -> p (n f)"), xN).then_inc(x_landed, 16)
                sp.wait_ge(x1_made, 1)
                sp.dma_start(table1.rearrange("(n p) f -> p n f", p=P), x1[:]).then_inc(x1_stored, 16)
                sp.dma_start(rows_d, x1[:].rearrange("p n f -> p (n f)")).then_inc(x1_stored, 16)
                sp.wait_ge(x1_made, 2)
                sp.dma_start(parts_d[0:NN * P].rearrange("(n p) f -> p n f", p=P), parts3[:]).then_inc(x1_stored, 16)
                sp.dma_start(parts_d[NN * P:(NN + 1) * P], no_part[:]).then_inc(x1_stored, 16)
                sp.wait_ge(x1_stored, 64)

            @block.tensor
            def _(pe):
                for g in range(NN // NG):
                    if g >= 2:
                        pe.wait_ge(sums_copied, g - 1)
                    for j in range(NG):
                        n = g * NG + j
                        for half, part in enumerate((acc_a, acc_b)):
                            at = 64 * half
                            mm = pe.transpose(p_n[g % 2][half][:, j * R0:(j + 1) * R0], part[:, n * P:(n + 1) * P],
                                              ident[at:at + R0, at:at + R0])
                    mm.then_inc(sums_mm, 1)

            @block.scalar
            def _(act):
                for g in range(NN // NG):
                    act.wait_ge(sums_mm, g + 1)
                    act.activation(sums[:, g * NG:(g + 1) * NG].rearrange("p n f -> p (n f)"),
                                   p_n[g % 2][0][:, 0:NG * R0], ACT.Copy).then_inc(half_copied, 1)
                act.wait_ge(self_ready, 1)
                act.activation(stat[:, 1], stat[:, 0], ACT.Exp).then_inc(self_exp, 1)
                act.wait_ge(want_sqrt, 1)
                act.activation(stat[:, 0], stat[:, 1], ACT.Sqrt).then_inc(got_sqrt, 1)

            @block.vector
            def _(dve):
                done = [0]

                def then(ins):
                    done[0] += 1
                    ins.then_inc(d4, 1)
                    dve.wait_ge(d4, done[0])

                for g in range(NN // NG):
                    dve.wait_ge(half_copied, g + 1)
                    group = sums[:, g * NG:(g + 1) * NG].rearrange("p n f -> p (n f)")
                    dve.tensor_tensor(group, group, p_n[g % 2][1][:, 0:NG * R0], ALU.add).then_inc(sums_copied, 1)
                dve.wait_ge(sums_copied, NN // NG)
                s0 = stat[:, 0]
                then(dve.tensor_tensor(s0, nodes0[:, :, F], nodes0[:, :, F + 1], ALU.add))
                then(dve.scalar_tensor_tensor(out=s0, in0=s0, scalar=SLOPE, in1=s0, op0=ALU.mult, op1=ALU.max))
                then(dve.tensor_tensor(s0, s0, sums[:, :, F + 1], ALU.subtract))
                dve.sem_inc(self_ready, 1)
                dve.wait_ge(self_exp, 1)
                s1 = stat[:, 1]
                then(dve.tensor_tensor(x1[:], nodes0[:, :, 0:F], s1.unsqueeze(2).to_broadcast([P, NN, F]), ALU.mult))
                then(dve.tensor_tensor(x1[:], x1[:], sums[:, :, 0:F], ALU.add))
                then(dve.tensor_tensor(stat[:, 2], sums[:, :, F], s1, ALU.add))
                then(dve.reciprocal(stat[:, 3], stat[:, 2]))
                then(dve.tensor_tensor(x1[:], x1[:], stat[:, 3].unsqueeze(2).to_broadcast([P, NN, F]), ALU.mult))
                then(dve.tensor_tensor(x1[:], x1[:], bias_b[:].unsqueeze(1).to_broadcast([P, NN, F]), ALU.add))
                dve.wait_ge(x_landed, 16)
                then(dve.tensor_tensor(x1[:], x1[:], xn[:], ALU.add))
                layernorm(then, dve, got_sqrt, want_sqrt, x1[:], stat, sq[:])
                dve.sem_inc(x1_made, 1)
                then(dve.memset(no_part[:], 0.0))
                then(dve.tensor_copy(parts3[:, :, 0:F], x1[:]))
                then(dve.tensor_tensor(sq[:], x1[:], parts3[:, :, 0:F], ALU.subtract))
                then(dve.tensor_copy(parts3[:, :, F:2 * F], sq[:]))
                then(dve.tensor_tensor(sq[:], sq[:], parts3[:, :, F:2 * F], ALU.subtract))
                then(dve.tensor_copy(parts3[:, :, 2 * F:3 * F], sq[:]))
                dve.sem_inc(x1_made, 1)

        layer0.close()

        acc = outer.enter_context(nc.sbuf_tensor("acc1", [F, ACC], F32))
        edge_layer(nc, maker, NB, NT, ACC, local, first_i, iota_n, ident, minus_p, acc, table1,
                   parts_d, local_d, idx, hid_d, direction_d, weight, w2, parts_s)

        with ExitStack() as st:
            sb, ps, sem = maker(st)
            y = sb("y6", [P, NN, F])
            x1 = sb("x1_again", [P, NN, F])
            sq = sb("sq6", [P, NN, F])
            stat = sb("stat6", [P, 2, NN])
            p_n = [ps("p_m0"), ps("p_m1")]
            sums6_mm, sums6_copied, d6, want6, got6, y_made, y_stored, x1_back = (
                sem("sums6_mm"), sem("sums6_copied"), sem("d6"), sem("want6"), sem("got6"), sem("y_made"), sem("y_stored"),
                sem("x1_back"))

            block = st.enter_context(nc.Block())

            @block.sync
            def _(sp):
                sp.dma_start(x1[:].rearrange("p n f -> p (n f)"), rows_d).then_inc(x1_back, 16)
                sp.wait_ge(y_made, 1)
                sp.dma_start(out, y[:].rearrange("p n f -> p (n f)")).then_inc(y_stored, 16)
                sp.wait_ge(y_stored, 16)

            @block.tensor
            def _(pe):
                for g in range(NN // NG):
                    if g >= 2:
                        pe.wait_ge(sums6_copied, g - 1)
                    for j in range(NG):
                        n = g * NG + j
                        mm = pe.transpose(p_n[g % 2][:, j * F:(j + 1) * F], acc[0:F, n * P:(n + 1) * P],
                                          ident[0:F, 0:F])
                    mm.then_inc(sums6_mm, 1)

            @block.scalar
            def _(act):
                act.wait_ge(want6, 1)
                act.activation(stat[:, 0], stat[:, 1], ACT.Sqrt).then_inc(got6, 1)

            @block.vector
            def _(dve):
                done = [0]

                def then(ins):
                    done[0] += 1
                    ins.then_inc(d6, 1)
                    dve.wait_ge(d6, done[0])

                dve.wait_ge(x1_back, 16)
                for g in range(NN // NG):
                    dve.wait_ge(sums6_mm, g + 1)
                    dve.tensor_tensor(y[:, g * NG:(g + 1) * NG].rearrange("p n f -> p (n f)"),
                                      p_n[g % 2][:, 0:NG * F],
                                      x1[:, g * NG:(g + 1) * NG].rearrange("p n f -> p (n f)"), ALU.add
                                      ).then_inc(sums6_copied, 1)
                dve.wait_ge(sums6_copied, NN // NG)
                layernorm(then, dve, got6, want6, y[:], stat, sq[:])
                dve.sem_inc(y_made, 1)


def edge_layer(nc, maker, NB, NT, ACC, local, first_i, iota_n, ident, minus_p, acc, table1,
               parts_d, local_d, idx, hid_d, direction_d, weight, w2, parts_s):
    HT = T // 2
    OA = 48
    OB = 48
    QB = OB + 16
    LAST = 3
    with ExitStack() as st:
        sb, ps, sem = maker(st)
        vec_s = sb("vec_s", [P, NT, 3])
        weight_s = sb("weight_s", [P, NT])
        w_f = sb("w_f", [K6, 896])
        w_top = sb("w_top", [K6, 896], BF16)
        w_part = sb("w_part", [K6, 896], BF16)
        hid = sb("hid5", [K6, RING, 2, T * P], BF16)
        idx_b = sb("idx_b5", [P, RING, T, 2], I32)
        source = sb("source", [P, RING, T, F])
        dst_row = sb("dst_row", [P, 2, T * P])
        hot_n = sb("hot_n", [P, 2, T * P], BF16)
        nodes = sb("nodes", [P, RING, T, 3 * F], BF16)
        s1 = sb("s1", [P, 2, T, 16])
        v1 = sb("v1", [P, 2, T, 3, 16])
        vr = sb("vr", [P, T, 3, 16])
        vdot = sb("vdot", [P, 2, T, 16])
        prod = sb("prod", [P, 2, HT, 16, OA])
        suma = sb("suma", [P, 2, T, OA])
        in_b = sb("in_b", [P, T, 16])
        vt = sb("vt", [P, T, 3, 8])
        vt_r = sb("vt_r", [P, T, 3, 8])
        prodb = sb("prodb", [P, 2, HT, 8, QB])
        th = sb("th", [P, 2, T, 16])
        cv = sb("cv", [P, 2, T, 32])
        wg = sb("wg", [P, T, 8])
        msg = sb("msg", [P, T, 3, 8])
        z = sb("z5", [P, 2, T, F])
        hot = sb("hot5", [P, 2, T, P])
        absd = sb("absd", [P, T, P])
        p_w = [st.enter_context(nc.psum_tensor(f"p_w{n}", [P, 2, 512], F32)) for n in range(2)]
        p_suma, p_sumb = ps("p_suma"), ps("p_sumb")
        p_win, p_dst = ps("p_win"), ps("p_dst")
        dst_v = p_dst[:, 0:T * F].rearrange("p (t f) -> p t f", f=F)
        suma_v = p_suma[:, 0:T * OA].rearrange("p (t o) -> p t o", o=OA)
        sumb_v = p_sumb[:, 0:T * OB].rearrange("p (t o) -> p t o", o=OB)

        const_landed, vec_landed, weight_landed = sem("const_landed"), sem("vec_landed"), sem("weight_landed")
        setup_step = sem("setup_step")
        acc_zeroed5, weights_split = sem("acc_zeroed5"), sem("weights_split")
        hid_landed = [sem(f"hid_landed{b}") for b in range(RING)]
        idx_landed5 = [sem(f"idx_landed5_{b}") for b in range(RING)]
        source_landed = [sem(f"source_landed{b}") for b in range(RING)]
        row_landed = [sem(f"row_landed{b}") for b in range(2)]
        nodes_landed = [sem(f"nodes_landed{b}") for b in range(RING)]
        row_abs, hot_n_done, dst_mm = sem("row_abs"), sem("hot_n_done"), sem("dst_mm")
        halved_a, joined_b = sem("halved_a"), sem("joined_b")
        ends_split, ends_read = sem("ends_split"), sem("ends_read")
        w_mm, w_used = sem("w_mm"), sem("w_used")
        suma_mm, suma_copied, sumb_mm = sem("suma_mm"), sem("suma_copied"), sem("sumb_mm")
        weighted = sem("weighted")
        vr_made, vdot_done = sem("vr_made"), sem("vdot_done")
        mid_step, msg_step = sem("mid_step"), sem("msg_step")
        sumb_read, z_done, abs_done, hot_done = sem("sumb_read"), sem("z_done"), sem("abs_done"), sem("hot_done")
        win_mm5, win_added5 = sem("win_mm5"), sem("win_added5")

        def run(eng, body):
            for b in range(RING):
                body(0, b, b)
            with eng.Fori(1, NB // RING - 1) as k:
                for b in range(RING):
                    body(k, b, None)
            for b in range(RING):
                body(NB // RING - 1, b, NB - RING + b)
            for b in range(LAST):
                body(NB // RING, b, NB + b)

        def has(lo, lag):
            return lo is None or 0 <= lo - lag < NB

        def past(lo, n):
            return lo is None or lo >= n

        def a_tiles(i, lo):
            return 0 if lo == 0 else 2 * T * i - T

        def b_tiles(i, lo):
            return 2 * T * NB - T if lo == NB else 2 * T * i

        def a_end(i, lo):
            return a_tiles(i, lo) + T

        def direction(i):
            return vec_s[:, bass.ds(i * T, T)]

        block = st.enter_context(nc.Block())

        @block.sync
        def _(sp):
            sp.dma_start(w_f[:], w2).then_inc(const_landed, 16)
            sp.dma_start(vec_s[:].rearrange("p t k -> p (t k)"), direction_d).then_inc(vec_landed, 16)
            sp.dma_start(weight_s[:], weight).then_inc(weight_landed, 16)

            def body(k, b, lo):
                i = k * RING + b
                if not has(lo, 0):
                    return
                if past(lo, RING):
                    sp.wait_ge(ends_read, i - RING + 1)
                    sp.nop(nofuse=True)
                sp.dma_start(idx_b[:, b].rearrange("p t two -> p (t two)"), idx[:, bass.ds(i * (2 * T), 2 * T)]
                             ).then_inc(idx_landed5[b], 16)
                if past(lo, RING):
                    sp.wait_ge(dst_mm, i - RING + 1)
                    sp.nop(nofuse=True)
                if past(lo, 2):
                    sp.wait_ge(hot_n_done, i - 1)
                    sp.nop(nofuse=True)
                sp.dma_start(dst_row[:, b % 2], local_d[bass.ds(i * (T * P), T * P)].partition_broadcast(P)
                             ).then_inc(row_landed[b % 2], 16)
                _, bases = nc.values_load_multi_w_load_instructions(
                    first_i[0:1, bass.ds(i * T, T)], engines=[mybir.EngineType.SP], min_val=0, max_val=ACC - P)
                for t in range(T):
                    sp.dma_start(nodes[:, b, t], parts_d[bass.ds(bases[t], P)]).then_inc(nodes_landed[b], 16)
                if past(lo, RING):
                    sp.wait_ge(w_mm, 2 * T * (i - 3) + T)
                    sp.nop(nofuse=True)
                sp.dma_start(hid[:, b].rearrange("p n e -> p (n e)"), hid_d[:, bass.ds(i * (2 * T * P), 2 * T * P)]
                             ).then_inc(hid_landed[b], 16)
            run(sp, body)

        @block.gpsimd
        def _(pool):
            def gather(k, b, i, lo, ts):
                if ts[0] == 0:
                    if past(lo, RING):
                        pool.wait_ge(ends_read, i - RING + 1)
                    pool.wait_ge(idx_landed5[b], 16 * (k + 1))
                    pool.nop(nofuse=True)
                for t in ts:
                    pool.indirect_dma_start(source[:, b, t], None, table1,
                                            bass.IndirectOffsetOnAxis(ap=idx_b[:, b, t, 0:1], axis=0)
                                            ).then_inc(source_landed[b], 16)

            def halve_a(i, lo, h):
                pool.wait_ge(w_used, a_tiles(i, lo) + (h + 1) * HT)
                pool.tensor_tensor(prod[:, h, :, 0:8, :], prod[:, h, :, 0:8, :], prod[:, h, :, 8:16, :], ALU.add
                                   ).then_inc(halved_a, 1)

            def body(k, b, lo):
                i = k * RING + b
                kn, bn = k + (b + 2) // RING, (b + 2) % RING
                ahead = None if lo is None else lo + 2
                if has(lo, 0):
                    halve_a(i, lo, 0)
                if has(lo, -2):
                    gather(kn, bn, i + 2, ahead, range(0, 1))
                if has(lo, 0):
                    halve_a(i, lo, 1)
                if has(lo, 2):
                    weigh(b, i - 2, lo)
                if has(lo, -1):
                    along((b + 1) % RING, i + 1, None if lo is None else lo + 1)
                if has(lo, -2):
                    gather(kn, bn, i + 2, ahead, range(1, T))

            def weigh(b, i, lo):
                edge_weight = weight_s[:, bass.ds(i * T, T)].unsqueeze(2).to_broadcast([P, T, 8])
                pool.wait_ge(sumb_read, 2 * (i + 1))
                if past(lo, 3):
                    pool.wait_ge(z_done, i)
                pool.nop(nofuse=True)
                pool.tensor_tensor(wg[:], th[:, b % 2, :, 8:16], edge_weight, ALU.mult).then_inc(weighted, 1)
                if past(lo, 4):
                    pool.wait_ge(win_mm5, 2 * (i - 1))
                    pool.nop(nofuse=True)
                pool.tensor_tensor(z[:, b % 2, :, 0:8], th[:, b % 2, :, 0:8], edge_weight, ALU.mult).then_inc(weighted, 1)

            def along(b, i, lo):
                pool.wait_ge(ends_split, 4 * (i + 1))
                if past(lo, 1):
                    pool.wait_ge(vdot_done, i)
                pool.nop(nofuse=True)
                pool.tensor_tensor(vr[:], v1[:, b % 2], direction(i).unsqueeze(3).to_broadcast([P, T, 3, 16]), ALU.mult
                                   ).then_inc(vr_made, 1)
            gather(0, 0, 0, 0, range(T))
            gather(0, 1, 1, 1, range(T))
            pool.wait_ge(vec_landed, 16)
            pool.wait_ge(weight_landed, 16)
            along(0, 0, 0)
            run(pool, body)

        @block.tensor
        def _(pe):
            def tile_weights(k, b, i, lo, t, net):
                n = (b_tiles if net else a_tiles)(i, lo) + t
                if t == 0 and net == 0:
                    pe.wait_ge(hid_landed[b], 16 * (k + 1))
                if past(lo, 1) or t >= 4:
                    pe.wait_ge(w_used, n - 3)
                cols = slice(512, 896) if net else slice(0, 512)
                pe.matmul(p_w[t // 2 % 2][:, t % 2, 0:cols.stop - cols.start], hid[:, (b - net) % RING, net, t * P:(t + 1) * P],
                          w_part[:, cols], start=True, stop=True).then_inc(w_mm, 1)

            def body(k, b, lo):
                i = k * RING + b

                def weights(*tiles, net):
                    for t in tiles:
                        if has(lo, net):
                            tile_weights(k, b, i, lo, t, net)

                def sum_a(h, us):
                    if not has(lo, 0):
                        return
                    if us[0] == 0:
                        pe.wait_ge(halved_a, 2 * i + h + 1)
                        if past(lo, 1) and h == 0:
                            pe.wait_ge(suma_copied, i)
                    for u in us:
                        mm = pe.matmul(p_suma[:, h * HT * OA:(h + 1) * HT * OA], ident[:], prod[:, h, :, u, :],
                                       start=(u == 0), stop=(u == 7))
                    if us[-1] == 7:
                        mm.then_inc(suma_mm, 1)

                def sum_b(h, us):
                    if not has(lo, 2):
                        return
                    if us[0] == 0:
                        pe.wait_ge(joined_b, 2 * i - 3 + h)
                        if past(lo, 3) and h == 0:
                            pe.wait_ge(sumb_read, 2 * (i - 2))
                    for u in us:
                        mm = pe.matmul(p_sumb[:, h * HT * OB:(h + 1) * HT * OB], ident[:], prodb[:, h, :, u, 0:OB],
                                       start=(u == 0), stop=(u == 7))
                    if us[-1] == 7:
                        mm.then_inc(sumb_mm, 1)

                def windows(h):
                    if not has(lo, 3):
                        return
                    if h == 0:
                        pe.wait_ge(weighted, 2 * (i - 2))
                        pe.wait_ge(z_done, i - 2)
                        pe.wait_ge(hot_done, i - 2)
                    if past(lo, 4) or h:
                        pe.wait_ge(win_added5, 2 * T * (i - 3) + h * T)
                    for t in range(h * HT, (h + 1) * HT):
                        mm = pe.matmul(p_win[0:F, (t % HT) * P:(t % HT + 1) * P], z[:, (b - 3) % 2, t], hot[:, (b - 3) % 2, t],
                                       start=True, stop=True)
                    mm.then_inc(win_mm5, 1)

                weights(2, 3, net=0)
                sum_b(0, range(0, 5))
                weights(4, 5, net=0)
                sum_b(0, range(5, 8))
                sum_b(1, range(0, 2))
                weights(6, 7, net=0)
                sum_b(1, range(2, 8))
                weights(0, 1, net=1)
                if has(lo, -1):
                    destinations(k + (b + 1) // RING, (b + 1) % RING, i + 1, None if lo is None else lo + 1)
                weights(2, 3, net=1)
                windows(0)
                sum_a(0, range(0, 3))
                weights(4, 5, net=1)
                sum_a(0, range(3, 8))
                weights(6, 7, net=1)
                windows(1)
                if has(lo, -1):
                    for t in range(2):
                        tile_weights(k + (b + 1) // RING, (b + 1) % RING, i + 1, None if lo is None else lo + 1, t, 0)
                sum_a(1, range(0, 8))

            def destinations(k, b, i, lo):
                pe.wait_ge(nodes_landed[b], 16 * T * (k + 1))
                pe.wait_ge(hot_n_done, i + 1)
                if past(lo, 1):
                    pe.wait_ge(ends_split, 4 * i)
                for t in range(T):
                    for part in range(3):
                        mm = pe.matmul(dst_v[:, t], hot_n[:, b % 2, t * P:(t + 1) * P], nodes[:, b, t, part * F:(part + 1) * F],
                                       start=(part == 0), stop=(part == 2))
                mm.then_inc(dst_mm, 1)
            destinations(0, 0, 0, 0)
            pe.wait_ge(weights_split, 1)
            for t in range(2):
                tile_weights(0, 0, 0, 0, t, 0)
            run(pe, body)

        @block.scalar
        def _(act):
            def split(k, b, i, lo):
                act.wait_ge(source_landed[b], (k + 1) * 16 * T)
                act.wait_ge(dst_mm, i + 1)
                if past(lo, 2):
                    act.wait_ge(w_used, a_end(i - 2, None if lo is None else lo - 2))
                for j, end in enumerate((source[:, b], dst_v)):
                    act.activation(s1[:, b % 2, :, 8 * j:8 * j + 8], end[:, :, 0:8], ACT.Copy).then_inc(ends_split, 1)
                    act.activation(v1[:, b % 2, :, :, 8 * j:8 * j + 8],
                                   end[:, :, 8:F].rearrange("p t (u k) -> p t k u", k=3), ACT.Copy
                                   ).then_inc(ends_split, 1)

            def one_hot_nodes(k, b, i, lo):
                act.wait_ge(row_landed[b % 2], 32 * k + 16 * (b // 2) + 16)
                act.activation(dst_row[:, b % 2], dst_row[:, b % 2], ACT.Abs, bias=minus_p[:, 0:1]).then_inc(row_abs, 1)
                if past(lo, 2):
                    act.wait_ge(dst_mm, i - 1)
                act.wait_ge(row_abs, i + 1)
                act.activation(hot_n[:, b % 2], dst_row[:, b % 2], ACT.Relu, scale=-1.0, bias=1.0).then_inc(hot_n_done, 1)

            def body(k, b, lo):
                i = k * RING + b
                if has(lo, 1):
                    act.wait_ge(suma_mm, 2 * i)
                    if past(lo, 3):
                        act.wait_ge(mid_step, 5 * (i - 2))
                    act.activation(suma[:, (b - 1) % 2], suma_v, ACT.Copy).then_inc(suma_copied, 1)
                if lo == 2:
                    act.wait_ge(acc_zeroed5, 1)
                if has(lo, 2):
                    if past(lo, 3):
                        act.wait_ge(hot_done, i - 2)
                    for t in range(T):
                        act.activation(absd[:, t], iota_n[:], ACT.Abs, bias=local[:, bass.ds((i - 2) * T + t, 1)]
                                       ).then_inc(abs_done, 1)
                    act.wait_ge(abs_done, (i - 1) * T)
                    if past(lo, 4):
                        act.wait_ge(win_mm5, 2 * (i - 3))
                    act.activation(hot[:, b % 2], absd[:], ACT.Relu, scale=-1.0, bias=1.0).then_inc(hot_done, 1)
                if has(lo, 3):
                    _, bases = nc.values_load_multi_w_load_instructions(
                        first_i[0:1, bass.ds((i - 3) * T, T)], engines=[mybir.EngineType.Activation],
                        min_val=0, max_val=ACC - P)
                if has(lo, 2):
                    act.wait_ge(sumb_mm, 2 * (i - 1))
                    if past(lo, 4):
                        act.wait_ge(weighted, 2 * (i - 3))
                        act.wait_ge(z_done, i - 3)
                    act.activation(th[:, b % 2], sumb_v[:, :, 0:16], ACT.Tanh).then_inc(sumb_read, 1)
                    act.activation(cv[:, b % 2], sumb_v[:, :, 16:48], ACT.Copy).then_inc(sumb_read, 1)
                if has(lo, -1):
                    split(k + (b + 1) // RING, (b + 1) % RING, i + 1, None if lo is None else lo + 1)
                if has(lo, -1):
                    act.wait_ge(ends_split, 4 * (i + 2))
                    act.sem_inc(ends_read, 1)
                if has(lo, 3):
                    add_windows(lo, i, 0, bases)
                if has(lo, -2):
                    one_hot_nodes(k + (b + 2) // RING, (b + 2) % RING, i + 2, None if lo is None else lo + 2)
                if has(lo, 3):
                    add_windows(lo, i, 1, bases)

            def add_windows(lo, i, h, bases):
                act.wait_ge(win_mm5, 2 * (i - 3) + h + 1)
                for t in range(h * HT, (h + 1) * HT):
                    pw = p_win[0:F, (t % HT) * P:(t % HT + 1) * P]
                    if past(lo, 4) or t:
                        act.wait_ge(win_added5, 2 * (T * (i - 3) + t))
                    act.activation(acc[:, bass.ds(bases[t], 1)], pw[:, 0:1], ACT.Identity,
                                   bias=acc[:, bass.ds(bases[t], 1)]).then_inc(win_added5, 1)
                    act.activation(acc[:, bass.ds(bases[t] + 1, P - 1)], pw[:, 1:P], ACT.Copy).then_inc(win_added5, 1)
            one_hot_nodes(0, 0, 0, 0)
            one_hot_nodes(0, 1, 1, 1)
            split(0, 0, 0, 0)
            act.wait_ge(ends_split, 4)
            act.sem_inc(ends_read, 1)
            run(act, body)
            act.wait_ge(win_added5, 2 * T * NB)

        @block.vector
        def _(dve):
            done = [0]

            def then(ins):
                done[0] += 1
                ins.then_inc(setup_step, 1)
                dve.wait_ge(setup_step, done[0])

            dve.wait_ge(const_landed, 16)
            sa, sb_ = 1.0 / np.sqrt(H) / np.sqrt(32.0), 1.0 / np.sqrt(H) / np.sqrt(16.0)
            for a, b, scale in ((0, 128, sa), (128, 256, sa * np.sqrt(3.0)), (256, 512, sa), (512, 640, sb_),
                                (640, 704, sb_ * np.sqrt(3.0)), (704, 896, sb_)):
                then(dve.tensor_scalar(w_f[:, a:b], w_f[:, a:b], float(scale), None, ALU.mult))
            then(dve.tensor_copy(w_top[:], w_f[:]))
            then(dve.scalar_tensor_tensor(out=w_f[:], in0=w_top[:], scalar=parts_s[:, 2:3], in1=w_f[:],
                                          op0=ALU.mult, op1=ALU.add))
            then(dve.tensor_copy(w_top[:], w_f[:]))
            then(dve.scalar_tensor_tensor(out=w_part[:], in0=w_top[:], scalar=parts_s[:, 3:4], in1=w_f[:],
                                          op0=ALU.mult, op1=ALU.add))
            dve.sem_inc(weights_split, 1)
            then(dve.tensor_scalar(local[:], local[:], -1.0, None, ALU.mult))
            then(dve.memset(acc[:], 0.0))
            dve.sem_inc(acc_zeroed5, 1)
            dve.wait_ge(vec_landed, 16)

            def vdot_sum(b, i, lo):
                dve.wait_ge(vr_made, i + 1)
                if past(lo, 2):
                    dve.wait_ge(w_used, a_end(i - 2, None if lo is None else lo - 2))
                dve.tensor_reduce(vdot[:, b % 2], vr[:].rearrange("p t k u -> p t u k"), AX_X, ALU.add
                                  ).then_inc(vdot_done, 1)

            def join_b(i, lo, h):
                dve.wait_ge(w_used, b_tiles(i, lo) + (h + 1) * HT)
                dve.tensor_tensor(prodb[:, h, :, :, 0:16], prodb[:, h, :, :, 0:16], prodb[:, h, :, :, OB:QB], ALU.add
                                  ).then_inc(joined_b, 1)

            def multiply_a(b, i, lo, t):
                r, h = b % 2, t // HT
                pw = p_w[t // 2 % 2]
                o = prod[:, h, t % HT:t % HT + 2].rearrange("p t u o -> p t o u")
                if t == 0:
                    dve.wait_ge(ends_split, 4 * (i + 1))
                if t % HT == 0 and past(lo, 1):
                    dve.wait_ge(suma_mm, 2 * i - 1 + h)
                dve.wait_ge(w_mm, a_tiles(i, lo) + t + 2)
                dve.tensor_tensor(o[:, :, 0:16], pw[:, :, 0:256].rearrange("p t (o u) -> p t o u", u=16),
                                  s1[:, r, t:t + 2].unsqueeze(2).to_broadcast([P, 2, 16, 16]), ALU.mult)
                if t == 0:
                    dve.wait_ge(vdot_done, i + 1)
                dve.tensor_tensor(o[:, :, 16:24], pw[:, :, 256:384].rearrange("p t (o u) -> p t o u", u=16),
                                  vdot[:, r, t:t + 2].unsqueeze(2).to_broadcast([P, 2, 8, 16]), ALU.mult)
                for j in range(2):
                    dve.tensor_tensor(o[:, j, 24:48].rearrange("p (k o) u -> p k o u", k=3),
                                      pw[:, j, 384:512].rearrange("p (o u) -> p o u", u=16).unsqueeze(1).to_broadcast([P, 3, 8, 16]),
                                      v1[:, r, t + j].unsqueeze(2).to_broadcast([P, 3, 8, 16]), ALU.mult
                                      ).then_inc(w_used, 1)

            def mid_steps(b, i, lo):
                sa = suma[:, b % 2]

                def one():
                    dve.wait_ge(suma_copied, i + 1)
                    if past(lo, 2):
                        dve.wait_ge(w_used, 2 * T * i + T)
                    dve.tensor_tensor(in_b[:, :, 0:8], sa[:, :, 0:8], sa[:, :, 16:24], ALU.add).then_inc(mid_step, 1)

                def two():
                    dve.tensor_tensor(vt_r[:], sa[:, :, 8:16].unsqueeze(2).to_broadcast([P, T, 3, 8]),
                                      direction(i).unsqueeze(3).to_broadcast([P, T, 3, 8]), ALU.mult).then_inc(mid_step, 1)

                def three():
                    dve.wait_ge(mid_step, 5 * i + 2)
                    dve.tensor_tensor(vt[:].rearrange("p t k o -> p t (k o)"), vt_r[:].rearrange("p t k o -> p t (k o)"),
                                      sa[:, :, 24:48], ALU.add).then_inc(mid_step, 1)

                def four():
                    dve.wait_ge(mid_step, 5 * i + 3)
                    dve.tensor_tensor(vt_r[:], vt[:], direction(i).unsqueeze(3).to_broadcast([P, T, 3, 8]), ALU.mult
                                      ).then_inc(mid_step, 1)

                def five():
                    dve.wait_ge(mid_step, 5 * i + 4)
                    dve.tensor_reduce(in_b[:, :, 8:16], vt_r[:].rearrange("p t k o -> p t o k"), AX_X, ALU.add
                                      ).then_inc(mid_step, 1)
                return [[one, two], [three], [four], [five]]

            def multiply_b(b, i, it, lo, t):
                h = t // HT
                pw = p_w[t // 2 % 2]
                q = prodb[:, h, t % HT:t % HT + 2].rearrange("p t u o -> p t o u")
                if t == 0:
                    dve.wait_ge(mid_step, 5 * i + 3)
                if t % HT == 0 and past(lo, 2):
                    dve.wait_ge(sumb_mm, 2 * i - 1 + h)
                dve.wait_ge(w_mm, b_tiles(it, lo) + t + 2)
                dve.tensor_tensor(q[:, :, 0:24], pw[:, :, 0:192].rearrange("p t (o u) -> p t o u", u=8),
                                  in_b[:, t:t + 2, 0:8].unsqueeze(2).to_broadcast([P, 2, 24, 8]), ALU.mult)
                if t == 0:
                    dve.wait_ge(mid_step, 5 * i + 5)
                dve.tensor_tensor(q[:, :, OB:QB], pw[:, :, 192:320].rearrange("p t (o u) -> p t o u", u=8),
                                  in_b[:, t:t + 2, 8:16].unsqueeze(2).to_broadcast([P, 2, 16, 8]), ALU.mult)
                for j in range(2):
                    dve.tensor_tensor(q[:, j, 24:48].rearrange("p (k o) u -> p k o u", k=3),
                                      pw[:, j, 320:384].rearrange("p (o u) -> p o u", u=8).unsqueeze(1).to_broadcast([P, 3, 8, 8]),
                                      vt[:, t + j].unsqueeze(2).to_broadcast([P, 3, 8, 8]), ALU.mult).then_inc(w_used, 1)

            def message_steps(b, i, lo):
                r = b % 2

                def one():
                    dve.wait_ge(sumb_read, 2 * (i + 1))
                    dve.tensor_tensor(msg[:], cv[:, r, :, 0:8].unsqueeze(2).to_broadcast([P, T, 3, 8]),
                                      direction(i).unsqueeze(3).to_broadcast([P, T, 3, 8]), ALU.mult).then_inc(msg_step, 1)

                def two():
                    dve.wait_ge(msg_step, 2 * i + 1)
                    dve.tensor_tensor(msg[:].rearrange("p t k o -> p t (k o)"), msg[:].rearrange("p t k o -> p t (k o)"),
                                      cv[:, r, :, 8:32], ALU.add).then_inc(msg_step, 1)

                def three():
                    dve.wait_ge(msg_step, 2 * i + 2)
                    dve.wait_ge(weighted, 2 * (i + 1))
                    dve.tensor_tensor(z[:, r, :, 8:F].rearrange("p t (o k) -> p t k o", k=3), msg[:],
                                      wg[:].unsqueeze(2).to_broadcast([P, T, 3, 8]), ALU.mult).then_inc(z_done, 1)
                return [[one], [two], [three]]

            def body(k, b, lo):
                i = k * RING + b
                mid = mid_steps(b - 1, i - 1, lo) if has(lo, 1) else [[]] * 4
                message = message_steps(b - 2, i - 2, lo) if has(lo, 2) else [[]] * 3
                for n in range(4):
                    if has(lo, 0):
                        multiply_a(b, i, lo, 2 * n)
                    for step in mid[n]:
                        step()
                for n, steps in enumerate(message + [[]]):
                    if has(lo, 1):
                        multiply_b(b - 1, i - 1, i, lo, 2 * n)
                        if n == 2:
                            join_b(i, lo, 0)
                    for step in steps:
                        step()
                if has(lo, -1):
                    vdot_sum(b + 1, i + 1, None if lo is None else lo + 1)
                if has(lo, 1):
                    join_b(i, lo, 1)
            vdot_sum(0, 0, 0)
            run(dve, body)


def kernel(x, src, dst, edge_attr_10, edge_attr_3, edge_weight, L0_gnn_W, L0_gnn_att_src, L0_gnn_att_dst, L0_gnn_bias,
           L1_gnn_fc1_w1, L1_gnn_fc1_w2, L1_gnn_fc2_w1, L1_gnn_fc2_w2):
    import concourse.bacc as bacc
    from concourse.bass_utils import run_bass_kernel_spmd

    n, e = x.shape[0], src.shape[0]
    NN = -(-(n + 1) // (P * NG)) * NG
    NT = -(-e // (P * P)) * P
    x, src, dst = np.asarray(x), np.asarray(src), np.asarray(dst)
    e10, e3, ew = np.asarray(edge_attr_10), np.asarray(edge_attr_3), np.asarray(edge_weight)
    E = NT * P

    x_pad = np.zeros((NN * P, F), x.dtype)
    x_pad[:n] = x
    src_pad = np.full(E, n, src.dtype)
    src_pad[:e] = src
    dst_ext = np.full(E + P + 1, n + 1, dst.dtype)
    dst_ext[0] = -1
    dst_ext[1:e + 1] = dst
    dst_ext[e + 1:E + 1] = n
    emb = np.zeros((EMB, E), e10.dtype)
    emb[:, :e] = e10.T
    vec = np.ones((E, 3), e3.dtype)
    vec[:e] = e3
    wgt = np.zeros(E, ew.dtype)
    wgt[:e] = ew

    def by_tile(a):
        return np.ascontiguousarray(np.moveaxis(a.reshape((NT, P) + a.shape[1:]), 0, 1))

    def columns(w, first, u):
        return np.asarray(w)[:, first:first + u * 8].reshape(H, u, 8).transpose(0, 2, 1).reshape(H, u * 8)

    f1, f2 = L1_gnn_fc1_w2, L1_gnn_fc2_w2
    w2 = [columns(f1, first, 16) for first in (0, 256, 128, 384)]
    w2 += [columns(f2, first, 8) for first in (0, 128, 256, 64, 192, 320)]
    parts = np.repeat(np.array([[-float(a > 0), -float(a > 1), -float(b > 0), -float(b > 1)]
                                for a, b in zip(HID_PART, W_PART)], np.float32), H, axis=0)

    arrays = {
        "xT": np.ascontiguousarray(x_pad.T),
        "xN": np.ascontiguousarray(x_pad.reshape(NN, P, F).transpose(1, 0, 2)).reshape(P, NN * F),
        "w": np.asarray(L0_gnn_W), "wT": np.ascontiguousarray(np.asarray(L0_gnn_W).T),
        "att": np.stack([np.asarray(L0_gnn_att_src), np.asarray(L0_gnn_att_dst)], axis=1),
        "bias": np.asarray(L0_gnn_bias),
        "idx": by_tile(np.stack([src_pad, dst_ext[1:E + 1]], axis=1)).reshape(P, NT * 2),
        "dst_ext": dst_ext, "src_flat": src_pad,
        "emb": emb, "vec": by_tile(vec).reshape(P, NT * 3), "weight": by_tile(wgt),
        "fc1": np.concatenate([np.tile(np.asarray(L1_gnn_fc1_w1), (1, 6)), np.tile(np.asarray(L1_gnn_fc2_w1), (1, 6))],
                              axis=1),
        "w2": np.tile(np.concatenate(w2, axis=1), (6, 1)), "parts": parts,
    }
    nc = bacc.Bacc("TRN2", target_bir_lowering=False, num_devices=1)
    args = [nc.dram_tensor("in_" + name, a.shape, mybir.dt.from_np(a.dtype), kind="ExternalInput").ap()
            for name, a in arrays.items()]
    out = nc.dram_tensor("nodes_out", (P, NN * F), F32, kind="ExternalOutput").ap()
    gnn_kernel(nc, *args, out, NN, NT)
    r = run_bass_kernel_spmd(nc, [{"in_" + name: a for name, a in arrays.items()}], core_ids=[0])
    return r.results[0]["nodes_out"].reshape(P, NN, F).transpose(1, 0, 2).reshape(NN * P, F)[:n]
```
